# Optimizing a Trainium2 kernel written in Bass

```python
import numpy as np
import jax
import jax.numpy as jnp

def _softmax(x, axis=-1):
    return jax.nn.softmax(x, axis=axis)

def _gelu(x):
    return jax.nn.gelu(x, approximate=True)

def _silu(x):
    return jax.nn.silu(x)

def _sigmoid(x):
    return jax.nn.sigmoid(x)

def _layernorm(x, axis=-1, eps=1e-05):
    m = jnp.mean(x, axis=axis, keepdims=True)
    v = jnp.var(x, axis=axis, keepdims=True)
    return (x - m) / jnp.sqrt(v + eps)

def _scatter_add(tgt, idx, src, axis=0):
    return tgt.at[idx].add(src)

def _segment_sum(src, seg, n):
    return jax.ops.segment_sum(src, seg, n)
kernel_name = 'mk_seq_preln_d2_jaxref_r8_b31a83'

def setup_inputs(seed: int=0):
    np.random.seed(seed)
    _w = jnp.asarray

    def _L0_attn_setup():
        import jax, jax.numpy as jnp
        import numpy as np
        EMBED_DIM = 128
        NUM_HEADS = 16
        HEAD_DIM = EMBED_DIM // NUM_HEADS
        SCALE = 1.0 / np.sqrt(HEAD_DIM)
        key = jax.random.key(seed)
        ks = jax.random.split(key, 5)
        B, S, D = (2, 256, EMBED_DIM)
        s = 0.02
        return {'x': jax.random.normal(ks[0], (B, S, D), jnp.float32), 'Wqkv': jax.random.normal(ks[1], (D, 3 * D), jnp.float32) * s, 'bqkv': jax.random.normal(ks[2], (3 * D,), jnp.float32) * s, 'Wout': jax.random.normal(ks[3], (D, D), jnp.float32) * s, 'bout': jax.random.normal(ks[4], (D,), jnp.float32) * s}
    _L0_attn_in = _L0_attn_setup()

    def _L0_ffn_setup():
        import jax, jax.numpy as jnp
        import numpy as np
        from jax import lax
        T, B, I, M, O = (32, 64, 128, 128, 128)

        def _xavier(key, shape):
            fan_out, fan_in = shape
            limit = float(np.sqrt(6.0 / (fan_in + fan_out)))
            return jax.random.uniform(key, shape, jnp.float32, -limit, limit)
        key = jax.random.key(seed)
        ks = jax.random.split(key, 9)
        x = jax.random.normal(ks[0], (T, B, I), jnp.float32)
        return {'x': x, 'wf': _xavier(ks[1], (M, I)), 'uf': _xavier(ks[2], (M, M)), 'bf': jnp.zeros((M,), jnp.float32), 'wi': _xavier(ks[3], (M, I)), 'ui': _xavier(ks[4], (M, M)), 'bi': jnp.zeros((M,), jnp.float32), 'wc': _xavier(ks[5], (M, I)), 'uc': _xavier(ks[6], (M, M)), 'bc': jnp.zeros((M,), jnp.float32), 'wo': _xavier(ks[7], (O, I)), 'uo': _xavier(ks[8], (O, M)), 'bo': jnp.zeros((O,), jnp.float32), 'in_c': jnp.zeros((M,), jnp.float32)}
    _L0_ffn_in = _L0_ffn_setup()

    def _L1_attn_setup():
        import jax, jax.numpy as jnp
        import numpy as np
        HEADS = 16
        ROPE_BASE = 10000.0

        def _rope_tables(T, head_dim, dtype):
            half = head_dim // 2
            inv_freq = 1.0 / ROPE_BASE ** (jnp.arange(0, head_dim, 2, dtype=jnp.float32) / head_dim)
            t = jnp.arange(T, dtype=jnp.float32)
            freqs = t[:, None] * inv_freq[None, :]
            cos = jnp.cos(freqs).astype(dtype)[None, None]
            sin = jnp.sin(freqs).astype(dtype)[None, None]
            return (cos, sin)

        def _apply_rope(x, cos, sin):
            xe, xo = jnp.split(x, 2, axis=-1)
            return jnp.concatenate([xe * cos - xo * sin, xe * sin + xo * cos], axis=-1)
        key = jax.random.key(seed)
        k1, k2, k3 = jax.random.split(key, 3)
        B, T, D = (4, 512, 128)
        x = jax.random.normal(k1, (B, T, D), dtype=jnp.float32)
        w_qkv = jax.random.normal(k2, (3 * D, D), dtype=jnp.float32) * 0.02
        w_out = jax.random.normal(k3, (D, D), dtype=jnp.float32) * 0.02
        return {'x': x, 'w_qkv': w_qkv, 'w_out': w_out}
    _L1_attn_in = _L1_attn_setup()

    def _L1_ffn_setup():
        import jax, jax.numpy as jnp
        import numpy as np
        B, S, D, E, H = (2, 128, 128, 16, 256)
        TOP_K = 2
        TEMP = 1.0
        key = jax.random.key(seed)
        ks = jax.random.split(key, 4)
        sc_d = 1.0 / np.sqrt(D)
        sc_h = 1.0 / np.sqrt(H)
        return {'x': jax.random.normal(ks[0], (B, S, D), dtype=jnp.float32), 'Wr': jax.random.normal(ks[1], (D, E), dtype=jnp.float32) * sc_d, 'br': jnp.zeros((E,), dtype=jnp.float32), 'W1': jax.random.normal(ks[2], (E, D, H), dtype=jnp.float32) * sc_d, 'b1': jnp.zeros((E, H), dtype=jnp.float32), 'W2': jax.random.normal(ks[3], (E, H, D), dtype=jnp.float32) * sc_h, 'b2': jnp.zeros((E, D), dtype=jnp.float32)}
    _L1_ffn_in = _L1_ffn_setup()
    _d = {'L0_attn_x': _L0_attn_in['x'], 'L0_attn_Wqkv': _L0_attn_in['Wqkv'], 'L0_attn_bqkv': _L0_attn_in['bqkv'], 'L0_attn_Wout': _L0_attn_in['Wout'], 'L0_attn_bout': _L0_attn_in['bout'], 'L0_ffn_wf': _L0_ffn_in['wf'], 'L0_ffn_uf': _L0_ffn_in['uf'], 'L0_ffn_bf': _L0_ffn_in['bf'], 'L0_ffn_wi': _L0_ffn_in['wi'], 'L0_ffn_ui': _L0_ffn_in['ui'], 'L0_ffn_bi': _L0_ffn_in['bi'], 'L0_ffn_wc': _L0_ffn_in['wc'], 'L0_ffn_uc': _L0_ffn_in['uc'], 'L0_ffn_bc': _L0_ffn_in['bc'], 'L0_ffn_wo': _L0_ffn_in['wo'], 'L0_ffn_uo': _L0_ffn_in['uo'], 'L0_ffn_bo': _L0_ffn_in['bo'], 'L0_ffn_in_c': _L0_ffn_in['in_c'], 'L1_attn_w_qkv': _L1_attn_in['w_qkv'], 'L1_attn_w_out': _L1_attn_in['w_out'], 'L1_ffn_Wr': _L1_ffn_in['Wr'], 'L1_ffn_br': _L1_ffn_in['br'], 'L1_ffn_W1': _L1_ffn_in['W1'], 'L1_ffn_b1': _L1_ffn_in['b1'], 'L1_ffn_W2': _L1_ffn_in['W2'], 'L1_ffn_b2': _L1_ffn_in['b2']}
    _x0 = _d['L0_attn_x']
    _d['L0_attn_x'] = jax.random.normal(jax.random.fold_in(jax.random.key(seed), 1), (16, 256, 128), dtype=_x0.dtype)
    del _x0
    return _d

def reference(L0_attn_x, L0_attn_Wqkv, L0_attn_bqkv, L0_attn_Wout, L0_attn_bout, L0_ffn_wf, L0_ffn_uf, L0_ffn_bf, L0_ffn_wi, L0_ffn_ui, L0_ffn_bi, L0_ffn_wc, L0_ffn_uc, L0_ffn_bc, L0_ffn_wo, L0_ffn_uo, L0_ffn_bo, L0_ffn_in_c, L1_attn_w_qkv, L1_attn_w_out, L1_ffn_Wr, L1_ffn_br, L1_ffn_W1, L1_ffn_b1, L1_ffn_W2, L1_ffn_b2):

    def _L0_attn_ref(x, Wqkv, bqkv, Wout, bout):
        import jax, jax.numpy as jnp
        import numpy as np
        EMBED_DIM = 128
        NUM_HEADS = 16
        HEAD_DIM = EMBED_DIM // NUM_HEADS
        SCALE = 1.0 / np.sqrt(HEAD_DIM)
        B, S, D = x.shape
        qkv = (x @ Wqkv + bqkv).reshape(B, S, 3, NUM_HEADS, HEAD_DIM)
        qkv = jnp.transpose(qkv, (2, 0, 3, 1, 4))
        q, k, v = (qkv[0] * SCALE, qkv[1], qkv[2])
        scores = jnp.einsum('bhqd,bhkd->bhqk', q, k)
        attn = jax.nn.softmax(scores, axis=-1)
        out = jnp.einsum('bhqk,bhkd->bhqd', attn, v)
        out = jnp.transpose(out, (0, 2, 1, 3)).reshape(B, S, D)
        return out @ Wout + bout

    def _L0_ffn_ref(x, wf, uf, bf, wi, ui, bi, wc, uc, bc, wo, uo, bo, in_c):
        import jax, jax.numpy as jnp
        import numpy as np
        from jax import lax
        T, B, I, M, O = (32, 64, 128, 128, 128)

        def _xavier(key, shape):
            fan_out, fan_in = shape
            limit = float(np.sqrt(6.0 / (fan_in + fan_out)))
            return jax.random.uniform(key, shape, jnp.float32, -limit, limit)
        batch = x.shape[1]
        c0 = jnp.broadcast_to(in_c, (batch, in_c.shape[0]))

        def step(c, xt):
            ft = jax.nn.sigmoid(xt @ wf.T + c @ uf.T + bf)
            it = jax.nn.sigmoid(xt @ wi.T + c @ ui.T + bi)
            gt = jnp.tanh(xt @ wc.T + c @ uc.T + bc)
            c = ft * c + it * gt
            return (c, None)
        c_final, _ = lax.scan(step, c0, x)
        h = jnp.tanh(jnp.einsum('tbi,oi->tbo', x, wo) + c_final @ uo.T + bo)
        return h

    def _L1_attn_ref(x, w_qkv, w_out):
        import jax, jax.numpy as jnp
        import numpy as np
        HEADS = 16
        ROPE_BASE = 10000.0

        def _rope_tables(T, head_dim, dtype):
            half = head_dim // 2
            inv_freq = 1.0 / ROPE_BASE ** (jnp.arange(0, head_dim, 2, dtype=jnp.float32) / head_dim)
            t = jnp.arange(T, dtype=jnp.float32)
            freqs = t[:, None] * inv_freq[None, :]
            cos = jnp.cos(freqs).astype(dtype)[None, None]
            sin = jnp.sin(freqs).astype(dtype)[None, None]
            return (cos, sin)

        def _apply_rope(x, cos, sin):
            xe, xo = jnp.split(x, 2, axis=-1)
            return jnp.concatenate([xe * cos - xo * sin, xe * sin + xo * cos], axis=-1)
        B, T, D = x.shape
        H = HEADS
        hd = D // H
        scale = hd ** (-0.5)
        qkv = (x @ w_qkv.T).reshape(B, T, 3, H, hd)
        qkv = jnp.transpose(qkv, (2, 0, 3, 1, 4))
        q, k, v = (qkv[0], qkv[1], qkv[2])
        cos, sin = _rope_tables(T, hd, x.dtype)
        q = _apply_rope(q, cos, sin)
        k = _apply_rope(k, cos, sin)
        q_feat = jax.nn.elu(q * scale) + 1.0
        k_feat = jax.nn.elu(k) + 1.0
        kv = jnp.einsum('bhtd,bhtv->bhdv', k_feat, v)
        k_sum = k_feat.sum(axis=2)
        denom = jnp.maximum(jnp.einsum('bhtd,bhd->bht', q_feat, k_sum), 1e-06)
        out = jnp.einsum('bhtd,bhdv->bhtv', q_feat, kv) / denom[..., None]
        out = jnp.transpose(out, (0, 2, 1, 3)).reshape(B, T, D)
        return out @ w_out.T

    def _L1_ffn_ref(x, Wr, br, W1, b1, W2, b2):
        import jax, jax.numpy as jnp
        import numpy as np
        B, S, D, E, H = (2, 128, 128, 16, 256)
        TOP_K = 2
        TEMP = 1.0
        token_shape = x.shape[:-1]
        d = x.shape[-1]
        xt = x.reshape(-1, d)
        T = xt.shape[0]
        logits = (xt @ Wr + br) / TEMP
        probs = jax.nn.softmax(logits, axis=-1)
        w, idx = jax.lax.top_k(probs, TOP_K)
        w = w / jnp.clip(jnp.sum(w, axis=-1, keepdims=True), 1e-09)
        comb = jnp.zeros((T, E), dtype=xt.dtype)
        comb = comb.at[jnp.arange(T)[:, None], idx].add(w)
        h = jax.nn.gelu(jnp.einsum('td,edh->teh', xt, W1) + b1, approximate=False)
        o = jnp.einsum('teh,eho->teo', h, W2) + b2
        y = jnp.einsum('teo,te->to', o, comb)
        y = xt + y
        return y.reshape(*token_shape, d)
    x = L0_attn_x
    x = x + _L0_attn_ref(_layernorm(x, axis=-1), L0_attn_Wqkv, L0_attn_bqkv, L0_attn_Wout, L0_attn_bout)
    x = x + _L0_ffn_ref(_layernorm(x, axis=-1), L0_ffn_wf, L0_ffn_uf, L0_ffn_bf, L0_ffn_wi, L0_ffn_ui, L0_ffn_bi, L0_ffn_wc, L0_ffn_uc, L0_ffn_bc, L0_ffn_wo, L0_ffn_uo, L0_ffn_bo, L0_ffn_in_c)
    x = x + _L1_attn_ref(_layernorm(x, axis=-1), L1_attn_w_qkv, L1_attn_w_out)
    x = x + _L1_ffn_ref(_layernorm(x, axis=-1), L1_ffn_Wr, L1_ffn_br, L1_ffn_W1, L1_ffn_b1, L1_ffn_W2, L1_ffn_b2)
    return x

_drawn_inputs = setup_inputs


def setup_inputs(seed=0):
    import zlib

    import numpy as np

    out = dict(_drawn_inputs(seed))
    spreads = {'L0_ffn_bf': (0.0, 0.315),
     'L0_ffn_bi': (0.0, 0.324),
     'L0_ffn_bc': (0.0, 0.1),
     'L0_ffn_bo': (0.0, 0.1),
     'L0_ffn_in_c': (0.0, 0.8),
     'L1_ffn_br': (0.0, 0.1),
     'L1_ffn_b1': (0.0, 0.352),
     'L1_ffn_b2': (0.0, 0.1)}
    factors = {'L0_attn_Wqkv': 4.727,
     'L0_attn_bqkv': 3.958,
     'L0_attn_Wout': 3.454,
     'L1_attn_w_qkv': 4.992,
     'L1_attn_w_out': 4.833}
    for name, (base, spread) in spreads.items():
        noise = np.random.default_rng([zlib.crc32(name.encode()), seed]).standard_normal(out[name].shape)
        drawn = base * np.exp(spread * noise) if base else spread * noise
        out[name] = jnp.asarray(drawn.astype(out[name].dtype))
    for name, factor in factors.items():
        out[name] = (out[name] * factor).astype(out[name].dtype)
    return out
```

```python
from contextlib import ExitStack

import concourse.bass as bass
from concourse import mybir

F32 = mybir.dt.float32
BF16 = mybir.dt.bfloat16
I32 = mybir.dt.int32
U32 = mybir.dt.uint32
ALU = mybir.AluOpType
ACT = mybir.ActivationFunctionType
AX = mybir.AxisListType

P = 128
B = 16
S = 256
D = 128
H = 16
HD = D // H
TT = S // P
EPS = 1e-5
NG = 4
RING = 3
PARTS = 3
PAIRS = 6 * HD
SCALE = HD ** -0.5
MAX_AT = [range(3 * s, min(3 * s + 3, 16)) for s in range(8)]
MAGIC = 0x5F3759DF
NEWTON = 3


class Signal:

    def __init__(self, nc, ctx, name, per=1):
        self.sem = ctx.enter_context(nc.semaphore(name))
        self.per = per

    def at(self, b, part=None):
        value = b * self.per + (self.per if part is None else part)
        assert not isinstance(value, int) or value > 0
        return value

    def due(self, b, part=None):
        value = b * self.per + (self.per if part is None else part)
        return not isinstance(value, int) or value > 0


def steady(eng, t):
    eng.nop(nofuse=True)


def newton_steps(t, pool, root, mark, b):
    y, u, v = root[:, 0, :], root[:, 1, :], root[:, 3, :]
    j = 0
    for _ in range(NEWTON):
        if j:
            pool.wait_ge(mark.sem, mark.at(b, j))
        pool.tensor_tensor(u, y, y, ALU.mult).then_inc(mark.sem, 1)
        pool.wait_ge(mark.sem, mark.at(b, j + 1))
        pool.tensor_tensor(u, u, v, ALU.mult).then_inc(mark.sem, 1)
        pool.wait_ge(mark.sem, mark.at(b, j + 2))
        steady(pool, t)
        pool.tensor_scalar(u, u, -0.5, 1.5, ALU.mult, ALU.add).then_inc(mark.sem, 1)
        pool.wait_ge(mark.sem, mark.at(b, j + 3))
        pool.tensor_tensor(y, y, u, ALU.mult).then_inc(mark.sem, 1)
        j += 4


def attention_and_recurrence(nc, ctx, t, out_dbg=None):

    def sb(name, shape, dt=F32):
        return ctx.enter_context(nc.sbuf_tensor(name, shape, dt))

    def sig(name, per=1):
        return Signal(nc, ctx, name, per)

    with ExitStack() as scope:
        def psum(name, cols=512):
            return scope.enter_context(nc.psum_tensor(name, [P, cols], F32))

        def tmp(name, shape, dt=F32):
            return scope.enter_context(nc.sbuf_tensor(name, shape, dt))

        X, XN2T, state = t["X"], t["XN2T"], t["state"]
        ident, ident16 = t["ident"], t["ident16"]

        Wqkv, Wout = tmp("Wqkv", [P, 3 * D]), tmp("Wout", [P, D])
        bqk, bqk_s = tmp("bqk", [P, 2]), tmp("bqk_s", [P, 2])
        bv, bo = tmp("bv", [P, D]), tmp("bo", [P, D])
        gates_w, gates_u, gates_uh = tmp("gates_w", [P, 3, D]), tmp("gates_u", [P, 3, D]), tmp("gates_uh", [P, 3, D])
        gates_b, gates_bh = tmp("gates_b", [P, 3]), tmp("gates_bh", [P, 3])
        c_start, zeros = tmp("c_start", [P, 1]), tmp("zeros", [P, S])

        stats1, mv1 = [tmp(f"stats1_{r}", [P, TT, 6]) for r in range(RING)], [tmp(f"mv1_{r}", [P, TT, 2]) for r in range(RING)]
        stats2, mv2 = [tmp(f"stats2_{r}", [P, TT, 6]) for r in range(RING)], [tmp(f"mv2_{r}", [P, TT, 2]) for r in range(RING)]
        root1, root2 = [tmp(f"root1_{r}", [P, 5, TT]) for r in range(RING)], [tmp(f"root2_{r}", [P, 5, TT]) for r in range(RING)]
        xn1 = [tmp(f"xn1_{r}", [P, TT, D]) for r in range(RING)]
        xn1T = [tmp(f"xn1T_{r}", [P, S]) for r in range(RING)]
        qk = [tmp(f"qk_{r}", [P, 2, S]) for r in range(RING)]
        part = tmp("part", [P, PARTS, 2, S], BF16)
        rest = tmp("rest", [P, 2, S])
        QS = [tmp(f"QS_{r}", [PAIRS + PARTS, H, S], BF16) for r in range(RING)]
        KS = [tmp(f"KS_{r}", [PAIRS + PARTS, H, S], BF16) for r in range(RING)]
        V = [tmp(f"V_{r}", [P, TT, H, 32]) for r in range(RING)]
        negmax = tmp("negmax", [P, TT, H])
        maxrest = tmp("maxrest", [P, TT, H])
        maxpart = tmp("maxpart", [P, TT, PARTS, H], BF16)
        maxT = tmp("maxT", [PARTS * H, S], BF16)
        probs = [tmp(f"probs_{r}", [P, 4, S]) for r in range(2)]
        OT = [tmp(f"OT_{r}", [P, NG, S]) for r in range(RING)]
        rz = tmp("rz", [P, TT, H])
        on = tmp("on", [P, TT, D])
        onT = tmp("onT", [P, S])
        xb = [tmp(f"xb_{r}", [P, TT, D]) for r in range(RING)]
        xn2 = [tmp(f"xn2_{r}", [P, TT, D]) for r in range(RING)]
        xn2T = tmp("xn2T", [P, S])
        gate = tmp("gate", [P, 3, S])
        ca, cb = tmp("ca", [P, S]), tmp("cb", [P, S])

        p_exp = [psum(f"p_exp{i}", 1024) for i in range(2)]
        p_max = [psum(f"p_max{i}") for i in range(2)]
        p_out = psum("p_out")
        p_misc = psum("p_misc")

        scratch = [nc.dram_tensor(f"scratch_{r}", [2, PARTS, HD, H, S], BF16).ap() for r in range(RING)]

        x_in = [sig(f"x_in{i}") for i in range(3)]
        w_in = sig("w_in")
        consts = t["consts"]
        setup_done = sig("setup_done", 8)
        stats_a = sig("stats_a", 4)
        seed_a = sig("seed_a", 3)
        newton_a = sig("newton_a", 4 * NEWTON)
        norm_a = sig("norm_a", 2)
        xnT_p = sig("xnT_p")
        xnT_s = sig("xnT_s")
        qk_p = sig("qk_p")
        qk_s = sig("qk_s", 4)
        v_p = sig("v_p")
        v_s = sig("v_s")
        split = sig("split", 3)
        parts_out = sig("parts_out", 16 * 2 * PARTS)
        stack_in = sig("stack_in", 16 * 6)
        max_p = sig("max_p", 16)
        max_s = sig("max_s", 16)
        msplit = sig("msplit", 5)
        maxT_p = sig("maxT_p")
        maxT_s = sig("maxT_s")
        maxrow_in = sig("maxrow_in", 16 * PARTS)
        score_p = sig("score_p", 8)
        prob_s = sig("prob_s", 8)
        pv_p = sig("pv_p", 8)
        OT_s = sig("OT_s", 4)
        xb_s = sig("xb_s")
        OQ_p = sig("OQ_p", 2)
        rz_s = sig("rz_s", 2)
        on_s = sig("on_s", 2)
        onT_p = sig("onT_p")
        onT_s = sig("onT_s")
        proj_p = sig("proj_p")
        x1_s = sig("x1_s")
        stats_b = sig("stats_b", 4)
        seed_b = sig("seed_b", 3)
        newton_b = sig("newton_b", 4 * NEWTON)
        norm_b = sig("norm_b", 2)
        xn2T_p = sig("xn2T_p")
        xn2T_s = sig("xn2T_s")
        xn2T_k = sig("xn2T_k")
        gfi_p = sig("gfi_p")
        gfi_s = sig("gfi_s", 2)
        gc_p = sig("gc_p")
        gc_s = sig("gc_s")
        cell = sig("cell", 3)
        t["cell"], t["x1_s"], t["xn2T_k"] = cell, x1_s, xn2T_k

        LAST = B + 5
        PEEL = 6

        def pipeline(eng, iteration):
            for n in range(-1, PEEL):
                iteration(n, n % RING)
            with eng.Fori(0, (B - 1 - PEEL) // RING, 1) as k:
                for c in range(RING):
                    iteration(k * RING + (PEEL + c), (PEEL + c) % RING)
            for n in range(B - 1, LAST):
                iteration(n, n % RING)

        def active(n, lag):
            return not isinstance(n, int) or 0 <= n - lag < B

        def at(n, first):
            return isinstance(n, int) and n == first

        block = scope.enter_context(nc.Block())

        @block.sync
        def _(sp):
            xv = t["x_dram"].rearrange("(n p) d -> p n d", p=P)
            sp.dma_start(X[:, 0:2, :], xv[:, 0:2, :]).then_inc(x_in[0].sem, 16)
            sp.dma_start(Wqkv[:, :], t["Wqkv"]).then_inc(w_in.sem, 16)
            sp.dma_start(bqk[:, :], t["bqk"]).then_inc(w_in.sem, 16)
            sp.dma_start(bv[:, :], t["bv"].partition_broadcast(P)).then_inc(w_in.sem, 16)
            sp.dma_start(bo[:, :], t["bout"].partition_broadcast(P)).then_inc(w_in.sem, 16)
            sp.dma_start(X[:, 2:4, :], xv[:, 2:4, :]).then_inc(x_in[1].sem, 16)
            sp.dma_start(X[:, 4:2 * B, :], xv[:, 4:2 * B, :]).then_inc(x_in[2].sem, 16)
            sp.dma_start(Wout[:, :], t["Wout"]).then_inc(w_in.sem, 16)
            sp.dma_start(gates_w[:, :, :], t["gates_w"]).then_inc(w_in.sem, 16)
            sp.dma_start(gates_u[:, :, :], t["gates_u"]).then_inc(w_in.sem, 16)
            sp.dma_start(gates_b[:, :], t["gates_b"]).then_inc(w_in.sem, 16)
            sp.dma_start(c_start[:, :], t["in_c"]).then_inc(w_in.sem, 16)

            def iteration(n, r):
                if at(n, 2):
                    for dst, src in t["w2_loads"]:
                        sp.dma_start(dst[tuple(slice(None) for _ in dst.shape)], src).then_inc(t["w2"]["loaded"].sem, 16)
                if active(n, 0):
                    b = n
                    if stack_in.due(b - 1):
                        sp.wait_ge(stack_in.sem, stack_in.at(b - 1))
                    for i in range(PARTS):
                        if i == 0:
                            sp.wait_ge(qk_s.sem, qk_s.at(b))
                        else:
                            sp.wait_ge(split.sem, split.at(b, 1 + i))
                        for j in range(2):
                            sp.dma_start(scratch[r][j, i].rearrange("d h t -> h d t"), part[:, i, j, :])\
                                .then_inc(parts_out.sem, 16)
                    sp.wait_ge(parts_out.sem, parts_out.at(b))
                    if score_p.due(b - RING):
                        sp.wait_ge(score_p.sem, score_p.at(b - RING))
                    first = 0
                    for i in range(PARTS):
                        k = PARTS - i
                        src = scratch[r][0, i].rearrange("(o d) h t -> o d (h t)", o=1)
                        sp.dma_start(QS[r][first:first + k * HD, :, :], src.broadcast_to([k, HD, H * S])).then_inc(stack_in.sem, 16)
                        sp.dma_start(KS[r][first:first + k * HD, :, :], scratch[r][1, 0:k].rearrange("k d h t -> (k d) (h t)"))\
                            .then_inc(stack_in.sem, 16)
                        first += k * HD
                if active(n, 1):
                    b, q = n - 1, (r - 1) % RING
                    sp.wait_ge(maxT_s.sem, maxT_s.at(b))
                    sp.wait_ge(stack_in.sem, stack_in.at(b))
                    for i in range(PARTS):
                        sp.dma_start(QS[q][PAIRS + i:PAIRS + i + 1, :, :], maxT[i * H:(i + 1) * H, :])\
                            .then_inc(maxrow_in.sem, 16)
                    sp.wait_ge(maxrow_in.sem, maxrow_in.at(b))
                    steady(sp, t)

            pipeline(sp, iteration)

        @block.gpsimd
        def _(pool):
            for r in range(RING):
                pool.memset(KS[r][:, :, :], 1.0).then_inc(setup_done.sem, 1)
            pool.wait_ge(w_in.sem, w_in.at(0, 16 * 9))
            pool.tensor_scalar(bqk_s[:, :], bqk[:, :], SCALE, None, ALU.mult).then_inc(setup_done.sem, 1)
            pool.tensor_scalar(gates_uh[:, :, :], gates_u[:, :, :], 0.5, None, ALU.mult).then_inc(setup_done.sem, 1)
            pool.tensor_scalar(gates_bh[:, :], gates_b[:, :], 0.5, None, ALU.mult).then_inc(setup_done.sem, 1)
            pool.memset(zeros[:, :], 0.0).then_inc(setup_done.sem, 1)
            pool.wait_ge(setup_done.sem, 7)
            pool.tensor_scalar(state[:, :], zeros[:, :], c_start[:, 0:1], 2.0, ALU.add, ALU.mult)\
                .then_inc(setup_done.sem, 1)

            newton = lambda root, mark, b: newton_steps(t, pool, root, mark, b)

            def iteration(n, r):
                if active(n, 0):
                    pool.wait_ge(split.sem, split.at(n, 2))
                    if parts_out.due(n - 1):
                        pool.wait_ge(parts_out.sem, parts_out.at(n - 1))
                    pool.tensor_tensor(part[:, 2, :, :], rest[:, :, :], part[:, 1, :, :], ALU.subtract).then_inc(split.sem, 1)
                if active(n, 2):
                    b, q = n - 2, (r - 2) % RING
                    if x1_s.due(b - RING):
                        pool.wait_ge(x1_s.sem, x1_s.at(b - RING))
                    steady(pool, t)
                    pool.tensor_tensor(xb[q][:, :, :], X[:, bass.ds(2 * b, 2), :],
                                       bo[:, :].rearrange("p (o d) -> p o d", o=1).broadcast_to([P, TT, D]), ALU.add)\
                        .then_inc(xb_s.sem, 1)
                if active(n, 3):
                    b, q = n - 3, (r - 3) % RING
                    pool.wait_ge(seed_b.sem, seed_b.at(b))
                    newton(root2[q], newton_b, b)
                if active(n, -1):
                    pool.wait_ge(seed_a.sem, seed_a.at(n + 1))
                    newton(root1[(r + 1) % RING], newton_a, n + 1)

            pipeline(pool, iteration)

        @block.vector
        def _(dve):
            for r in range(RING):
                dve.memset(V[r][:, :, :, :], 0.0).then_inc(t["v_set"].sem, 1)
            dve.wait_ge(t["v_set"].sem, 3)
            for r in range(RING):
                dve.memset(V[r][:, :, :, HD:HD + 1], 1.0).then_inc(t["v_set"].sem, 1)
            dve.wait_ge(t["v_set"].sem, 6)

            def layer_stats(b, stats, mv, root, st, sd, prev_norm):
                steady(dve, t)
                for i in range(TT):
                    dve.bn_stats(stats[:, i, :], X[:, 2 * b + i, :]).then_inc(st.sem, 1)
                if prev_norm.due(b - RING):
                    dve.wait_ge(prev_norm.sem, prev_norm.at(b - RING))
                for i in range(TT):
                    dve.wait_ge(st.sem, st.at(b, 1 + i))
                    steady(dve, t)
                    dve.bn_aggr(mv[:, i, :], stats[:, i, :]).then_inc(st.sem, 1)
                dve.wait_ge(st.sem, st.at(b))
                dve.tensor_scalar(root[:, 3, :], mv[:, :, 1], EPS, None, ALU.add).then_inc(sd.sem, 1)
                dve.wait_ge(sd.sem, sd.at(b, 1))
                dve.tensor_scalar(root[:, 4, :].bitcast(U32), root[:, 3, :].bitcast(U32), 1, None, ALU.logical_shift_right)\
                    .then_inc(sd.sem, 1)
                dve.wait_ge(sd.sem, sd.at(b, 2))
                dve.tensor_scalar(root[:, 0, :].bitcast(I32), root[:, 4, :].bitcast(I32), -1.0, float(MAGIC), ALU.mult, ALU.add)\
                    .then_inc(sd.sem, 1)

            def layer_norm(b, mv, root, dst, nw, nm):
                dve.wait_ge(nw.sem, nw.at(b))
                for i in range(TT):
                    dve.tensor_scalar(dst[:, i, :], X[:, 2 * b + i, :], mv[:, i, 0:1], root[:, 0, i:i + 1], ALU.subtract, ALU.mult)\
                        .then_inc(nm.sem, 1)

            def row_max(b, u):
                i, hp = u // 8, u % 8
                dve.wait_ge(max_p.sem, max_p.at(b, u + 1))
                if u == 0:
                    if msplit.due(b - 1):
                        dve.wait_ge(msplit.sem, msplit.at(b - 1))
                dve.tensor_reduce(negmax[:, i, 2 * hp:2 * hp + 2], p_max[u % 2][:, :].rearrange("p (h k) -> p h k", h=2),
                                  AX.X, ALU.max, negate=True).then_inc(max_s.sem, 1)

            def split_max(b):
                dve.wait_ge(max_s.sem, max_s.at(b))
                if maxT_p.due(b - 1):
                    dve.wait_ge(maxT_p.sem, maxT_p.at(b - 1))
                hs = [maxpart[:, :, i, :] for i in range(PARTS)]
                dve.tensor_copy(hs[0], negmax[:, :, :]).then_inc(msplit.sem, 1)
                dve.wait_ge(msplit.sem, msplit.at(b, 1))
                dve.tensor_tensor(maxrest[:, :, :], negmax[:, :, :], hs[0], ALU.subtract).then_inc(msplit.sem, 1)
                dve.wait_ge(msplit.sem, msplit.at(b, 2))
                dve.tensor_copy(hs[1], maxrest[:, :, :]).then_inc(msplit.sem, 1)
                dve.wait_ge(msplit.sem, msplit.at(b, 3))
                dve.tensor_tensor(hs[2], maxrest[:, :, :], hs[1], ALU.subtract).then_inc(msplit.sem, 2)

            def step_cell(b):
                dve.wait_ge(gfi_s.sem, gfi_s.at(b))
                if at(b, 0):
                    dve.wait_ge(setup_done.sem, 8)
                dve.scalar_tensor_tensor(out=ca[:, :], in0=gate[:, 0, :], scalar=1.0, in1=state[:, :], op0=ALU.add, op1=ALU.mult)\
                    .then_inc(cell.sem, 1)
                dve.wait_ge(gc_s.sem, gc_s.at(b))
                dve.scalar_tensor_tensor(out=cb[:, :], in0=gate[:, 1, :], scalar=1.0, in1=gate[:, 2, :], op0=ALU.add, op1=ALU.mult)\
                    .then_inc(cell.sem, 1)
                dve.wait_ge(cell.sem, cell.at(b, 2))
                dve.scalar_tensor_tensor(out=state[:, :], in0=ca[:, :], scalar=0.5, in1=cb[:, :], op0=ALU.mult, op1=ALU.add)\
                    .then_inc(cell.sem, 1)

            def quotient(b, i):
                dve.wait_ge(OQ_p.sem, OQ_p.at(b, i + 1))
                if onT_p.due(b - 1):
                    dve.wait_ge(onT_p.sem, onT_p.at(b - 1))
                heads = p_misc[:, :].rearrange("p (h c) -> p h c", c=32)
                dve.reciprocal(rz[:, i, :], heads[:, :, HD]).then_inc(rz_s.sem, 1)
                dve.wait_ge(rz_s.sem, rz_s.at(b, i + 1))
                dve.tensor_tensor(on[:, i, :].rearrange("p (h d) -> p h d", d=HD), heads[:, :, 0:HD],
                                  rz[:, i, :].rearrange("p (h o) -> p h o", o=1).broadcast_to([P, H, HD]), ALU.mult)\
                    .then_inc(on_s.sem, 1)

            def iteration(n, r):
                for i in range(3):
                    if at(n, i - 1):
                        dve.wait_ge(x_in[i].sem, 16)
                for s in range(8):
                    if active(n, 1):
                        for u in MAX_AT[s]:
                            row_max(n - 1, u)
                    if s == 0 and active(n, 5):
                        step_cell(n - 5)
                    if s == 2 and active(n, 0):
                        dve.wait_ge(qk_s.sem, qk_s.at(n))
                        if split.due(n - 1):
                            dve.wait_ge(split.sem, split.at(n - 1))
                        if parts_out.due(n - 1):
                            dve.wait_ge(parts_out.sem, parts_out.at(n - 1))
                        dve.tensor_tensor(rest[:, :, :], qk[r][:, :, :], part[:, 0, :, :], ALU.subtract).then_inc(split.sem, 1)
                        dve.wait_ge(split.sem, split.at(n, 1))
                        dve.tensor_copy(part[:, 1, :, :], rest[:, :, :]).then_inc(split.sem, 1)
                    if s == 2 and active(n, 0):
                        dve.wait_ge(v_p.sem, v_p.at(n))
                        if pv_p.due(n - RING):
                            dve.wait_ge(pv_p.sem, pv_p.at(n - RING))
                        dve.tensor_tensor(V[r][:, :, :, 0:HD], p_misc[:, 0:S].rearrange("p (i h d) -> p i h d", i=TT, d=HD),
                                          bv[:, :].rearrange("p (o h d) -> p o h d", o=1, d=HD).broadcast_to([P, TT, H, HD]), ALU.add)\
                            .then_inc(v_s.sem, 1)
                    if s == 3 and active(n, 3):
                        quotient(n - 3, 0)
                        quotient(n - 3, 1)
                    if s == 4 and active(n, 3):
                        b, q = n - 3, (r - 3) % RING
                        dve.wait_ge(proj_p.sem, proj_p.at(b))
                        dve.wait_ge(xb_s.sem, xb_s.at(b))
                        dve.tensor_tensor(X[:, bass.ds(2 * b, 2), :], p_misc[:, 0:S].rearrange("p (i d) -> p i d", i=TT), xb[q][:, :, :], ALU.add)\
                            .then_inc(x1_s.sem, 1)
                        dve.wait_ge(x1_s.sem, x1_s.at(b))
                        layer_stats(b, stats2[q], mv2[q], root2[q], stats_b, seed_b, norm_b)
                    if s == 5 and active(n, 1):
                        split_max(n - 1)
                    if s == 5 and active(n, -1):
                        q = (r + 1) % RING
                        layer_stats(n + 1, stats1[q], mv1[q], root1[q], stats_a, seed_a, norm_a)
                    if s == 6 and active(n, 3):
                        b, q = n - 3, (r - 3) % RING
                        if xn2T_p.due(b - RING):
                            dve.wait_ge(xn2T_p.sem, xn2T_p.at(b - RING))
                        layer_norm(b, mv2[q], root2[q], xn2[q], newton_b, norm_b)
                    if s == 7 and active(n, -1):
                        q = (r + 1) % RING
                        if xnT_p.due(n + 1 - RING):
                            dve.wait_ge(xnT_p.sem, xnT_p.at(n + 1 - RING))
                        layer_norm(n + 1, mv1[q], root1[q], xn1[q], newton_a, norm_a)

            pipeline(dve, iteration)

        @block.scalar
        def _(act):
            def iteration(n, r):
                for s in range(8):
                    if s == 0 and active(n, 0):
                        act.wait_ge(xnT_p.sem, xnT_p.at(n))
                        if v_p.due(n - RING):
                            act.wait_ge(v_p.sem, v_p.at(n - RING))
                        act.activation(xn1T[r][:, :], p_misc[:, 0:S], ACT.Copy).then_inc(xnT_s.sem, 1)
                    if s == 1 and active(n, 0):
                        act.wait_ge(qk_p.sem, qk_p.at(n))
                        if parts_out.due(n - 1):
                            act.wait_ge(parts_out.sem, parts_out.at(n - 1))
                        if split.due(n - 1):
                            act.wait_ge(split.sem, split.at(n - 1))
                        if at(n, 0):
                            act.wait_ge(setup_done.sem, 8)
                        for j, sc in enumerate((SCALE, 1.0)):
                            for dst in (qk[r][:, j, :], part[:, 0, j, :]):
                                act.activation(dst, p_misc[:, j * S:(j + 1) * S], ACT.Identity,
                                               bias=(bqk_s if j == 0 else bqk)[:, j:j + 1], scale=sc).then_inc(qk_s.sem, 1)
                    if s == 4 and active(n, 3):
                        b = n - 3
                        act.wait_ge(onT_p.sem, onT_p.at(b))
                        if proj_p.due(b - 1):
                            act.wait_ge(proj_p.sem, proj_p.at(b - 1))
                        act.activation(onT[:, :], p_misc[:, 0:S], ACT.Copy).then_inc(onT_s.sem, 1)
                    if s == 5 and active(n, 4):
                        b = n - 4
                        act.wait_ge(xn2T_p.sem, xn2T_p.at(b))
                        if gc_p.due(b - 1):
                            act.wait_ge(gc_p.sem, gc_p.at(b - 1))
                        act.activation(xn2T[:, :], p_misc[:, 0:S], ACT.Copy).then_inc(xn2T_s.sem, 1)
                        act.activation(XN2T[:, b, :], p_misc[:, 0:S], ACT.Copy).then_inc(xn2T_k.sem, 1)
                    if s == 6 and active(n, 4):
                        b = n - 4
                        act.wait_ge(gfi_p.sem, gfi_p.at(b))
                        if cell.due(b - 1):
                            act.wait_ge(cell.sem, cell.at(b - 1))
                        for j in range(2):
                            act.activation(gate[:, j, :], p_misc[:, j * S:(j + 1) * S], ACT.Tanh, bias=gates_bh[:, j:j + 1], scale=0.5)\
                                .then_inc(gfi_s.sem, 1)
                    if s == 7 and active(n, 1):
                        b = n - 1
                        act.wait_ge(maxT_p.sem, maxT_p.at(b))
                        if maxrow_in.due(b - 1):
                            act.wait_ge(maxrow_in.sem, maxrow_in.at(b - 1))
                        act.activation(maxT[:, :], p_misc[0:PARTS * H, 0:S // 2].bitcast(BF16), ACT.Copy).then_inc(maxT_s.sem, 1)
                    if active(n, 2):
                        b = n - 2
                        if score_p.due(b, s + 1):
                            act.wait_ge(score_p.sem, score_p.at(b, s + 1))
                        if pv_p.due(b, s - 1):
                            act.wait_ge(pv_p.sem, pv_p.at(b, s - 1))
                        act.activation(probs[s % 2][:, :, :].rearrange("p j q -> p (j q)"), p_exp[s % 2][:, :], ACT.Exp)\
                            .then_inc(prob_s.sem, 1)
                        if s % 2 == 0 and s > 0:
                            copy_out(n - 2, (r - 2) % RING, s // 2 - 1)
                    if s == 7 and active(n, 4):
                        b = n - 4
                        act.wait_ge(gc_p.sem, gc_p.at(b))
                        act.activation(gate[:, 2, :], p_misc[:, 0:S], ACT.Tanh, bias=gates_b[:, 2:3]).then_inc(gc_s.sem, 1)
                if active(n, 2):
                    copy_out(n - 2, (r - 2) % RING, 3)

            def copy_out(b, q, g):
                act.wait_ge(pv_p.sem, pv_p.at(b, 2 * g + 2))
                if g == 0:
                    if OQ_p.due(b - RING):
                        act.wait_ge(OQ_p.sem, OQ_p.at(b - RING))
                act.activation(OT[q][:, g, :], p_out[:, 0:S], ACT.Copy).then_inc(OT_s.sem, 1)

            pipeline(act, iteration)

        @block.tensor
        def _(pe):
            def scores(b, q, s):
                g, kt = s // 2, s % 2
                if prob_s.due(b, s - 1):
                    pe.wait_ge(prob_s.sem, prob_s.at(b, s - 1))
                for j in range(4):
                    h = 4 * g + j
                    mm = pe.matmul(p_exp[s % 2][:, j * S:(j + 1) * S], KS[q][:, h, kt * P:(kt + 1) * P], QS[q][:, h, :],
                                   start=True, stop=True)
                mm.then_inc(score_p.sem, 1)

            def weigh(b, q, s):
                g, kt = s // 2, s % 2
                if prob_s.due(b, s + 1):
                    pe.wait_ge(prob_s.sem, prob_s.at(b, s + 1))
                if s == 0:
                    pe.wait_ge(v_s.sem, v_s.at(b))
                if kt == 0:
                    if OT_s.due(b, g):
                        pe.wait_ge(OT_s.sem, OT_s.at(b, g))
                for j in range(4):
                    mm = pe.matmul(p_out[32 * j:32 * j + 32, 0:S], V[q][:, kt, 4 * g + j, :], probs[s % 2][:, j, :],
                                   start=(kt == 0), stop=(kt == 1))
                mm.then_inc(pv_p.sem, 1)

            def maxima(b, q, u):
                i, hp = u // 8, u % 8
                if max_s.due(b, u - 1):
                    pe.wait_ge(max_s.sem, max_s.at(b, u - 1))
                for j in range(2):
                    h = 2 * hp + j
                    mm = pe.matmul(p_max[u % 2][:, j * S:(j + 1) * S], QS[q][0:PAIRS, h, i * P:(i + 1) * P], KS[q][0:PAIRS, h, :],
                                   start=True, stop=True)
                mm.then_inc(max_p.sem, 1)

            def turn(src, n_tiles=TT):
                for i in range(n_tiles):
                    mm = pe.transpose(p_misc[:, i * P:(i + 1) * P], src[:, i, :], ident[:, :])
                return mm

            def misc(n, r, at_slot):
                b3, b4, q3, q4 = n - 3, n - 4, (r - 3) % RING, (r - 4) % RING
                if at_slot == "0" and active(n, 0):
                    pe.wait_ge(norm_a.sem, norm_a.at(n))
                    if active(n, 5):
                        if gc_s.due(n - 5):
                            pe.wait_ge(gc_s.sem, gc_s.at(n - 5))
                    elif active(n, 2):
                        if maxT_s.due(n - 2):
                            pe.wait_ge(maxT_s.sem, maxT_s.at(n - 2))
                    elif active(n, 1):
                        if v_s.due(n - 1):
                            pe.wait_ge(v_s.sem, v_s.at(n - 1))
                    turn(xn1[r]).then_inc(xnT_p.sem, 1)
                if at_slot == "1" and active(n, 0):
                    pe.wait_ge(xnT_s.sem, xnT_s.at(n))
                    for j in range(2):
                        mm = pe.matmul(p_misc[:, j * S:(j + 1) * S], Wqkv[:, j * D:(j + 1) * D], xn1T[r][:, :], start=True, stop=True)
                    mm.then_inc(qk_p.sem, 1)
                if at_slot == "2" and active(n, 0):
                    pe.wait_ge(qk_s.sem, qk_s.at(n))
                    for i in range(TT):
                        mm = pe.matmul(p_misc[:, i * P:(i + 1) * P], xn1T[r][:, i * P:(i + 1) * P], Wqkv[:, 2 * D:3 * D], start=True, stop=True)
                    mm.then_inc(v_p.sem, 1)
                if at_slot in ("3", "3b") and active(n, 3):
                    i = ("3", "3b").index(at_slot)
                    if i:
                        pe.wait_ge(on_s.sem, on_s.at(b3, 1))
                    else:
                        pe.wait_ge(OT_s.sem, OT_s.at(b3))
                        if active(n, 0):
                            pe.wait_ge(v_s.sem, v_s.at(n))
                        elif active(n, 5):
                            if gc_s.due(n - 5):
                                pe.wait_ge(gc_s.sem, gc_s.at(n - 5))
                    for g in range(NG):
                        mm = pe.transpose(p_misc[:, g * P:(g + 1) * P], OT[q3][:, g, i * P:(i + 1) * P], ident[:, :])
                    mm.then_inc(OQ_p.sem, 1)
                if at_slot == "4" and active(n, 3):
                    pe.wait_ge(on_s.sem, on_s.at(b3))
                    turn(on).then_inc(onT_p.sem, 1)
                if at_slot == "4b" and active(n, 3):
                    pe.wait_ge(onT_s.sem, onT_s.at(b3))
                    for i in range(TT):
                        mm = pe.matmul(p_misc[:, i * P:(i + 1) * P], onT[:, i * P:(i + 1) * P], Wout[:, :], start=True, stop=True)
                    mm.then_inc(proj_p.sem, 1)
                if at_slot == "5" and active(n, 4):
                    pe.wait_ge(norm_b.sem, norm_b.at(b4))
                    if active(n, 3):
                        pe.wait_ge(x1_s.sem, x1_s.at(b3))
                    else:
                        if gc_s.due(n - 5):
                            pe.wait_ge(gc_s.sem, gc_s.at(n - 5))
                    turn(xn2[q4]).then_inc(xn2T_p.sem, 1)
                if at_slot == "6" and active(n, 4):
                    pe.wait_ge(xn2T_s.sem, xn2T_s.at(b4))
                    pe.wait_ge(xn2T_k.sem, xn2T_k.at(b4))
                    if cell.due(b4 - 1):
                        pe.wait_ge(cell.sem, cell.at(b4 - 1))
                    for j in range(2):
                        pe.matmul(p_misc[:, j * S:(j + 1) * S], gates_w[:, j, :], xn2T[:, :], start=True, stop=False)
                        mm = pe.matmul(p_misc[:, j * S:(j + 1) * S], gates_uh[:, j, :], state[:, :], start=False, stop=True)
                    mm.then_inc(gfi_p.sem, 1)
                if at_slot == "7" and active(n, 1):
                    if msplit.due(n - 1):
                        pe.wait_ge(msplit.sem, msplit.at(n - 1))
                    if active(n, 4):
                        pe.wait_ge(gfi_s.sem, gfi_s.at(b4))
                    elif active(n, 3):
                        pe.wait_ge(x1_s.sem, x1_s.at(b3))
                    else:
                        pe.wait_ge(v_s.sem, v_s.at(n))
                    steady(pe, t)
                    for i in range(TT):
                        mm = pe.transpose(p_misc[0:PARTS * H, i * P // 2:(i + 1) * P // 2].bitcast(BF16),
                                          maxpart[:, i, :, :].rearrange("p k h -> p (k h)"), ident16[:, :])
                    mm.then_inc(maxT_p.sem, 1)
                if at_slot == "7b" and active(n, 4):
                    if active(n, 1):
                        if maxT_s.due(n - 1):
                            pe.wait_ge(maxT_s.sem, maxT_s.at(n - 1))
                    pe.wait_ge(gfi_s.sem, gfi_s.at(b4))
                    pe.matmul(p_misc[:, 0:S], gates_w[:, 2, :], xn2T[:, :], start=True, stop=False)
                    pe.matmul(p_misc[:, 0:S], gates_uh[:, 2, :], state[:, :], start=False, stop=True).then_inc(gc_p.sem, 1)

            def iteration(n, r):
                q1, q2 = (r - 1) % RING, (r - 2) % RING
                if at(n, -1):
                    pe.wait_ge(w_in.sem, w_in.at(0, 16 * 9))
                    pe.wait_ge(consts.sem, t["n_consts"])
                    pe.wait_ge(setup_done.sem, 8)
                    pe.wait_ge(t["v_set"].sem, 6)
                if active(n, 1):
                    if stack_in.due(n - 1):
                        pe.wait_ge(stack_in.sem, stack_in.at(n - 1))
                for s in range(8):
                    if active(n, 1):
                        for u in MAX_AT[s]:
                            maxima(n - 1, q1, u)
                    misc(n, r, str(s))
                    if active(n, 2):
                        if s == 0:
                            if maxrow_in.due(n - 2):
                                pe.wait_ge(maxrow_in.sem, maxrow_in.at(n - 2))
                        scores(n - 2, q2, s)
                        if s:
                            weigh(n - 2, q2, s - 1)
                    misc(n, r, str(s) + "b")
                if active(n, 2):
                    weigh(n - 2, q2, 7)

            pipeline(pe, iteration)


E = 16
HID = 256
TOP = 2
TOKENS = B * S
REGION = TOKENS + P
TILES = 80
ROW = D + 2
NOWHERE = float(4 * TOKENS)
PAIR = 2
Z2 = 3 * D


def linear_attention_and_routing(nc, ctx, t):

    def sig(name, per=1):
        return Signal(nc, ctx, name, per)

    with ExitStack() as scope:
        def psum(name, cols=512):
            return scope.enter_context(nc.psum_tensor(name, [P, cols], F32))

        def tmp(name, shape, dt=F32):
            return scope.enter_context(nc.sbuf_tensor(name, shape, dt))

        X, XN2T, state, ident = t["X"], t["XN2T"], t["state"], t["ident"]
        w = t["w2"]
        count = t["count"]
        disp = t["disp"]

        UC = tmp("UC", [P, S])
        uoh = tmp("uoh", [P, D])
        KVones = [tmp(f"KVones_{r}", [P, TT, D + 2]) for r in range(PAIR)]
        zs = [tmp(f"zs_{r}", [P, S]) for r in range(PAIR)]
        hT = [tmp(f"hT_{r}", [P, S]) for r in range(PAIR)]
        stats3, mv3 = [tmp(f"stats3_{r}", [P, TT, 6]) for r in range(PAIR)], [tmp(f"mv3_{r}", [P, TT, 2]) for r in range(PAIR)]
        stats4, mv4 = [tmp(f"stats4_{r}", [P, TT, 6]) for r in range(PAIR)], [tmp(f"mv4_{r}", [P, TT, 2]) for r in range(PAIR)]
        root3, root4 = [tmp(f"root3_{r}", [P, 5, TT]) for r in range(PAIR)], [tmp(f"root4_{r}", [P, 5, TT]) for r in range(PAIR)]
        xn3 = [tmp(f"xn3_{r}", [P, TT, D]) for r in range(PAIR)]
        xn3T = [tmp(f"xn3T_{r}", [P, S]) for r in range(PAIR)]
        t1, t2 = tmp("t1", [P, TT, 2 * D]), tmp("t2", [P, TT, 2 * D])
        rot = [tmp(f"rot_{r}", [P, TT, 2 * D]) for r in range(PAIR)]
        ex, rl = tmp("ex", [P, TT, 2 * D]), tmp("rl", [P, TT, 2 * D])
        feat = [tmp(f"feat_{r}", [P, TT, 2 * D]) for r in range(PAIR)]
        KVm = tmp("KVm", [P, D + H])
        qfT = tmp("qfT", [P, S])
        den, on3, on3T = tmp("den", [P, TT, H]), tmp("on3", [P, TT, D]), tmp("on3T", [P, S])
        pay = [[tmp(f"pay{k}_{r}", [P, TT, ROW]) for k in range(TOP)] for r in range(PAIR)]
        xn4T = tmp("xn4T", [P, S])
        lg, negtop, probs4, z = tmp("lg", [P, TT, E]), tmp("negtop", [P, TT]), tmp("probs4", [P, TT, E]), tmp("z", [P, TT])
        best = tmp("best", [P, TT, 8])
        where = tmp("where", [P, TT, 8], U32)
        wheref = tmp("wheref", [P, TT, TOP])
        hot = [tmp(f"hot_{r}", [P, TT, TOP, E]) for r in range(PAIR)]
        sel = [tmp(f"sel_{r}", [P, TT, E], BF16) for r in range(PAIR)]
        ids = tmp("ids", [P, TT, TOP])
        place, mine, posf = tmp("place", [P, TT, E]), tmp("mine", [P, TT, TOP, E]), tmp("posf", [P, TT, TOP])
        pos = [tmp(f"pos_{r}", [P, TT, TOP], U32) for r in range(PAIR)]
        nup = [count, tmp("count_b", [P, E])]

        p_h, p_t, p_qkv = psum("p_h"), psum("p_t"), psum("p_qkv", 1024)
        p_kv, p_o, p_u, p_r = psum("p_kv"), psum("p_o"), psum("p_u"), psum("p_r")

        uc_ready = sig("uc_ready", 2)
        s2 = sig("setup2")
        z_p, z_s, h_s, hT_p, x2_s = sig("z_p"), sig("z_s"), sig("h_s"), sig("hT_p"), sig("x2_s")
        st3, sd3, nw3, nm3 = sig("st3", 4), sig("sd3", 3), sig("nw3", 4 * NEWTON), sig("nm3", 2)
        x3T_p, x3T_s, qkv_p = sig("x3T_p"), sig("x3T_s"), sig("qkv_p")
        v3_s, t_s, rot_s, el_s, feat_s = sig("v3_s"), sig("t_s", 3), sig("rot_s"), sig("el_s", 2), sig("feat_s")
        kv_p, kv_s, qfT_p, qfT_s, o_p = sig("kv_p"), sig("kv_s", 2), sig("qfT_p"), sig("qfT_s"), sig("o_p")
        o_s, onT3_p, onT3_s, u_p, x3_s = sig("o_s", 3), sig("onT3_p"), sig("onT3_s"), sig("u_p"), sig("x3_s")
        st4, sd4, nw4, nm4, res = sig("st4", 4), sig("sd4", 3), sig("nw4", 4 * NEWTON), sig("nm4", 4), sig("res")
        x4T_p, x4T_s, lg_p, lg_s, ex4_s = sig("x4T_p"), sig("x4T_s"), sig("lg_p"), sig("lg_s", 3), sig("ex4_s")
        pr_s, top_s, hot_s, pay_s = sig("pr_s", 3), sig("top_s", 4), sig("hot_s", 3), sig("pay_s", 5)
        rank_p, pos_s, sent = sig("rank_p"), sig("pos_s", 6), sig("sent", 16 * TT * TOP)
        t["pos_s"], t["sent"], t["res"], t["rank_p"] = pos_s, sent, res, rank_p
        sel_s, gate_in, ids_up = sig("sel_s"), sig("gate_in", TOP), sig("ids_up")

        LAST, PEEL = B + 4, 5

        def active(n, lag):
            return not isinstance(n, int) or 0 <= n - lag < B

        def at(n, first):
            return isinstance(n, int) and n == first

        def pipeline(eng, iteration):
            for n in range(PEEL):
                iteration(n, n % PAIR)
            with eng.Fori(0, (B - 1 - PEEL) // PAIR, 1) as k:
                for c in range(PAIR):
                    iteration(k * PAIR + (PEEL + c), (PEEL + c) % PAIR)
            for n in range(B - 1, LAST):
                iteration(n, n % PAIR)

        block = scope.enter_context(nc.Block())

        @block.gpsimd
        def _(pool):
            pool.wait_ge(w["loaded"].sem, w["loaded"].at(0))
            pool.tensor_scalar(uoh[:, :], w["uo"][:, :], 0.5, None, ALU.mult).then_inc(s2.sem, 1)
            for r in range(PAIR):
                pool.memset(KVones[r][:, :, D:D + 2], 1.0).then_inc(s2.sem, 1)
            pool.iota(ids[:, :, :], pattern=[[2 * P, TT], [1, TOP]], base=0, channel_multiplier=2,
                      allow_small_or_imprecise_dtypes=True).then_inc(s2.sem, 1)

            newton = lambda root, mark, b: newton_steps(t, pool, root, mark, b)

            def iteration(n, r):
                o = 1 - r
                if active(n, 4):
                    b = n - 4
                    pool.wait_ge(pos_s.sem, pos_s.at(b))
                    pool.wait_ge(pay_s.sem, pay_s.at(b))
                    pool.wait_ge(gate_in.sem, gate_in.at(b))
                    pool.wait_ge(nm4.sem, nm4.at(b))
                    if sent.due(b - 1):
                        pool.wait_ge(sent.sem, sent.at(b - 1))
                    steady(pool, t)
                    for i in range(TT):
                        for k in range(TOP):
                            pool.indirect_dma_start(out=disp, out_offset=bass.IndirectOffsetOnAxis(ap=pos[r][:, i, k:k + 1], axis=0),
                                                    in_=pay[r][k][:, i, :], in_offset=None).then_inc(sent.sem, 16)
                if active(n, 0):
                    pool.wait_ge(sd3.sem, sd3.at(n))
                    newton(root3[r], nw3, n)
                if active(n, 2):
                    if sd4.due(n - 2):
                        pool.wait_ge(sd4.sem, sd4.at(n - 2))
                    newton(root4[r], nw4, n - 2)
                if active(n, 1):
                    if t_s.due(n - 1):
                        pool.wait_ge(t_s.sem, t_s.at(n - 1))
                    if el_s.due(n - 1 - PAIR):
                        pool.wait_ge(el_s.sem, el_s.at(n - 1 - PAIR))
                    pool.tensor_tensor(rot[o][:, :, :], t1[:, :, :], t2[:, :, :], ALU.add).then_inc(rot_s.sem, 1)
                if active(n, 2):
                    b = n - 2
                    pool.wait_ge(nm4.sem, nm4.at(b))
                    steady(pool, t)
                    pool.tensor_tensor(X[:, bass.ds(2 * b, 2), :], X[:, bass.ds(2 * b, 2), :], pay[r][0][:, :, 0:D], ALU.add)\
                        .then_inc(res.sem, 1)

            pipeline(pool, iteration)

        @block.vector
        def _(dve):
            def layer_stats(b, stats, mv, root, st, sd, prev_norm):
                steady(dve, t)
                for i in range(TT):
                    dve.bn_stats(stats[:, i, :], X[:, 2 * b + i, :]).then_inc(st.sem, 1)
                if prev_norm.due(b - PAIR):
                    dve.wait_ge(prev_norm.sem, prev_norm.at(b - PAIR))
                for i in range(TT):
                    dve.wait_ge(st.sem, st.at(b, 1 + i))
                    steady(dve, t)
                    dve.bn_aggr(mv[:, i, :], stats[:, i, :]).then_inc(st.sem, 1)
                dve.wait_ge(st.sem, st.at(b))
                dve.tensor_scalar(root[:, 3, :], mv[:, :, 1], EPS, None, ALU.add).then_inc(sd.sem, 1)
                dve.wait_ge(sd.sem, sd.at(b, 1))
                dve.tensor_scalar(root[:, 4, :].bitcast(U32), root[:, 3, :].bitcast(U32), 1, None, ALU.logical_shift_right)\
                    .then_inc(sd.sem, 1)
                dve.wait_ge(sd.sem, sd.at(b, 2))
                dve.tensor_scalar(root[:, 0, :].bitcast(I32), root[:, 4, :].bitcast(I32), -1.0, float(MAGIC), ALU.mult, ALU.add)\
                    .then_inc(sd.sem, 1)

            def layer_norm(b, mv, root, dsts, nw, nm):
                dve.wait_ge(nw.sem, nw.at(b))
                for dst in dsts:
                    for i in range(TT):
                        dve.tensor_scalar(dst[:, i, 0:D], X[:, 2 * b + i, :], mv[:, i, 0:1], root[:, 0, i:i + 1], ALU.subtract, ALU.mult)\
                            .then_inc(nm.sem, 1)

            def wide(ap, shape):
                return ap.broadcast_to(shape)

            def iteration(n, r):
                o = 1 - r
                if active(n, 4):
                    b = n - 4
                    cur, nxt = nup[r], nup[o]
                    dve.wait_ge(rank_p.sem, rank_p.at(b))
                    if at(n, 4):
                        dve.wait_ge(t["count_set"].sem, 2)
                    ranks = p_r[:, 64:64 + TT * E].rearrange("p (i e) -> p i e", i=TT)
                    dve.tensor_tensor(place[:, :, :], ranks, wide(cur[:, :].rearrange("p (o e) -> p o e", o=1), [P, TT, E]), ALU.add)\
                        .then_inc(pos_s.sem, 1)
                    dve.tensor_tensor(nxt[:, :], p_r[:, 96:96 + E], cur[:, :], ALU.add).then_inc(pos_s.sem, 1)
                    dve.wait_ge(pos_s.sem, pos_s.at(b, 2))
                    for i in range(TT):
                        dve.tensor_tensor(mine[:, i, :, :], hot[r][:, i, :, :],
                                          wide(place[:, i, :].rearrange("p (o e) -> p o e", o=1), [P, TOP, E]), ALU.mult).then_inc(pos_s.sem, 1)
                    dve.wait_ge(pos_s.sem, pos_s.at(b, 4))
                    dve.tensor_reduce(posf[:, :, :], mine[:, :, :, :], AX.X, ALU.add).then_inc(pos_s.sem, 1)
                    dve.wait_ge(pos_s.sem, pos_s.at(b, 5))
                    dve.tensor_copy(pos[r][:, :, :], posf[:, :, :]).then_inc(pos_s.sem, 1)
                if active(n, 2):
                    b = n - 2
                    dve.wait_ge(kv_p.sem, kv_p.at(b))
                    if o_p.due(b - 1):
                        dve.wait_ge(o_p.sem, o_p.at(b - 1))
                    dve.tensor_tensor(KVm[:, 0:D], p_kv[:, 0:D], w["block_mask"][:, :], ALU.mult).then_inc(kv_s.sem, 1)
                    dve.tensor_scalar(KVm[:, D:D + H], w["head_mask"][:, :], p_kv[:, D:D + 1], None, ALU.mult).then_inc(kv_s.sem, 1)
                if active(n, 0):
                    dve.wait_ge(z_p.sem, z_p.at(n))
                    if at(n, 0):
                        dve.wait_ge(uc_ready.sem, 2)
                    if h_s.due(n - PAIR):
                        dve.wait_ge(h_s.sem, h_s.at(n - PAIR))
                    dve.tensor_tensor(zs[r][:, :], p_h[:, 0:S], UC[:, :], ALU.add).then_inc(z_s.sem, 1)
                if active(n, 2):
                    b = n - 2
                    dve.wait_ge(o_p.sem, o_p.at(b))
                    if onT3_p.due(b - 1):
                        dve.wait_ge(onT3_p.sem, onT3_p.at(b - 1))
                    outs = p_o[:, :].rearrange("p (i c) -> p i c", i=TT)
                    dve.tensor_scalar(den[:, :, :], outs[:, :, D:D + H], 1e-6, None, ALU.max).then_inc(o_s.sem, 1)
                    dve.wait_ge(o_s.sem, o_s.at(b, 1))
                    dve.reciprocal(den[:, :, :], den[:, :, :]).then_inc(o_s.sem, 1)
                    dve.wait_ge(o_s.sem, o_s.at(b, 2))
                    dve.tensor_tensor(on3[:, :, :].rearrange("p i (h d) -> p i h d", d=HD), outs[:, :, 0:D].rearrange("p i (h d) -> p i h d", d=HD),
                                      wide(den[:, :, :].rearrange("p i (h o) -> p i h o", o=1), [P, TT, H, HD]), ALU.mult).then_inc(o_s.sem, 1)
                if active(n, 0):
                    dve.wait_ge(hT_p.sem, hT_p.at(n))
                    dve.tensor_tensor(X[:, bass.ds(2 * n, 2), :], p_h[:, 0:S].rearrange("p (i d) -> p i d", i=TT), X[:, bass.ds(2 * n, 2), :], ALU.add)\
                        .then_inc(x2_s.sem, 1)
                    dve.wait_ge(x2_s.sem, x2_s.at(n))
                    layer_stats(n, stats3[r], mv3[r], root3[r], st3, sd3, nm3)
                if active(n, 3):
                    b = n - 3
                    dve.wait_ge(lg_p.sem, lg_p.at(b))
                    if ex4_s.due(b - 1):
                        dve.wait_ge(ex4_s.sem, ex4_s.at(b - 1))
                    dve.tensor_tensor(lg[:, :, :], p_r[:, 0:TT * E].rearrange("p (i e) -> p i e", i=TT),
                                      wide(w["br"][:, :].rearrange("p (o e) -> p o e", o=1), [P, TT, E]), ALU.add).then_inc(lg_s.sem, 1)
                    dve.wait_ge(lg_s.sem, lg_s.at(b, 1))
                    dve.tensor_reduce(negtop[:, :], lg[:, :, :], AX.X, ALU.max, negate=True).then_inc(lg_s.sem, 1)
                    dve.wait_ge(lg_s.sem, lg_s.at(b, 2))
                    dve.tensor_tensor(lg[:, :, :], lg[:, :, :], wide(negtop[:, :].rearrange("p (i o) -> p i o", o=1), [P, TT, E]), ALU.add)\
                        .then_inc(lg_s.sem, 1)
                if active(n, 1):
                    b = n - 1
                    dve.wait_ge(qkv_p.sem, qkv_p.at(b))
                    if rot_s.due(b - 1):
                        dve.wait_ge(rot_s.sem, rot_s.at(b - 1))
                    qkp = p_qkv[:, :].rearrange("p (i c) -> p i c", i=TT)[:, :, 0:2 * D]
                    dve.tensor_tensor(t1[:, :, :], qkp, w["cosf"][:, :, :], ALU.mult).then_inc(t_s.sem, 1)
                    halves = [x.rearrange("p i (g a d) -> p i g a d", a=2, d=HD // 2) for x in (qkp, t2[:, :, :], w["sinf"][:, :, :])]
                    for a in range(2):
                        dve.tensor_tensor(halves[1][:, :, :, a, :], halves[0][:, :, :, 1 - a, :], halves[2][:, :, :, a, :], ALU.mult)\
                            .then_inc(t_s.sem, 1)
                if active(n, 3):
                    b = n - 3
                    dve.wait_ge(ex4_s.sem, ex4_s.at(b))
                    dve.tensor_reduce(z[:, :], probs4[:, :, :], AX.X, ALU.add).then_inc(pr_s.sem, 1)
                    dve.wait_ge(pr_s.sem, pr_s.at(b, 1))
                    dve.reciprocal(z[:, :], z[:, :]).then_inc(pr_s.sem, 1)
                    dve.wait_ge(pr_s.sem, pr_s.at(b, 2))
                    dve.tensor_tensor(probs4[:, :, :], probs4[:, :, :], wide(z[:, :].rearrange("p (i o) -> p i o", o=1), [P, TT, E]), ALU.mult)\
                        .then_inc(pr_s.sem, 1)
                    dve.wait_ge(pr_s.sem, pr_s.at(b, 3))
                    steady(dve, t)
                    for i in range(TT):
                        dve.max(best[:, i, :], probs4[:, i, :]).then_inc(top_s.sem, 1)
                    for i in range(TT):
                        dve.wait_ge(top_s.sem, top_s.at(b, 1 + i))
                        steady(dve, t)
                        dve.max_index(where[:, i, :], best[:, i, :], probs4[:, i, :]).then_inc(top_s.sem, 1)
                    dve.wait_ge(top_s.sem, top_s.at(b))
                if active(n, 2):
                    b = n - 2
                    dve.wait_ge(u_p.sem, u_p.at(b))
                    dve.tensor_tensor(X[:, bass.ds(2 * b, 2), :], p_u[:, 0:S].rearrange("p (i d) -> p i d", i=TT), X[:, bass.ds(2 * b, 2), :], ALU.add)\
                        .then_inc(x3_s.sem, 1)
                    dve.wait_ge(x3_s.sem, x3_s.at(b))
                    layer_stats(b, stats4[r], mv4[r], root4[r], st4, sd4, nm4)
                if active(n, 3):
                    b = n - 3
                    dve.tensor_copy(wheref[:, :, :], where[:, :, 0:TOP]).then_inc(hot_s.sem, 1)
                    if sent.due(b - PAIR):
                        dve.wait_ge(sent.sem, sent.at(b - PAIR))
                    dve.tensor_tensor(z[:, :], best[:, :, 0], best[:, :, 1], ALU.add).then_inc(pay_s.sem, 1)
                    dve.wait_ge(hot_s.sem, hot_s.at(b, 1))
                    for i in range(TT):
                        dve.tensor_tensor(hot[o][:, i, :, :], wide(w["iota_e"][:, :].rearrange("p (o e) -> p o e", o=1), [P, TOP, E]),
                                          wide(wheref[:, i, :].rearrange("p (k o) -> p k o", o=1), [P, TOP, E]), ALU.is_equal)\
                            .then_inc(hot_s.sem, 1)
                    dve.wait_ge(pay_s.sem, pay_s.at(b, 1))
                    dve.tensor_scalar(z[:, :], z[:, :], 1e-9, None, ALU.max).then_inc(pay_s.sem, 1)
                    dve.wait_ge(hot_s.sem, hot_s.at(b))
                    if rank_p.due(b - PAIR):
                        dve.wait_ge(rank_p.sem, rank_p.at(b - PAIR))
                    dve.tensor_tensor(sel[o][:, :, :], hot[o][:, :, 0, :], hot[o][:, :, 1, :], ALU.add).then_inc(sel_s.sem, 1)
                    dve.wait_ge(pay_s.sem, pay_s.at(b, 2))
                    dve.reciprocal(z[:, :], z[:, :]).then_inc(pay_s.sem, 1)
                    dve.wait_ge(pay_s.sem, pay_s.at(b, 3))
                    for k in range(TOP):
                        dve.tensor_tensor(pay[o][k][:, :, D], best[:, :, k], z[:, :], ALU.mult).then_inc(gate_in.sem, 1)
                    if at(n, 3):
                        dve.wait_ge(s2.sem, 4)
                    for k in range(TOP):
                        dve.tensor_copy(pay[o][k][:, :, D + 1], ids[:, :, k]).then_inc(pay_s.sem, 1)
                    dve.wait_ge(pay_s.sem, pay_s.at(b))
                    dve.tensor_scalar(ids[:, :, :], ids[:, :, :], float(TOP * S), None, ALU.add).then_inc(ids_up.sem, 1)
                    dve.wait_ge(ids_up.sem, ids_up.at(b))
                if active(n, 0):
                    if x3T_p.due(n - PAIR):
                        dve.wait_ge(x3T_p.sem, x3T_p.at(n - PAIR))
                    layer_norm(n, mv3[r], root3[r], [xn3[r]], nw3, nm3)
                if active(n, 1):
                    b = n - 1
                    dve.wait_ge(el_s.sem, el_s.at(b))
                    if qfT_p.due(b - PAIR):
                        dve.wait_ge(qfT_p.sem, qfT_p.at(b - PAIR))
                    dve.scalar_tensor_tensor(out=feat[o][:, :, :], in0=ex[:, :, :], scalar=1.0, in1=rl[:, :, :], op0=ALU.min, op1=ALU.add)\
                        .then_inc(feat_s.sem, 1)
                if active(n, 2):
                    if sent.due(n - 2 - PAIR):
                        dve.wait_ge(sent.sem, sent.at(n - 2 - PAIR))
                    if res.due(n - 2 - PAIR):
                        dve.wait_ge(res.sem, res.at(n - 2 - PAIR))
                    layer_norm(n - 2, mv4[r], root4[r], pay[r], nw4, nm4)

            pipeline(dve, iteration)

        @block.scalar
        def _(act):
            act.wait_ge(uc_ready.sem, 1)
            act.activation(UC[:, :], p_u[:, 0:S], ACT.Identity, bias=w["bo"][:, 0:1]).then_inc(uc_ready.sem, 1)

            def iteration(n, r):
                o = 1 - r
                if active(n, 2):
                    if qfT_p.due(n - 2):
                        act.wait_ge(qfT_p.sem, qfT_p.at(n - 2))
                    if o_p.due(n - 3):
                        act.wait_ge(o_p.sem, o_p.at(n - 3))
                    act.activation(qfT[:, :], p_t[:, 0:S], ACT.Copy).then_inc(qfT_s.sem, 1)
                if active(n, 0):
                    act.wait_ge(z_s.sem, z_s.at(n))
                    if hT_p.due(n - PAIR):
                        act.wait_ge(hT_p.sem, hT_p.at(n - PAIR))
                    act.activation(hT[r][:, :], zs[r][:, :], ACT.Tanh).then_inc(h_s.sem, 1)
                if active(n, 3):
                    if x4T_p.due(n - 3):
                        act.wait_ge(x4T_p.sem, x4T_p.at(n - 3))
                    if lg_p.due(n - 4):
                        act.wait_ge(lg_p.sem, lg_p.at(n - 4))
                    act.activation(xn4T[:, :], p_t[:, 0:S], ACT.Copy).then_inc(x4T_s.sem, 1)
                if active(n, 1):
                    if x3T_p.due(n - 1):
                        act.wait_ge(x3T_p.sem, x3T_p.at(n - 1))
                    if qkv_p.due(n - 1 - PAIR):
                        act.wait_ge(qkv_p.sem, qkv_p.at(n - 1 - PAIR))
                    act.activation(xn3T[o][:, :], p_t[:, 0:S], ACT.Copy).then_inc(x3T_s.sem, 1)
                if active(n, 3):
                    b = n - 3
                    act.wait_ge(lg_s.sem, lg_s.at(b))
                    if top_s.due(b - 1):
                        act.wait_ge(top_s.sem, top_s.at(b - 1))
                    act.activation(probs4[:, :, :], lg[:, :, :], ACT.Exp).then_inc(ex4_s.sem, 1)
                if active(n, 2):
                    if onT3_p.due(n - 2):
                        act.wait_ge(onT3_p.sem, onT3_p.at(n - 2))
                    if u_p.due(n - 3):
                        act.wait_ge(u_p.sem, u_p.at(n - 3))
                    act.activation(on3T[:, :], p_t[:, 0:S], ACT.Copy).then_inc(onT3_s.sem, 1)
                if active(n, 1):
                    b = n - 1
                    act.wait_ge(qkv_p.sem, qkv_p.at(b))
                    act.wait_ge(t_s.sem, t_s.at(b))
                    if kv_p.due(b - PAIR):
                        act.wait_ge(kv_p.sem, kv_p.at(b - PAIR))
                    if at(n, 1):
                        act.wait_ge(s2.sem, 4)
                    act.activation(KVones[o][:, :, 0:D], p_qkv[:, :].rearrange("p (i c) -> p i c", i=TT)[:, :, 2 * D:3 * D], ACT.Copy)\
                        .then_inc(v3_s.sem, 1)
                    act.wait_ge(rot_s.sem, rot_s.at(b))
                    if feat_s.due(b - 1):
                        act.wait_ge(feat_s.sem, feat_s.at(b - 1))
                    act.activation(ex[:, :, :], rot[o][:, :, :], ACT.Exp).then_inc(el_s.sem, 1)
                    act.activation(rl[:, :, :], rot[o][:, :, :], ACT.Relu).then_inc(el_s.sem, 1)

            pipeline(act, iteration)

        @block.tensor
        def _(pe):
            if t["cell"].due(B - 1):
                pe.wait_ge(t["cell"].sem, t["cell"].at(B - 1))
            pe.wait_ge(s2.sem, 4)
            pe.wait_ge(w["loaded"].sem, w["loaded"].at(0))
            pe.matmul(p_u[:, 0:S], uoh[:, :], state[:, :], start=True, stop=True).then_inc(uc_ready.sem, 1)
            pe.wait_ge(uc_ready.sem, 2)

            def turn(dst, src):
                for i in range(TT):
                    mm = pe.transpose(dst[:, i * P:(i + 1) * P], src[:, i, 0:P], ident[:, :])
                return mm

            def iteration(n, r):
                o = 1 - r
                if active(n, 4):
                    b = n - 4
                    pe.wait_ge(sel_s.sem, sel_s.at(b))
                    pe.wait_ge(lg_s.sem, lg_s.at(b, 1))
                    tri, ones = w["before"], w["ones16"]
                    k0, k1 = sel[r][:, 0, :], sel[r][:, 1, :]
                    c = 64
                    pe.matmul(p_r[:, c:c + E], tri[:, :], k0, start=True, stop=True)
                    pe.matmul(p_r[:, c + E:c + 2 * E], tri[:, :], k1, start=True, stop=False)
                    pe.matmul(p_r[:, c + E:c + 2 * E], ones[:, :], k0, start=False, stop=True)
                    pe.matmul(p_r[:, c + 2 * E:c + 3 * E], ones[:, :], k0, start=True, stop=False)
                    pe.matmul(p_r[:, c + 2 * E:c + 3 * E], ones[:, :], k1, start=False, stop=True).then_inc(rank_p.sem, 1)
                if active(n, 2):
                    b = n - 2
                    pe.wait_ge(feat_s.sem, feat_s.at(b))
                    pe.wait_ge(v3_s.sem, v3_s.at(b))
                    if kv_s.due(b - 1):
                        pe.wait_ge(kv_s.sem, kv_s.at(b - 1))
                    for i in range(TT):
                        mm = pe.matmul(p_kv[:, 0:D + 2], feat[r][:, i, D:2 * D], KVones[r][:, i, :], start=(i == 0), stop=(i == 1))
                    mm.then_inc(kv_p.sem, 1)
                    if active(n, 3):
                        if onT3_s.due(b - 1):
                            pe.wait_ge(onT3_s.sem, onT3_s.at(b - 1))
                    elif active(n, 1):
                        if x3T_s.due(n - 2):
                            pe.wait_ge(x3T_s.sem, x3T_s.at(n - 2))
                    turn(p_t, feat[r]).then_inc(qfT_p.sem, 1)
                if active(n, 0):
                    if x2_s.due(n - 1):
                        pe.wait_ge(x2_s.sem, x2_s.at(n - 1))
                    pe.matmul(p_h[:, 0:S], w["wo"][:, :], XN2T[:, n, :], start=True, stop=True).then_inc(z_p.sem, 1)
                if active(n, 3):
                    b = n - 3
                    pe.wait_ge(nm4.sem, nm4.at(b))
                    if active(n, 2):
                        if qfT_s.due(n - 2):
                            pe.wait_ge(qfT_s.sem, qfT_s.at(n - 2))
                    else:
                        if x4T_s.due(b - 1):
                            pe.wait_ge(x4T_s.sem, x4T_s.at(b - 1))
                        pe.wait_ge(onT3_s.sem, onT3_s.at(b))
                    turn(p_t, pay[o][0]).then_inc(x4T_p.sem, 1)
                if active(n, 2):
                    b = n - 2
                    pe.wait_ge(qfT_s.sem, qfT_s.at(b))
                    pe.wait_ge(kv_s.sem, kv_s.at(b))
                    if o_s.due(b - 1):
                        pe.wait_ge(o_s.sem, o_s.at(b - 1))
                    for i in range(TT):
                        mm = pe.matmul(p_o[:, i * S:i * S + D + H], qfT[:, i * P:(i + 1) * P], KVm[:, :], start=True, stop=True)
                    mm.then_inc(o_p.sem, 1)
                if active(n, 1):
                    b = n - 1
                    pe.wait_ge(nm3.sem, nm3.at(b))
                    if active(n, 3):
                        if x4T_s.due(n - 3):
                            pe.wait_ge(x4T_s.sem, x4T_s.at(n - 3))
                    elif active(n, 2):
                        if qfT_s.due(n - 2):
                            pe.wait_ge(qfT_s.sem, qfT_s.at(n - 2))
                    turn(p_t, xn3[o]).then_inc(x3T_p.sem, 1)
                if active(n, 0):
                    pe.wait_ge(h_s.sem, h_s.at(n))
                    pe.wait_ge(z_s.sem, z_s.at(n))
                    turn(p_h, hT[r][:, :].rearrange("p (i d) -> p i d", i=TT)).then_inc(hT_p.sem, 1)
                if active(n, 3):
                    b = n - 3
                    pe.wait_ge(x4T_s.sem, x4T_s.at(b))
                    if pos_s.due(b - 1):
                        pe.wait_ge(pos_s.sem, pos_s.at(b - 1))
                    for i in range(TT):
                        mm = pe.matmul(p_r[:, i * E:(i + 1) * E], xn4T[:, i * P:(i + 1) * P], w["Wr"][:, :], start=True, stop=True)
                    mm.then_inc(lg_p.sem, 1)
                if active(n, 2):
                    b = n - 2
                    pe.wait_ge(o_s.sem, o_s.at(b))
                    if active(n, 1):
                        if x3T_s.due(n - 1):
                            pe.wait_ge(x3T_s.sem, x3T_s.at(n - 1))
                    elif active(n, 3):
                        if x4T_s.due(n - 3):
                            pe.wait_ge(x4T_s.sem, x4T_s.at(n - 3))
                    turn(p_t, on3).then_inc(onT3_p.sem, 1)
                if active(n, 1):
                    b = n - 1
                    pe.wait_ge(x3T_s.sem, x3T_s.at(b))
                    if t_s.due(b - 1):
                        pe.wait_ge(t_s.sem, t_s.at(b - 1))
                    if v3_s.due(b - 1):
                        pe.wait_ge(v3_s.sem, v3_s.at(b - 1))
                    for i in range(TT):
                        mm = pe.matmul(p_qkv[:, i * 512:i * 512 + Z2], xn3T[o][:, i * P:(i + 1) * P], w["Wqkv2"][:, :], start=True, stop=True)
                    mm.then_inc(qkv_p.sem, 1)
                if active(n, 2):
                    b = n - 2
                    pe.wait_ge(onT3_s.sem, onT3_s.at(b))
                    if x3_s.due(b - 1):
                        pe.wait_ge(x3_s.sem, x3_s.at(b - 1))
                    for i in range(TT):
                        mm = pe.matmul(p_u[:, i * P:(i + 1) * P], on3T[:, i * P:(i + 1) * P], w["Wout2"][:, :], start=True, stop=True)
                    mm.then_inc(u_p.sem, 1)

            pipeline(pe, iteration)


def experts(nc, ctx, t):

    def sig(name, per=1):
        return Signal(nc, ctx, name, per)

    with ExitStack() as scope:
        def psum(name, cols=512):
            return scope.enter_context(nc.psum_tensor(name, [P, cols], F32))

        def tmp(name, shape, dt=F32):
            return scope.enter_context(nc.sbuf_tensor(name, shape, dt))

        w, X, ident, disp, back = t["w2"], t["X"], t["ident"], t["disp"], t["back"]
        count = t["count"]
        R3 = 4

        fill = tmp("fill", [P, ROW])
        counti, endi = tmp("counti", [P, E], I32), tmp("endi", [P, E], I32)
        full, tiles = tmp("full", [P, E]), [tmp(f"tiles{i}", [P, E]) for i in range(2)]
        passed, prev, eno, prevt, off = tmp("passed", [P, TILES, E]), tmp("prev", [P, TILES, E]), tmp("eno", [P, TILES]), tmp("prevt", [P, TILES]), tmp("off", [P, TILES])
        offi, enoi = tmp("offi", [P, TILES], I32), tmp("enoi", [P, TILES], I32)
        rows = [tmp(f"rows{r}", [P, ROW]) for r in range(R3)]
        xT = [tmp(f"xT{r}", [P, P]) for r in range(R3)]
        w1 = [tmp(f"w1_{r}", [P, HID + 2]) for r in range(R3)]
        hid = [tmp(f"hid{r}", [P, 2, P]) for r in range(R3)]
        y = [tmp(f"y{r}", [P, D]) for r in range(R3)]
        to = [tmp(f"to{r}", [P, 1], U32) for r in range(R3)]
        NB = 4
        yb = [tmp(f"yb{i}", [P, NB, TOP * D]) for i in range(2 * B // NB)]

        p_x = [psum(f"p_x{i}") for i in range(2)]
        p_hid = [psum(f"p_hid{i}") for i in range(2)]
        p_y = [psum(f"p_y{i}") for i in range(2)]

        fill_s, plan, table, pad = sig("fill_s"), sig("plan"), sig("table"), sig("pad")
        rows_in = [sig(f"rows_in{i}", 16) for i in range(R3)]
        x_p, x_s, w_s, hid_p, hid_s, y_p, y_s, to_s = sig("x_p"), sig("x_s"), sig("w_s"), sig("hid_p"), sig("hid_s", 2), sig("y_p"), sig("y_s"), sig("to_s")
        yout = [sig(f"yout{i}", 16) for i in range(R3)]
        yb_in = [sig(f"yb_in{i}", 16) for i in range(2 * B // NB)]
        sum_s, out_done = sig("sum_s", 2), sig("out_done")

        def pipeline(eng, step):
            for k in range(2):
                for r in range(R3):
                    step(k * R3 + r, k, r)
            with eng.Fori(2, TILES // R3, 1) as k:
                for r in range(R3):
                    step(k * R3 + r, k, r)
            for r in range(2):
                step(None, TILES // R3, r)

        def behind(i, k, r, lag):
            last = i is None
            i = TILES + r if last else i
            if isinstance(i, int) and (i < lag or i - lag >= TILES):
                return []
            return [(i - lag, (r - lag) % R3, k if r >= lag else k - 1)]

        block = scope.enter_context(nc.Block())

        @block.gpsimd
        def _(pool):
            pool.memset(fill[:, 0:D + 1], 0.0).then_inc(fill_s.sem, 1)
            pool.memset(fill[:, D + 1:ROW], NOWHERE).then_inc(fill_s.sem, 1)

            def step(i, k, r):
                if i is None:
                    return
                pool.wait_ge(y_s.sem, y_s.at(i))
                pool.wait_ge(to_s.sem, to_s.at(i))
                steady(pool, t)
                pool.indirect_dma_start(out=back, out_offset=bass.IndirectOffsetOnAxis(ap=to[r][:, 0:1], axis=0), in_=y[r][:, :],
                                        in_offset=None, bounds_check=TOP * TOKENS - 1, oob_is_err=False).then_inc(yout[r].sem, 16)

            pipeline(pool, step)

        @block.sync
        def _(sp):
            sp.wait_ge(fill_s.sem, 2)
            if t["sent"].due(B - 1):
                sp.wait_ge(t["sent"].sem, t["sent"].at(B - 1))
            sp.wait_ge(plan.sem, plan.at(0, 1))
            for e in range(E):
                end = sp.value_load(endi[0:1, e:e + 1], min_val=e * REGION, max_val=e * REGION + TOKENS)
                sp.dma_start(disp[bass.ds(end, P), :], fill[:, :]).then_inc(pad.sem, 16)
            sp.dma_start(disp[E * REGION:E * REGION + P, :], fill[:, :]).then_inc(pad.sem, 16)
            sp.wait_ge(pad.sem, 16 * (E + 1))
            sp.wait_ge(table.sem, 2)

            def step(i, k, r):
                if i is None:
                    return
                at = sp.value_load(offi[0:1, bass.ds(i, 1)], min_val=0, max_val=E * REGION)
                if x_p.due(i - R3):
                    sp.wait_ge(x_p.sem, x_p.at(i - R3))
                if to_s.due(i - R3):
                    sp.wait_ge(to_s.sem, to_s.at(i - R3))
                if y_s.due(i - R3):
                    sp.wait_ge(y_s.sem, y_s.at(i - R3))
                steady(sp, t)
                sp.dma_start(rows[r][:, :], disp[bass.ds(at, P), :]).then_inc(rows_in[r].sem, 16)

            pipeline(sp, step)
            for r in range(R3):
                if yout[r].due(TILES // R3 - 1):
                    sp.wait_ge(yout[r].sem, yout[r].at(TILES // R3 - 1))
            bv = back.rearrange("(n p k) d -> p n (k d)", p=P, k=TOP)
            ov = t["out"].rearrange("(n p) d -> p n d", p=P)
            for c in range(2 * B // NB):
                sp.dma_start(yb[c][:, :, :], bv[:, c * NB:(c + 1) * NB, :]).then_inc(yb_in[c].sem, 16)
            for c in range(2 * B // NB):
                sp.wait_ge(sum_s.sem, sum_s.at(c))
                sp.dma_start(ov[:, c * NB:(c + 1) * NB, :], X[:, c * NB:(c + 1) * NB, :]).then_inc(out_done.sem, 16)
            sp.wait_ge(out_done.sem, 16 * (2 * B // NB))

        @block.vector
        def _(dve):
            n = [0]

            def then(ins, mark=plan):
                n[0] += 1
                ins.then_inc(mark.sem, 1)
                dve.wait_ge(mark.sem, n[0])

            if t["pos_s"].due(B - 1):
                dve.wait_ge(t["pos_s"].sem, t["pos_s"].at(B - 1))
            then(dve.tensor_copy(endi[:, :], count[:, :]))
            then(dve.tensor_tensor(full[:, :], count[:, :], w["region"][:, :], ALU.subtract))
            then(dve.tensor_scalar(counti[:, :], full[:, :], float(P - 1), None, ALU.add))
            then(dve.tensor_scalar(counti[:, :], counti[:, :], 7, None, ALU.logical_shift_right))
            then(dve.tensor_copy(tiles[0][:, :], counti[:, :]))
            for j, s in enumerate((1, 2, 4, 8)):
                a, b = tiles[j % 2], tiles[(j + 1) % 2]
                then(dve.tensor_copy(b[:, 0:s], a[:, 0:s]))
                then(dve.tensor_tensor(b[:, s:E], a[:, s:E], a[:, 0:E - s], ALU.add))
            cum = tiles[0]
            shape = [P, TILES, E]
            cw = cum[:, :].rearrange("p (o e) -> p o e", o=1).broadcast_to(shape)
            then(dve.tensor_tensor(passed[:, :, :], w["iota_t"][:, :].rearrange("p (t o) -> p t o", o=1).broadcast_to(shape), cw, ALU.is_ge))
            then(dve.tensor_tensor(prev[:, :, :], passed[:, :, :], cw, ALU.mult))
            then(dve.tensor_reduce(eno[:, :], passed[:, :, :], AX.X, ALU.add))
            then(dve.tensor_reduce(prevt[:, :], prev[:, :, :], AX.X, ALU.max))
            then(dve.tensor_tensor(off[:, :], w["iota_t"][:, :], prevt[:, :], ALU.subtract))
            then(dve.tensor_scalar(off[:, :], off[:, :], float(P), None, ALU.mult))
            then(dve.scalar_tensor_tensor(out=off[:, :], in0=eno[:, :], scalar=float(REGION), in1=off[:, :], op0=ALU.mult, op1=ALU.add))
            then(dve.tensor_scalar(off[:, :], off[:, :], float(E * REGION), None, ALU.min))
            then(dve.tensor_scalar(eno[:, :], eno[:, :], float(E - 1), None, ALU.min))
            dve.tensor_copy(offi[:, :], off[:, :]).then_inc(table.sem, 1)
            dve.tensor_copy(enoi[:, :], eno[:, :]).then_inc(table.sem, 1)
            dve.wait_ge(table.sem, 2)

            def step(i, k, r):
                if i is not None:
                    e = dve.value_load(enoi[0:1, bass.ds(i, 1)], min_val=0, max_val=E - 1)
                    if hid_p.due(i - R3):
                        dve.wait_ge(hid_p.sem, hid_p.at(i - R3))
                    if hid_s.due(i - R3):
                        dve.wait_ge(hid_s.sem, hid_s.at(i - R3))
                    dve.tensor_copy(w1[r][:, :], w["W1"][:, bass.ds(e, 1), :].rearrange("p o c -> p (o c)")).then_inc(w_s.sem, 1)
                    dve.wait_ge(rows_in[r].sem, rows_in[r].at(k))
                    if yout[r].due(k - 1):
                        dve.wait_ge(yout[r].sem, yout[r].at(k - 1))
                    dve.tensor_copy(to[r][:, :], rows[r][:, D + 1:ROW]).then_inc(to_s.sem, 1)
                for j, q, kq in behind(i, k, r, 2):
                    dve.wait_ge(y_p.sem, y_p.at(j))
                    if yout[q].due(kq - 1):
                        dve.wait_ge(yout[q].sem, yout[q].at(kq - 1))
                    dve.tensor_scalar(y[q][:, :], p_y[q % 2][:, 0:D], rows[q][:, D:D + 1], None, ALU.mult).then_inc(y_s.sem, 1)

            pipeline(dve, step)
            for c in range(2 * B // NB):
                sl = X[:, c * NB:(c + 1) * NB, :]
                dve.wait_ge(yb_in[c].sem, yb_in[c].at(0))
                dve.tensor_tensor(sl, sl, yb[c][:, :, 0:D], ALU.add).then_inc(sum_s.sem, 1)
                dve.wait_ge(sum_s.sem, sum_s.at(c, 1))
                dve.tensor_tensor(sl, sl, yb[c][:, :, D:2 * D], ALU.add).then_inc(sum_s.sem, 1)

        @block.scalar
        def _(act):
            def step(i, k, r):
                if i is not None:
                    act.wait_ge(x_p.sem, x_p.at(i))
                    if hid_p.due(i - R3):
                        act.wait_ge(hid_p.sem, hid_p.at(i - R3))
                    act.activation(xT[r][:, :], p_x[r % 2][:, 0:P], ACT.Copy).then_inc(x_s.sem, 1)
                for j, q, _ in behind(i, k, r, 1):
                    act.wait_ge(hid_p.sem, hid_p.at(j))
                    act.wait_ge(w_s.sem, w_s.at(j))
                    if y_p.due(j - R3):
                        act.wait_ge(y_p.sem, y_p.at(j - R3))
                    for c in range(2):
                        act.activation(hid[q][:, c, :], p_hid[q % 2][:, c * P:(c + 1) * P], ACT.Gelu, bias=w1[q][:, HID + c:HID + c + 1])\
                            .then_inc(hid_s.sem, 1)

            pipeline(act, step)

        @block.tensor
        def _(pe):
            pe.wait_ge(table.sem, 2)

            def step(i, k, r):
                if i is not None:
                    pe.wait_ge(rows_in[r].sem, rows_in[r].at(k))
                    if x_s.due(i - 2):
                        pe.wait_ge(x_s.sem, x_s.at(i - 2))
                    pe.transpose(p_x[r % 2][:, 0:P], rows[r][:, 0:D], ident[:, :]).then_inc(x_p.sem, 1)
                for j, q, _ in behind(i, k, r, 1):
                    pe.wait_ge(x_s.sem, x_s.at(j))
                    pe.wait_ge(w_s.sem, w_s.at(j))
                    if hid_s.due(j - 2):
                        pe.wait_ge(hid_s.sem, hid_s.at(j - 2))
                    for c in range(2):
                        mm = pe.matmul(p_hid[q % 2][:, c * P:(c + 1) * P], w1[q][:, c * P:(c + 1) * P], xT[q][:, :], start=True, stop=True)
                    mm.then_inc(hid_p.sem, 1)
                for j, q, _ in behind(i, k, r, 2):
                    e = pe.value_load(enoi[0:1, bass.ds(j, 1)], min_val=0, max_val=E - 1)
                    if y_s.due(j - 2):
                        pe.wait_ge(y_s.sem, y_s.at(j - 2))
                    pe.matmul(p_y[q % 2][:, 0:D], w["one_row"][:, :], w["b2"][0:1, bass.ds(e, 1), :].rearrange("p o c -> p (o c)"),
                              start=True, stop=False)
                    pe.wait_ge(hid_s.sem, hid_s.at(j))
                    for c in range(2):
                        mm = pe.matmul(p_y[q % 2][:, 0:D], hid[q][:, c, :], w["W2"][:, bass.ds(e, 1), c, :].rearrange("p o c -> p (o c)"),
                                       start=False, stop=(c == 1))
                    mm.then_inc(y_p.sem, 1)

            pipeline(pe, step)


def program(nc, x, Wqkv, bqk, bv, Wout, bout, gates_w, gates_u, gates_b, in_c, wo, uo, bo, Wqkv2, Wout2, Wr, br, W1, W2, b2, cosf, sinf, out):
    with ExitStack() as ctx:
        def sb(name, shape, dt=F32):
            return ctx.enter_context(nc.sbuf_tensor(name, shape, dt))

        t = dict(x_dram=x, Wqkv=Wqkv, bqk=bqk, bv=bv, Wout=Wout, bout=bout, gates_w=gates_w, gates_u=gates_u, gates_b=gates_b,
                 in_c=in_c, out=out)
        t["X"], t["XN2T"], t["state"] = sb("X", [P, 2 * B, D]), sb("XN2T", [P, B, S]), sb("state", [P, S])
        t["ident"], t["ident16"] = sb("ident", [P, P]), sb("ident16", [P, P], BF16)
        t["disp"] = nc.dram_tensor("disp", [E * REGION + P, ROW], F32).ap()
        t["back"] = nc.dram_tensor("back", [TOP * TOKENS, D], F32).ap()
        t["count"] = sb("count", [P, E])
        w = t["w2"] = dict(wo=sb("wo", [P, D]), uo=sb("uo", [P, D]), bo=sb("bo2", [P, 1]), Wqkv2=sb("Wqkv2", [P, 3 * D]),
                           Wout2=sb("Wout2", [P, D]), Wr=sb("Wr", [P, E]), br=sb("br", [P, E]), cosf=sb("cosf", [P, TT, 2 * D]),
                           sinf=sb("sinf", [P, TT, 2 * D]), W1=sb("W1", [P, E, HID + 2]), W2=sb("W2", [P, E, 2, D]),
                           b2=sb("b2", [1, E, D]), block_mask=sb("block_mask", [P, D]), head_mask=sb("head_mask", [P, H]),
                           before=sb("before", [P, P], BF16), ones16=sb("ones16", [P, P], BF16), iota_e=sb("iota_e", [P, E]),
                           iota_t=sb("iota_t", [P, TILES]), region=sb("region", [P, E]), one_row=sb("one_row", [1, P]),
                           loaded=Signal(nc, ctx, "loaded", 16 * 12))
        for name in ("consts", "v_set", "count_set", "const_steps"):
            t[name] = Signal(nc, ctx, name)

        with nc.Block() as block:
            @block.gpsimd
            def _(pool):
                n = 0
                fills = [(t["ident"], 0.0), (t["ident16"], 0.0), (w["block_mask"], 1.0), (w["head_mask"], 1.0), (w["before"], 1.0),
                         (w["ones16"], 1.0), (w["one_row"], 1.0)]
                for m, value in fills:
                    pool.memset(m[:, :], value).then_inc(t["const_steps"].sem, 1)
                n += len(fills)
                pool.iota(w["iota_e"][:, :], pattern=[[1, E]], base=0, channel_multiplier=0, allow_small_or_imprecise_dtypes=True)\
                    .then_inc(t["const_steps"].sem, 1)
                pool.iota(w["iota_t"][:, :], pattern=[[1, TILES]], base=0, channel_multiplier=0, allow_small_or_imprecise_dtypes=True)\
                    .then_inc(t["const_steps"].sem, 1)
                n += 2
                for m in (w["region"], t["count"]):
                    pool.iota(m[:, :], pattern=[[REGION, E]], base=0, channel_multiplier=0, allow_small_or_imprecise_dtypes=True)\
                        .then_inc(t["count_set"].sem, 1)
                pool.wait_ge(t["const_steps"].sem, n)
                for m in (t["ident"], t["ident16"]):
                    pool.affine_select(out=m[:, :], in_=m[:, :], compare_op=ALU.not_equal, fill=1.0, base=0, pattern=[[-1, P]],
                                       channel_multiplier=1).then_inc(t["consts"].sem, 1)
                pool.affine_select(out=w["before"][:, :], in_=w["before"][:, :], compare_op=ALU.is_gt, fill=0.0, base=0,
                                   pattern=[[1, P]], channel_multiplier=-1).then_inc(t["consts"].sem, 1)
                for step, (op, base, sign) in enumerate(((ALU.is_ge, 0, 1), (ALU.is_ge, HD - 1, -1))):
                    m = w["block_mask"][:, :].rearrange("p (h d) -> p h d", d=HD)
                    pool.affine_select(out=m, in_=m, compare_op=op, fill=0.0, base=base, pattern=[[-HD * sign, H], [0, HD]],
                                       channel_multiplier=sign).then_inc(t["consts"].sem, 1)
                    pool.affine_select(out=w["head_mask"][:, :], in_=w["head_mask"][:, :], compare_op=op, fill=0.0, base=base,
                                       pattern=[[-HD * sign, H]], channel_multiplier=sign).then_inc(t["consts"].sem, 1)
                    pool.wait_ge(t["consts"].sem, 5 + 2 * step)
        t["n_consts"] = 7
        t["w2_loads"] = [(w["wo"], wo), (w["uo"], uo), (w["bo"], bo), (w["Wqkv2"], Wqkv2), (w["Wout2"], Wout2), (w["Wr"], Wr),
                         (w["br"], br.partition_broadcast(P)), (w["cosf"], cosf), (w["sinf"], sinf), (w["W1"], W1), (w["W2"], W2), (w["b2"], b2)]
        attention_and_recurrence(nc, ctx, t)
        linear_attention_and_routing(nc, ctx, t)
        experts(nc, ctx, t)


def kernel(**inputs):
    import numpy as np
    import concourse.bacc as bacc
    from concourse.bass_utils import run_bass_kernel_spmd

    g = {k: np.asarray(v) for k, v in inputs.items()}
    ffn = lambda name: g["L0_ffn_" + name]
    bqkv = g["L0_attn_bqkv"]
    angle = np.arange(S, dtype=np.float32)[:, None] * (1.0 / 10000.0 ** (np.arange(0, HD, 2, dtype=np.float32) / HD))[None, :]
    cos, sin = np.cos(angle), np.sin(angle)
    factors = np.array([SCALE, 1.0], np.float32)[None, :, None, None, None]
    full = lambda lo, hi: np.broadcast_to(factors * np.stack([lo, hi], 1)[:, None, None], (S, 2, H, 2, HD // 2))
    table = lambda a: np.ascontiguousarray(a.reshape(TT, P, 2 * D).transpose(1, 0, 2)).astype(np.float32)
    b1 = g["L1_ffn_b1"].reshape(E, 2, P).transpose(2, 0, 1)
    laid = {
        "x": g["L0_attn_x"].reshape(TOKENS, D),
        "Wqkv": g["L0_attn_Wqkv"], "bqk": bqkv[:2 * D].reshape(2, P).T, "bv": bqkv[2 * D:],
        "Wout": g["L0_attn_Wout"], "bout": g["L0_attn_bout"],
        "gates_w": np.stack([ffn("wf").T, ffn("wi").T, ffn("wc").T], 1),
        "gates_u": np.stack([ffn("uf").T, ffn("ui").T, ffn("uc").T], 1),
        "gates_b": np.stack([ffn("bf"), ffn("bi"), ffn("bc")], 1),
        "in_c": ffn("in_c").reshape(P, 1),
        "wo": ffn("wo").T, "uo": ffn("uo").T, "bo": ffn("bo").reshape(P, 1),
        "Wqkv2": g["L1_attn_w_qkv"].T, "Wout2": g["L1_attn_w_out"].T,
        "Wr": g["L1_ffn_Wr"], "br": g["L1_ffn_br"],
        "W1": np.concatenate([g["L1_ffn_W1"].transpose(1, 0, 2), b1], 2),
        "W2": g["L1_ffn_W2"].reshape(E, 2, P, D).transpose(2, 0, 1, 3),
        "b2": g["L1_ffn_b2"].reshape(1, E, D),
        "cosf": table(full(cos, cos)), "sinf": table(full(-sin, sin)),
    }
    nc = bacc.Bacc("TRN2", target_bir_lowering=False, num_devices=1)
    arrays, args = {}, []
    for name, a in laid.items():
        a = np.ascontiguousarray(a)
        arrays[f"in_{name}_dram"] = a
        args.append(nc.dram_tensor(f"in_{name}_dram", a.shape, mybir.dt.from_np(a.dtype), kind="ExternalInput").ap())
    args.append(nc.dram_tensor("out_dram", (TOKENS, D), F32, kind="ExternalOutput").ap())
    program(nc, *args)
    result = run_bass_kernel_spmd(nc, [arrays], core_ids=[0])
    return result.results[0]["out_dram"].reshape(B, S, D)
```

```python
from contextlib import ExitStack

import concourse.bass as bass
from concourse import mybir

F32 = mybir.dt.float32
BF16 = mybir.dt.bfloat16
I32 = mybir.dt.int32
U32 = mybir.dt.uint32
ALU = mybir.AluOpType
ACT = mybir.ActivationFunctionType
AX = mybir.AxisListType

P = 128
B = 16
S = 256
D = 128
H = 16
HD = D // H
TT = S // P
EPS = 1e-5
NG = 4
RING = 3
PARTS = 3
PAIRS = 6 * HD
SCALE = HD ** -0.5
MAX_AT = [range(3 * s, min(3 * s + 3, 16)) for s in range(8)]
MAGIC = 0x5F3759DF
NEWTON = 3


class Signal:

    def __init__(self, nc, ctx, name, per=1):
        self.sem = ctx.enter_context(nc.semaphore(name))
        self.per = per

    def at(self, b, part=None):
        value = b * self.per + (self.per if part is None else part)
        assert not isinstance(value, int) or value > 0
        return value

    def due(self, b, part=None):
        value = b * self.per + (self.per if part is None else part)
        return not isinstance(value, int) or value > 0


def steady(eng, t):
    eng.nop(nofuse=True)


def newton_steps(t, pool, root, mark, b):
    y, u, v = root[:, 0, :], root[:, 1, :], root[:, 3, :]
    j = 0
    for _ in range(NEWTON):
        if j:
            pool.wait_ge(mark.sem, mark.at(b, j))
        pool.tensor_tensor(u, y, y, ALU.mult).then_inc(mark.sem, 1)
        pool.wait_ge(mark.sem, mark.at(b, j + 1))
        pool.tensor_tensor(u, u, v, ALU.mult).then_inc(mark.sem, 1)
        pool.wait_ge(mark.sem, mark.at(b, j + 2))
        steady(pool, t)
        pool.tensor_scalar(u, u, -0.5, 1.5, ALU.mult, ALU.add).then_inc(mark.sem, 1)
        pool.wait_ge(mark.sem, mark.at(b, j + 3))
        pool.tensor_tensor(y, y, u, ALU.mult).then_inc(mark.sem, 1)
        j += 4


def attention_and_recurrence(nc, ctx, t, out_dbg=None):

    def sb(name, shape, dt=F32):
        return ctx.enter_context(nc.sbuf_tensor(name, shape, dt))

    def sig(name, per=1):
        return Signal(nc, ctx, name, per)

    with ExitStack() as scope:
        def psum(name, cols=512):
            return scope.enter_context(nc.psum_tensor(name, [P, cols], F32))

        def tmp(name, shape, dt=F32):
            return scope.enter_context(nc.sbuf_tensor(name, shape, dt))

        X, XN2T, state = t["X"], t["XN2T"], t["state"]
        ident, ident16 = t["ident"], t["ident16"]

        Wqkv, Wout = tmp("Wqkv", [P, 3 * D]), tmp("Wout", [P, D])
        bqk, bqk_s = tmp("bqk", [P, 2]), tmp("bqk_s", [P, 2])
        bv, bo = tmp("bv", [P, D]), tmp("bo", [P, D])
        gates_w, gates_u, gates_uh = tmp("gates_w", [P, 3, D]), tmp("gates_u", [P, 3, D]), tmp("gates_uh", [P, 3, D])
        gates_b, gates_bh = tmp("gates_b", [P, 3]), tmp("gates_bh", [P, 3])
        c_start, zeros = tmp("c_start", [P, 1]), tmp("zeros", [P, S])

        stats1, mv1 = [tmp(f"stats1_{r}", [P, TT, 6]) for r in range(RING)], [tmp(f"mv1_{r}", [P, TT, 2]) for r in range(RING)]
        stats2, mv2 = [tmp(f"stats2_{r}", [P, TT, 6]) for r in range(RING)], [tmp(f"mv2_{r}", [P, TT, 2]) for r in range(RING)]
        root1, root2 = [tmp(f"root1_{r}", [P, 5, TT]) for r in range(RING)], [tmp(f"root2_{r}", [P, 5, TT]) for r in range(RING)]
        xn1 = [tmp(f"xn1_{r}", [P, TT, D]) for r in range(RING)]
        xn1T = [tmp(f"xn1T_{r}", [P, S]) for r in range(RING)]
        qk = [tmp(f"qk_{r}", [P, 2, S]) for r in range(RING)]
        part = tmp("part", [P, PARTS, 2, S], BF16)
        rest = tmp("rest", [P, 2, S])
        QS = [tmp(f"QS_{r}", [PAIRS + PARTS, H, S], BF16) for r in range(RING)]
        KS = [tmp(f"KS_{r}", [PAIRS + PARTS, H, S], BF16) for r in range(RING)]
        V = [tmp(f"V_{r}", [P, TT, H, 32]) for r in range(RING)]
        negmax = tmp("negmax", [P, TT, H])
        maxrest = tmp("maxrest", [P, TT, H])
        maxpart = tmp("maxpart", [P, TT, PARTS, H], BF16)
        maxT = tmp("maxT", [PARTS * H, S], BF16)
        probs = [tmp(f"probs_{r}", [P, 4, S]) for r in range(2)]
        OT = [tmp(f"OT_{r}", [P, NG, S]) for r in range(RING)]
        rz = tmp("rz", [P, TT, H])
        on = tmp("on", [P, TT, D])
        onT = tmp("onT", [P, S])
        xb = [tmp(f"xb_{r}", [P, TT, D]) for r in range(RING)]
        xn2 = [tmp(f"xn2_{r}", [P, TT, D]) for r in range(RING)]
        xn2T = tmp("xn2T", [P, S])
        gate = tmp("gate", [P, 3, S])
        ca, cb = tmp("ca", [P, S]), tmp("cb", [P, S])

        p_exp = [psum(f"p_exp{i}", 1024) for i in range(2)]
        p_max = [psum(f"p_max{i}") for i in range(2)]
        p_out = psum("p_out")
        p_misc = psum("p_misc")

        scratch = [nc.dram_tensor(f"scratch_{r}", [2, PARTS, HD, H, S], BF16).ap() for r in range(RING)]

        x_in = [sig(f"x_in{i}") for i in range(3)]
        w_in = sig("w_in")
        consts = t["consts"]
        setup_done = sig("setup_done", 8)
        stats_a = sig("stats_a", 4)
        seed_a = sig("seed_a", 3)
        newton_a = sig("newton_a", 4 * NEWTON)
        norm_a = sig("norm_a", 2)
        xnT_p = sig("xnT_p")
        xnT_s = sig("xnT_s")
        qk_p = sig("qk_p")
        qk_s = sig("qk_s", 4)
        v_p = sig("v_p")
        v_s = sig("v_s")
        split = sig("split", 3)
        parts_out = sig("parts_out", 16 * 2 * PARTS)
        stack_in = sig("stack_in", 16 * 6)
        max_p = sig("max_p", 16)
        max_s = sig("max_s", 16)
        msplit = sig("msplit", 5)
        maxT_p = sig("maxT_p")
        maxT_s = sig("maxT_s")
        maxrow_in = sig("maxrow_in", 16 * PARTS)
        score_p = sig("score_p", 8)
        prob_s = sig("prob_s", 8)
        pv_p = sig("pv_p", 8)
        OT_s = sig("OT_s", 4)
        xb_s = sig("xb_s")
        OQ_p = sig("OQ_p", 2)
        rz_s = sig("rz_s", 2)
        on_s = sig("on_s", 2)
        onT_p = sig("onT_p")
        onT_s = sig("onT_s")
        proj_p = sig("proj_p")
        x1_s = sig("x1_s")
        stats_b = sig("stats_b", 4)
        seed_b = sig("seed_b", 3)
        newton_b = sig("newton_b", 4 * NEWTON)
        norm_b = sig("norm_b", 2)
        xn2T_p = sig("xn2T_p")
        xn2T_s = sig("xn2T_s")
        xn2T_k = sig("xn2T_k")
        gfi_p = sig("gfi_p")
        gfi_s = sig("gfi_s", 2)
        gc_p = sig("gc_p")
        gc_s = sig("gc_s")
        cell = sig("cell", 3)
        t["cell"], t["x1_s"], t["xn2T_k"] = cell, x1_s, xn2T_k

        LAST = B + 5
        PEEL = 6

        def pipeline(eng, iteration):
            for n in range(-1, PEEL):
                iteration(n, n % RING)
            with eng.Fori(0, (B - 1 - PEEL) // RING, 1) as k:
                for c in range(RING):
                    iteration(k * RING + (PEEL + c), (PEEL + c) % RING)
            for n in range(B - 1, LAST):
                iteration(n, n % RING)

        def active(n, lag):
            return not isinstance(n, int) or 0 <= n - lag < B

        def at(n, first):
            return isinstance(n, int) and n == first

        block = scope.enter_context(nc.Block())

        @block.sync
        def _(sp):
            xv = t["x_dram"].rearrange("(n p) d -> p n d", p=P)
            sp.dma_start(X[:, 0:2, :], xv[:, 0:2, :]).then_inc(x_in[0].sem, 16)
            sp.dma_start(Wqkv[:, :], t["Wqkv"]).then_inc(w_in.sem, 16)
            sp.dma_start(bqk[:, :], t["bqk"]).then_inc(w_in.sem, 16)
            sp.dma_start(bv[:, :], t["bv"].partition_broadcast(P)).then_inc(w_in.sem, 16)
            sp.dma_start(bo[:, :], t["bout"].partition_broadcast(P)).then_inc(w_in.sem, 16)
            sp.dma_start(X[:, 2:4, :], xv[:, 2:4, :]).then_inc(x_in[1].sem, 16)
            sp.dma_start(X[:, 4:2 * B, :], xv[:, 4:2 * B, :]).then_inc(x_in[2].sem, 16)
            sp.dma_start(Wout[:, :], t["Wout"]).then_inc(w_in.sem, 16)
            sp.dma_start(gates_w[:, :, :], t["gates_w"]).then_inc(w_in.sem, 16)
            sp.dma_start(gates_u[:, :, :], t["gates_u"]).then_inc(w_in.sem, 16)
            sp.dma_start(gates_b[:, :], t["gates_b"]).then_inc(w_in.sem, 16)
            sp.dma_start(c_start[:, :], t["in_c"]).then_inc(w_in.sem, 16)

            def iteration(n, r):
                if at(n, 2):
                    for dst, src in t["w2_loads"]:
                        sp.dma_start(dst[tuple(slice(None) for _ in dst.shape)], src).then_inc(t["w2"]["loaded"].sem, 16)
                if active(n, 0):
                    b = n
                    if stack_in.due(b - 1):
                        sp.wait_ge(stack_in.sem, stack_in.at(b - 1))
                    for i in range(PARTS):
                        if i == 0:
                            sp.wait_ge(qk_s.sem, qk_s.at(b))
                        else:
                            sp.wait_ge(split.sem, split.at(b, 1 + i))
                        for j in range(2):
                            sp.dma_start(scratch[r][j, i].rearrange("d h t -> h d t"), part[:, i, j, :])\
                                .then_inc(parts_out.sem, 16)
                    sp.wait_ge(parts_out.sem, parts_out.at(b))
                    if score_p.due(b - RING):
                        sp.wait_ge(score_p.sem, score_p.at(b - RING))
                    first = 0
                    for i in range(PARTS):
                        k = PARTS - i
                        src = scratch[r][0, i].rearrange("(o d) h t -> o d (h t)", o=1)
                        sp.dma_start(QS[r][first:first + k * HD, :, :], src.broadcast_to([k, HD, H * S])).then_inc(stack_in.sem, 16)
                        sp.dma_start(KS[r][first:first + k * HD, :, :], scratch[r][1, 0:k].rearrange("k d h t -> (k d) (h t)"))\
                            .then_inc(stack_in.sem, 16)
                        first += k * HD
                if active(n, 1):
                    b, q = n - 1, (r - 1) % RING
                    sp.wait_ge(maxT_s.sem, maxT_s.at(b))
                    sp.wait_ge(stack_in.sem, stack_in.at(b))
                    for i in range(PARTS):
                        sp.dma_start(QS[q][PAIRS + i:PAIRS + i + 1, :, :], maxT[i * H:(i + 1) * H, :])\
                            .then_inc(maxrow_in.sem, 16)
                    sp.wait_ge(maxrow_in.sem, maxrow_in.at(b))
                    steady(sp, t)

            pipeline(sp, iteration)

        @block.gpsimd
        def _(pool):
            for r in range(RING):
                pool.memset(KS[r][:, :, :], 1.0).then_inc(setup_done.sem, 1)
            pool.wait_ge(w_in.sem, w_in.at(0, 16 * 9))
            pool.tensor_scalar(bqk_s[:, :], bqk[:, :], SCALE, None, ALU.mult).then_inc(setup_done.sem, 1)
            pool.tensor_scalar(gates_uh[:, :, :], gates_u[:, :, :], 0.5, None, ALU.mult).then_inc(setup_done.sem, 1)
            pool.tensor_scalar(gates_bh[:, :], gates_b[:, :], 0.5, None, ALU.mult).then_inc(setup_done.sem, 1)
            pool.memset(zeros[:, :], 0.0).then_inc(setup_done.sem, 1)
            pool.wait_ge(setup_done.sem, 7)
            pool.tensor_scalar(state[:, :], zeros[:, :], c_start[:, 0:1], 2.0, ALU.add, ALU.mult)\
                .then_inc(setup_done.sem, 1)

            newton = lambda root, mark, b: newton_steps(t, pool, root, mark, b)

            def iteration(n, r):
                if active(n, 0):
                    pool.wait_ge(split.sem, split.at(n, 2))
                    if parts_out.due(n - 1):
                        pool.wait_ge(parts_out.sem, parts_out.at(n - 1))
                    pool.tensor_tensor(part[:, 2, :, :], rest[:, :, :], part[:, 1, :, :], ALU.subtract).then_inc(split.sem, 1)
                if active(n, 2):
                    b, q = n - 2, (r - 2) % RING
                    if x1_s.due(b - RING):
                        pool.wait_ge(x1_s.sem, x1_s.at(b - RING))
                    steady(pool, t)
                    pool.tensor_tensor(xb[q][:, :, :], X[:, bass.ds(2 * b, 2), :],
                                       bo[:, :].rearrange("p (o d) -> p o d", o=1).broadcast_to([P, TT, D]), ALU.add)\
                        .then_inc(xb_s.sem, 1)
                if active(n, 3):
                    b, q = n - 3, (r - 3) % RING
                    pool.wait_ge(seed_b.sem, seed_b.at(b))
                    newton(root2[q], newton_b, b)
                if active(n, -1):
                    pool.wait_ge(seed_a.sem, seed_a.at(n + 1))
                    newton(root1[(r + 1) % RING], newton_a, n + 1)

            pipeline(pool, iteration)

        @block.vector
        def _(dve):
            for r in range(RING):
                dve.memset(V[r][:, :, :, :], 0.0).then_inc(t["v_set"].sem, 1)
            dve.wait_ge(t["v_set"].sem, 3)
            for r in range(RING):
                dve.memset(V[r][:, :, :, HD:HD + 1], 1.0).then_inc(t["v_set"].sem, 1)
            dve.wait_ge(t["v_set"].sem, 6)

            def layer_stats(b, stats, mv, root, st, sd, prev_norm):
                steady(dve, t)
                for i in range(TT):
                    dve.bn_stats(stats[:, i, :], X[:, 2 * b + i, :]).then_inc(st.sem, 1)
                if prev_norm.due(b - RING):
                    dve.wait_ge(prev_norm.sem, prev_norm.at(b - RING))
                for i in range(TT):
                    dve.wait_ge(st.sem, st.at(b, 1 + i))
                    steady(dve, t)
                    dve.bn_aggr(mv[:, i, :], stats[:, i, :]).then_inc(st.sem, 1)
                dve.wait_ge(st.sem, st.at(b))
                dve.tensor_scalar(root[:, 3, :], mv[:, :, 1], EPS, None, ALU.add).then_inc(sd.sem, 1)
                dve.wait_ge(sd.sem, sd.at(b, 1))
                dve.tensor_scalar(root[:, 4, :].bitcast(U32), root[:, 3, :].bitcast(U32), 1, None, ALU.logical_shift_right)\
                    .then_inc(sd.sem, 1)
                dve.wait_ge(sd.sem, sd.at(b, 2))
                dve.tensor_scalar(root[:, 0, :].bitcast(I32), root[:, 4, :].bitcast(I32), -1.0, float(MAGIC), ALU.mult, ALU.add)\
                    .then_inc(sd.sem, 1)

            def layer_norm(b, mv, root, dst, nw, nm):
                dve.wait_ge(nw.sem, nw.at(b))
                for i in range(TT):
                    dve.tensor_scalar(dst[:, i, :], X[:, 2 * b + i, :], mv[:, i, 0:1], root[:, 0, i:i + 1], ALU.subtract, ALU.mult)\
                        .then_inc(nm.sem, 1)

            def row_max(b, u):
                i, hp = u // 8, u % 8
                dve.wait_ge(max_p.sem, max_p.at(b, u + 1))
                if u == 0:
                    if msplit.due(b - 1):
                        dve.wait_ge(msplit.sem, msplit.at(b - 1))
                dve.tensor_reduce(negmax[:, i, 2 * hp:2 * hp + 2], p_max[u % 2][:, :].rearrange("p (h k) -> p h k", h=2),
                                  AX.X, ALU.max, negate=True).then_inc(max_s.sem, 1)

            def split_max(b):
                dve.wait_ge(max_s.sem, max_s.at(b))
                if maxT_p.due(b - 1):
                    dve.wait_ge(maxT_p.sem, maxT_p.at(b - 1))
                hs = [maxpart[:, :, i, :] for i in range(PARTS)]
                dve.tensor_copy(hs[0], negmax[:, :, :]).then_inc(msplit.sem, 1)
                dve.wait_ge(msplit.sem, msplit.at(b, 1))
                dve.tensor_tensor(maxrest[:, :, :], negmax[:, :, :], hs[0], ALU.subtract).then_inc(msplit.sem, 1)
                dve.wait_ge(msplit.sem, msplit.at(b, 2))
                dve.tensor_copy(hs[1], maxrest[:, :, :]).then_inc(msplit.sem, 1)
                dve.wait_ge(msplit.sem, msplit.at(b, 3))
                dve.tensor_tensor(hs[2], maxrest[:, :, :], hs[1], ALU.subtract).then_inc(msplit.sem, 2)

            def step_cell(b):
                dve.wait_ge(gfi_s.sem, gfi_s.at(b))
                if at(b, 0):
                    dve.wait_ge(setup_done.sem, 8)
                dve.scalar_tensor_tensor(out=ca[:, :], in0=gate[:, 0, :], scalar=1.0, in1=state[:, :], op0=ALU.add, op1=ALU.mult)\
                    .then_inc(cell.sem, 1)
                dve.wait_ge(gc_s.sem, gc_s.at(b))
                dve.scalar_tensor_tensor(out=cb[:, :], in0=gate[:, 1, :], scalar=1.0, in1=gate[:, 2, :], op0=ALU.add, op1=ALU.mult)\
                    .then_inc(cell.sem, 1)
                dve.wait_ge(cell.sem, cell.at(b, 2))
                dve.scalar_tensor_tensor(out=state[:, :], in0=ca[:, :], scalar=0.5, in1=cb[:, :], op0=ALU.mult, op1=ALU.add)\
                    .then_inc(cell.sem, 1)

            def quotient(b, i):
                dve.wait_ge(OQ_p.sem, OQ_p.at(b, i + 1))
                if onT_p.due(b - 1):
                    dve.wait_ge(onT_p.sem, onT_p.at(b - 1))
                heads = p_misc[:, :].rearrange("p (h c) -> p h c", c=32)
                dve.reciprocal(rz[:, i, :], heads[:, :, HD]).then_inc(rz_s.sem, 1)
                dve.wait_ge(rz_s.sem, rz_s.at(b, i + 1))
                dve.tensor_tensor(on[:, i, :].rearrange("p (h d) -> p h d", d=HD), heads[:, :, 0:HD],
                                  rz[:, i, :].rearrange("p (h o) -> p h o", o=1).broadcast_to([P, H, HD]), ALU.mult)\
                    .then_inc(on_s.sem, 1)

            def iteration(n, r):
                for i in range(3):
                    if at(n, i - 1):
                        dve.wait_ge(x_in[i].sem, 16)
                for s in range(8):
                    if active(n, 1):
                        for u in MAX_AT[s]:
                            row_max(n - 1, u)
                    if s == 0 and active(n, 5):
                        step_cell(n - 5)
                    if s == 2 and active(n, 0):
                        dve.wait_ge(qk_s.sem, qk_s.at(n))
                        if split.due(n - 1):
                            dve.wait_ge(split.sem, split.at(n - 1))
                        if parts_out.due(n - 1):
                            dve.wait_ge(parts_out.sem, parts_out.at(n - 1))
                        dve.tensor_tensor(rest[:, :, :], qk[r][:, :, :], part[:, 0, :, :], ALU.subtract).then_inc(split.sem, 1)
                        dve.wait_ge(split.sem, split.at(n, 1))
                        dve.tensor_copy(part[:, 1, :, :], rest[:, :, :]).then_inc(split.sem, 1)
                    if s == 2 and active(n, 0):
                        dve.wait_ge(v_p.sem, v_p.at(n))
                        if pv_p.due(n - RING):
                            dve.wait_ge(pv_p.sem, pv_p.at(n - RING))
                        dve.tensor_tensor(V[r][:, :, :, 0:HD], p_misc[:, 0:S].rearrange("p (i h d) -> p i h d", i=TT, d=HD),
                                          bv[:, :].rearrange("p (o h d) -> p o h d", o=1, d=HD).broadcast_to([P, TT, H, HD]), ALU.add)\
                            .then_inc(v_s.sem, 1)
                    if s == 3 and active(n, 3):
                        quotient(n - 3, 0)
                        quotient(n - 3, 1)
                    if s == 4 and active(n, 3):
                        b, q = n - 3, (r - 3) % RING
                        dve.wait_ge(proj_p.sem, proj_p.at(b))
                        dve.wait_ge(xb_s.sem, xb_s.at(b))
                        dve.tensor_tensor(X[:, bass.ds(2 * b, 2), :], p_misc[:, 0:S].rearrange("p (i d) -> p i d", i=TT), xb[q][:, :, :], ALU.add)\
                            .then_inc(x1_s.sem, 1)
                        dve.wait_ge(x1_s.sem, x1_s.at(b))
                        layer_stats(b, stats2[q], mv2[q], root2[q], stats_b, seed_b, norm_b)
                    if s == 5 and active(n, 1):
                        split_max(n - 1)
                    if s == 5 and active(n, -1):
                        q = (r + 1) % RING
                        layer_stats(n + 1, stats1[q], mv1[q], root1[q], stats_a, seed_a, norm_a)
                    if s == 6 and active(n, 3):
                        b, q = n - 3, (r - 3) % RING
                        if xn2T_p.due(b - RING):
                            dve.wait_ge(xn2T_p.sem, xn2T_p.at(b - RING))
                        layer_norm(b, mv2[q], root2[q], xn2[q], newton_b, norm_b)
                    if s == 7 and active(n, -1):
                        q = (r + 1) % RING
                        if xnT_p.due(n + 1 - RING):
                            dve.wait_ge(xnT_p.sem, xnT_p.at(n + 1 - RING))
                        layer_norm(n + 1, mv1[q], root1[q], xn1[q], newton_a, norm_a)

            pipeline(dve, iteration)

        @block.scalar
        def _(act):
            def iteration(n, r):
                for s in range(8):
                    if s == 0 and active(n, 0):
                        act.wait_ge(xnT_p.sem, xnT_p.at(n))
                        if v_p.due(n - RING):
                            act.wait_ge(v_p.sem, v_p.at(n - RING))
                        act.activation(xn1T[r][:, :], p_misc[:, 0:S], ACT.Copy).then_inc(xnT_s.sem, 1)
                    if s == 1 and active(n, 0):
                        act.wait_ge(qk_p.sem, qk_p.at(n))
                        if parts_out.due(n - 1):
                            act.wait_ge(parts_out.sem, parts_out.at(n - 1))
                        if split.due(n - 1):
                            act.wait_ge(split.sem, split.at(n - 1))
                        if at(n, 0):
                            act.wait_ge(setup_done.sem, 8)
                        for j, sc in enumerate((SCALE, 1.0)):
                            for dst in (qk[r][:, j, :], part[:, 0, j, :]):
                                act.activation(dst, p_misc[:, j * S:(j + 1) * S], ACT.Identity,
                                               bias=(bqk_s if j == 0 else bqk)[:, j:j + 1], scale=sc).then_inc(qk_s.sem, 1)
                    if s == 4 and active(n, 3):
                        b = n - 3
                        act.wait_ge(onT_p.sem, onT_p.at(b))
                        if proj_p.due(b - 1):
                            act.wait_ge(proj_p.sem, proj_p.at(b - 1))
                        act.activation(onT[:, :], p_misc[:, 0:S], ACT.Copy).then_inc(onT_s.sem, 1)
                    if s == 5 and active(n, 4):
                        b = n - 4
                        act.wait_ge(xn2T_p.sem, xn2T_p.at(b))
                        if gc_p.due(b - 1):
                            act.wait_ge(gc_p.sem, gc_p.at(b - 1))
                        act.activation(xn2T[:, :], p_misc[:, 0:S], ACT.Copy).then_inc(xn2T_s.sem, 1)
                        act.activation(XN2T[:, b, :], p_misc[:, 0:S], ACT.Copy).then_inc(xn2T_k.sem, 1)
                    if s == 6 and active(n, 4):
                        b = n - 4
                        act.wait_ge(gfi_p.sem, gfi_p.at(b))
                        if cell.due(b - 1):
                            act.wait_ge(cell.sem, cell.at(b - 1))
                        for j in range(2):
                            act.activation(gate[:, j, :], p_misc[:, j * S:(j + 1) * S], ACT.Tanh, bias=gates_bh[:, j:j + 1], scale=0.5)\
                                .then_inc(gfi_s.sem, 1)
                    if s == 7 and active(n, 1):
                        b = n - 1
                        act.wait_ge(maxT_p.sem, maxT_p.at(b))
                        if maxrow_in.due(b - 1):
                            act.wait_ge(maxrow_in.sem, maxrow_in.at(b - 1))
                        act.activation(maxT[:, :], p_misc[0:PARTS * H, 0:S // 2].bitcast(BF16), ACT.Copy).then_inc(maxT_s.sem, 1)
                    if active(n, 2):
                        b = n - 2
                        if score_p.due(b, s + 1):
                            act.wait_ge(score_p.sem, score_p.at(b, s + 1))
                        if pv_p.due(b, s - 1):
                            act.wait_ge(pv_p.sem, pv_p.at(b, s - 1))
                        act.activation(probs[s % 2][:, :, :].rearrange("p j q -> p (j q)"), p_exp[s % 2][:, :], ACT.Exp)\
                            .then_inc(prob_s.sem, 1)
                        if s % 2 == 0 and s > 0:
                            copy_out(n - 2, (r - 2) % RING, s // 2 - 1)
                    if s == 7 and active(n, 4):
                        b = n - 4
                        act.wait_ge(gc_p.sem, gc_p.at(b))
                        act.activation(gate[:, 2, :], p_misc[:, 0:S], ACT.Tanh, bias=gates_b[:, 2:3]).then_inc(gc_s.sem, 1)
                if active(n, 2):
                    copy_out(n - 2, (r - 2) % RING, 3)

            def copy_out(b, q, g):
                act.wait_ge(pv_p.sem, pv_p.at(b, 2 * g + 2))
                if g == 0:
                    if OQ_p.due(b - RING):
                        act.wait_ge(OQ_p.sem, OQ_p.at(b - RING))
                act.activation(OT[q][:, g, :], p_out[:, 0:S], ACT.Copy).then_inc(OT_s.sem, 1)

            pipeline(act, iteration)

        @block.tensor
        def _(pe):
            def scores(b, q, s):
                g, kt = s // 2, s % 2
                if prob_s.due(b, s - 1):
                    pe.wait_ge(prob_s.sem, prob_s.at(b, s - 1))
                for j in range(4):
                    h = 4 * g + j
                    mm = pe.matmul(p_exp[s % 2][:, j * S:(j + 1) * S], KS[q][:, h, kt * P:(kt + 1) * P], QS[q][:, h, :],
                                   start=True, stop=True)
                mm.then_inc(score_p.sem, 1)

            def weigh(b, q, s):
                g, kt = s // 2, s % 2
                if prob_s.due(b, s + 1):
                    pe.wait_ge(prob_s.sem, prob_s.at(b, s + 1))
                if s == 0:
                    pe.wait_ge(v_s.sem, v_s.at(b))
                if kt == 0:
                    if OT_s.due(b, g):
                        pe.wait_ge(OT_s.sem, OT_s.at(b, g))
                for j in range(4):
                    mm = pe.matmul(p_out[32 * j:32 * j + 32, 0:S], V[q][:, kt, 4 * g + j, :], probs[s % 2][:, j, :],
                                   start=(kt == 0), stop=(kt == 1))
                mm.then_inc(pv_p.sem, 1)

            def maxima(b, q, u):
                i, hp = u // 8, u % 8
                if max_s.due(b, u - 1):
                    pe.wait_ge(max_s.sem, max_s.at(b, u - 1))
                for j in range(2):
                    h = 2 * hp + j
                    mm = pe.matmul(p_max[u % 2][:, j * S:(j + 1) * S], QS[q][0:PAIRS, h, i * P:(i + 1) * P], KS[q][0:PAIRS, h, :],
                                   start=True, stop=True)
                mm.then_inc(max_p.sem, 1)

            def turn(src, n_tiles=TT):
                for i in range(n_tiles):
                    mm = pe.transpose(p_misc[:, i * P:(i + 1) * P], src[:, i, :], ident[:, :])
                return mm

            def misc(n, r, at_slot):
                b3, b4, q3, q4 = n - 3, n - 4, (r - 3) % RING, (r - 4) % RING
                if at_slot == "0" and active(n, 0):
                    pe.wait_ge(norm_a.sem, norm_a.at(n))
                    if active(n, 5):
                        if gc_s.due(n - 5):
                            pe.wait_ge(gc_s.sem, gc_s.at(n - 5))
                    elif active(n, 2):
                        if maxT_s.due(n - 2):
                            pe.wait_ge(maxT_s.sem, maxT_s.at(n - 2))
                    elif active(n, 1):
                        if v_s.due(n - 1):
                            pe.wait_ge(v_s.sem, v_s.at(n - 1))
                    turn(xn1[r]).then_inc(xnT_p.sem, 1)
                if at_slot == "1" and active(n, 0):
                    pe.wait_ge(xnT_s.sem, xnT_s.at(n))
                    for j in range(2):
                        mm = pe.matmul(p_misc[:, j * S:(j + 1) * S], Wqkv[:, j * D:(j + 1) * D], xn1T[r][:, :], start=True, stop=True)
                    mm.then_inc(qk_p.sem, 1)
                if at_slot == "2" and active(n, 0):
                    pe.wait_ge(qk_s.sem, qk_s.at(n))
                    for i in range(TT):
                        mm = pe.matmul(p_misc[:, i * P:(i + 1) * P], xn1T[r][:, i * P:(i + 1) * P], Wqkv[:, 2 * D:3 * D], start=True, stop=True)
                    mm.then_inc(v_p.sem, 1)
                if at_slot in ("3", "3b") and active(n, 3):
                    i = ("3", "3b").index(at_slot)
                    if i:
                        pe.wait_ge(on_s.sem, on_s.at(b3, 1))
                    else:
                        pe.wait_ge(OT_s.sem, OT_s.at(b3))
                        if active(n, 0):
                            pe.wait_ge(v_s.sem, v_s.at(n))
                        elif active(n, 5):
                            if gc_s.due(n - 5):
                                pe.wait_ge(gc_s.sem, gc_s.at(n - 5))
                    for g in range(NG):
                        mm = pe.transpose(p_misc[:, g * P:(g + 1) * P], OT[q3][:, g, i * P:(i + 1) * P], ident[:, :])
                    mm.then_inc(OQ_p.sem, 1)
                if at_slot == "4" and active(n, 3):
                    pe.wait_ge(on_s.sem, on_s.at(b3))
                    turn(on).then_inc(onT_p.sem, 1)
                if at_slot == "4b" and active(n, 3):
                    pe.wait_ge(onT_s.sem, onT_s.at(b3))
                    for i in range(TT):
                        mm = pe.matmul(p_misc[:, i * P:(i + 1) * P], onT[:, i * P:(i + 1) * P], Wout[:, :], start=True, stop=True)
                    mm.then_inc(proj_p.sem, 1)
                if at_slot == "5" and active(n, 4):
                    pe.wait_ge(norm_b.sem, norm_b.at(b4))
                    if active(n, 3):
                        pe.wait_ge(x1_s.sem, x1_s.at(b3))
                    else:
                        if gc_s.due(n - 5):
                            pe.wait_ge(gc_s.sem, gc_s.at(n - 5))
                    turn(xn2[q4]).then_inc(xn2T_p.sem, 1)
                if at_slot == "6" and active(n, 4):
                    pe.wait_ge(xn2T_s.sem, xn2T_s.at(b4))
                    pe.wait_ge(xn2T_k.sem, xn2T_k.at(b4))
                    if cell.due(b4 - 1):
                        pe.wait_ge(cell.sem, cell.at(b4 - 1))
                    for j in range(2):
                        pe.matmul(p_misc[:, j * S:(j + 1) * S], gates_w[:, j, :], xn2T[:, :], start=True, stop=False)
                        mm = pe.matmul(p_misc[:, j * S:(j + 1) * S], gates_uh[:, j, :], state[:, :], start=False, stop=True)
                    mm.then_inc(gfi_p.sem, 1)
                if at_slot == "7" and active(n, 1):
                    if msplit.due(n - 1):
                        pe.wait_ge(msplit.sem, msplit.at(n - 1))
                    if active(n, 4):
                        pe.wait_ge(gfi_s.sem, gfi_s.at(b4))
                    elif active(n, 3):
                        pe.wait_ge(x1_s.sem, x1_s.at(b3))
                    else:
                        pe.wait_ge(v_s.sem, v_s.at(n))
                    steady(pe, t)
                    for i in range(TT):
                        mm = pe.transpose(p_misc[0:PARTS * H, i * P // 2:(i + 1) * P // 2].bitcast(BF16),
                                          maxpart[:, i, :, :].rearrange("p k h -> p (k h)"), ident16[:, :])
                    mm.then_inc(maxT_p.sem, 1)
                if at_slot == "7b" and active(n, 4):
                    if active(n, 1):
                        if maxT_s.due(n - 1):
                            pe.wait_ge(maxT_s.sem, maxT_s.at(n - 1))
                    pe.wait_ge(gfi_s.sem, gfi_s.at(b4))
                    pe.matmul(p_misc[:, 0:S], gates_w[:, 2, :], xn2T[:, :], start=True, stop=False)
                    pe.matmul(p_misc[:, 0:S], gates_uh[:, 2, :], state[:, :], start=False, stop=True).then_inc(gc_p.sem, 1)

            def iteration(n, r):
                q1, q2 = (r - 1) % RING, (r - 2) % RING
                if at(n, -1):
                    pe.wait_ge(w_in.sem, w_in.at(0, 16 * 9))
                    pe.wait_ge(consts.sem, t["n_consts"])
                    pe.wait_ge(setup_done.sem, 8)
                    pe.wait_ge(t["v_set"].sem, 6)
                if active(n, 1):
                    if stack_in.due(n - 1):
                        pe.wait_ge(stack_in.sem, stack_in.at(n - 1))
                for s in range(8):
                    if active(n, 1):
                        for u in MAX_AT[s]:
                            maxima(n - 1, q1, u)
                    misc(n, r, str(s))
                    if active(n, 2):
                        if s == 0:
                            if maxrow_in.due(n - 2):
                                pe.wait_ge(maxrow_in.sem, maxrow_in.at(n - 2))
                        scores(n - 2, q2, s)
                        if s:
                            weigh(n - 2, q2, s - 1)
                    misc(n, r, str(s) + "b")
                if active(n, 2):
                    weigh(n - 2, q2, 7)

            pipeline(pe, iteration)


E = 16
HID = 256
TOP = 2
TOKENS = B * S
REGION = TOKENS + P
TILES = 80
ROW = D + 2
NOWHERE = float(4 * TOKENS)
PAIR = 2
Z2 = 3 * D


def linear_attention_and_routing(nc, ctx, t):

    def sig(name, per=1):
        return Signal(nc, ctx, name, per)

    with ExitStack() as scope:
        def psum(name, cols=512):
            return scope.enter_context(nc.psum_tensor(name, [P, cols], F32))

        def tmp(name, shape, dt=F32):
            return scope.enter_context(nc.sbuf_tensor(name, shape, dt))

        X, XN2T, state, ident = t["X"], t["XN2T"], t["state"], t["ident"]
        w = t["w2"]
        count = t["count"]
        disp = t["disp"]

        UC = tmp("UC", [P, S])
        uoh = tmp("uoh", [P, D])
        KVones = [tmp(f"KVones_{r}", [P, TT, D + 2]) for r in range(PAIR)]
        zs = [tmp(f"zs_{r}", [P, S]) for r in range(PAIR)]
        hT = [tmp(f"hT_{r}", [P, S]) for r in range(PAIR)]
        stats3, stats4 = [tmp(f"stats3_{r}", [P, TT, 6]) for r in range(PAIR)], [tmp(f"stats4_{r}", [P, TT, 6]) for r in range(PAIR)]
        mv, root = [tmp(f"mv_{r}", [P, 2 * TT, 2]) for r in range(PAIR)], [tmp(f"root_{r}", [P, 5, 2 * TT]) for r in range(PAIR)]
        xn3 = [tmp(f"xn3_{r}", [P, TT, D]) for r in range(PAIR)]
        xn3T = [tmp(f"xn3T_{r}", [P, S]) for r in range(PAIR)]
        t1, t2 = tmp("t1", [P, TT, 2 * D]), tmp("t2", [P, TT, 2 * D])
        rot = [tmp(f"rot_{r}", [P, TT, 2 * D]) for r in range(PAIR)]
        ex, rl = tmp("ex", [P, TT, 2 * D]), tmp("rl", [P, TT, 2 * D])
        feat = [tmp(f"feat_{r}", [P, TT, 2 * D]) for r in range(PAIR)]
        KVm = tmp("KVm", [P, D + H])
        qfT = tmp("qfT", [P, S])
        den, on3, on3T = tmp("den", [P, TT, H]), tmp("on3", [P, TT, D]), tmp("on3T", [P, S])
        pay = [[tmp(f"pay{k}_{r}", [P, TT, ROW]) for k in range(TOP)] for r in range(PAIR)]
        xn4T = tmp("xn4T", [P, S])
        lg, negtop, probs4, z = tmp("lg", [P, TT, E]), tmp("negtop", [P, TT]), tmp("probs4", [P, TT, E]), tmp("z", [P, TT])
        best = tmp("best", [P, TT, 8])
        where = tmp("where", [P, TT, 8], U32)
        wheref = tmp("wheref", [P, TT, TOP])
        hot = [tmp(f"hot_{r}", [P, TT, TOP, E]) for r in range(PAIR)]
        sel = [tmp(f"sel_{r}", [P, TT, E], BF16) for r in range(PAIR)]
        ids = tmp("ids", [P, TT, TOP])
        place, mine, posf = tmp("place", [P, TT, E]), tmp("mine", [P, TT, TOP, E]), tmp("posf", [P, TT, TOP])
        pos = [tmp(f"pos_{r}", [P, TT, TOP], U32) for r in range(PAIR)]
        nup = [count, tmp("count_b", [P, E])]

        p_h, p_ta, p_tb, p_qkv = psum("p_h"), psum("p_ta"), psum("p_tb"), psum("p_qkv", 1024)
        p_kvo, p_u, p_r = psum("p_kvo"), psum("p_u"), psum("p_r")

        uc_ready = sig("uc_ready", 2)
        s2 = sig("setup2")
        z_p, z_s, h_s, hT_p, x2_s = sig("z_p"), sig("z_s"), sig("h_s"), sig("hT_p"), sig("x2_s")
        st3, sd, nw, nm3 = sig("st3", 4), sig("sd", 4), sig("nw", 3 * NEWTON + 1), sig("nm3", 2)
        x3T_p, x3T_s, qkv_p = sig("x3T_p"), sig("x3T_s"), sig("qkv_p")
        v3_s, t_s, rot_s, el_s, feat_s = sig("v3_s"), sig("t_s", 3), sig("rot_s"), sig("el_s", 2), sig("feat_s")
        kv_p, kv_s, qfT_p, qfT_s, o_p = sig("kv_p"), sig("kv_s", 2), sig("qfT_p"), sig("qfT_s"), sig("o_p")
        o_s, onT3_p, onT3_s, u_p, x3_s = sig("o_s", 3), sig("onT3_p"), sig("onT3_s"), sig("u_p"), sig("x3_s")
        st4, nm4, pay1_s, res, mv_set = sig("st4", 4), sig("nm4", 2), sig("pay1_s"), sig("res"), sig("mv_set")
        x4T_p, x4T_s, lg_p, lg_s, ex4_s = sig("x4T_p"), sig("x4T_s"), sig("lg_p"), sig("lg_s", 3), sig("ex4_s")
        pr_s, top_s, hot_s, pay_s = sig("pr_s", 3), sig("top_s", 4), sig("hot_s", 3), sig("pay_s", 5)
        rank_p, pos_s, sent = sig("rank_p"), sig("pos_s", 6), sig("sent", 16 * TT * TOP)
        t["pos_s"], t["sent"], t["res"], t["rank_p"] = pos_s, sent, res, rank_p
        sel_s, gate_in, ids_up = sig("sel_s"), sig("gate_in", TOP), sig("ids_up")

        LAST, PEEL = B + 5, 7

        def active(n, lag):
            return not isinstance(n, int) or 0 <= n - lag < B

        def at(n, first):
            return isinstance(n, int) and n == first

        def pipeline(eng, iteration):
            for n in range(PEEL):
                iteration(n, n % PAIR)
            with eng.Fori(0, (B - 1 - PEEL) // PAIR, 1) as k:
                for c in range(PAIR):
                    iteration(k * PAIR + (PEEL + c), (PEEL + c) % PAIR)
            for n in range(B - 1, LAST):
                iteration(n, n % PAIR)

        block = scope.enter_context(nc.Block())

        @block.gpsimd
        def _(pool):
            pool.wait_ge(w["loaded"].sem, w["loaded"].at(0))
            pool.tensor_scalar(uoh[:, :], w["uo"][:, :], 0.5, None, ALU.mult).then_inc(s2.sem, 1)
            for r in range(PAIR):
                pool.memset(KVones[r][:, :, D:D + 2], 1.0).then_inc(s2.sem, 1)
            pool.iota(ids[:, :, :], pattern=[[2 * P, TT], [1, TOP]], base=0, channel_multiplier=2,
                      allow_small_or_imprecise_dtypes=True).then_inc(s2.sem, 1)

            def iteration(n, r):
                o = 1 - r
                if active(n, 5):
                    b = n - 5
                    pool.wait_ge(pos_s.sem, pos_s.at(b))
                    pool.wait_ge(pay_s.sem, pay_s.at(b))
                    pool.wait_ge(gate_in.sem, gate_in.at(b))
                    pool.wait_ge(nm4.sem, nm4.at(b))
                    pool.wait_ge(pay1_s.sem, pay1_s.at(b))
                    if sent.due(b - 1):
                        pool.wait_ge(sent.sem, sent.at(b - 1))
                    steady(pool, t)
                    for i in range(TT):
                        for k in range(TOP):
                            pool.indirect_dma_start(out=disp, out_offset=bass.IndirectOffsetOnAxis(ap=pos[o][:, i, k:k + 1], axis=0),
                                                    in_=pay[o][k][:, i, :], in_offset=None).then_inc(sent.sem, 16)
                if active(n, 4):
                    b = n - 4
                    pool.wait_ge(nm4.sem, nm4.at(b))
                    steady(pool, t)
                    pool.tensor_tensor(X[:, bass.ds(2 * b, 2), :], X[:, bass.ds(2 * b, 2), :], pay[r][0][:, :, 0:D], ALU.add)\
                        .then_inc(res.sem, 1)
                if active(n, 1):
                    b = n - 1
                    pool.wait_ge(t_s.sem, t_s.at(b))
                    if el_s.due(b - PAIR):
                        pool.wait_ge(el_s.sem, el_s.at(b - PAIR))
                    pool.tensor_tensor(rot[o][:, :, :], t1[:, :, :], t2[:, :, :], ALU.add).then_inc(rot_s.sem, 1)

            pipeline(pool, iteration)

        @block.vector
        def _(dve):
            def root_step(m, r, step):
                if not (active(m, 0) or active(m, 3)):
                    return
                y, u, shift, half, v = (root[r][:, j, :] for j in range(5))
                newton = step - 3
                if step == 0:
                    if active(m, 0):
                        dve.wait_ge(st3.sem, st3.at(m))
                    if active(m, 3):
                        dve.wait_ge(st4.sem, st4.at(m - 3))
                    if active(m, PAIR):
                        dve.wait_ge(nm3.sem, nm3.at(m - PAIR))
                    if nm4.due(m - 3 - PAIR):
                        dve.wait_ge(nm4.sem, nm4.at(m - 3 - PAIR))
                    dve.tensor_scalar(v, mv[r][:, :, 1], EPS, None, ALU.add).then_inc(sd.sem, 1)
                elif step == 1:
                    dve.wait_ge(sd.sem, sd.at(m, 1))
                    dve.tensor_scalar(u.bitcast(U32), v.bitcast(U32), 1, None, ALU.logical_shift_right).then_inc(sd.sem, 1)
                    dve.tensor_scalar(half, v, -0.5, None, ALU.mult).then_inc(sd.sem, 1)
                elif step == 2:
                    dve.wait_ge(sd.sem, sd.at(m, 3))
                    dve.tensor_scalar(y.bitcast(I32), u.bitcast(I32), -1.0, float(MAGIC), ALU.mult, ALU.add).then_inc(sd.sem, 1)
                elif newton < 3 * NEWTON:
                    if newton:
                        dve.wait_ge(nw.sem, nw.at(m, newton))
                    else:
                        dve.wait_ge(sd.sem, sd.at(m))
                    if newton % 3 == 0:
                        dve.tensor_tensor(u, y, y, ALU.mult).then_inc(nw.sem, 1)
                    elif newton % 3 == 1:
                        dve.tensor_tensor(u, u, half, ALU.mult).then_inc(nw.sem, 1)
                    else:
                        dve.scalar_tensor_tensor(out=y, in0=u, scalar=1.5, in1=y, op0=ALU.add, op1=ALU.mult).then_inc(nw.sem, 1)
                else:
                    dve.wait_ge(nw.sem, nw.at(m, 3 * NEWTON))
                    dve.scalar_tensor_tensor(out=shift, in0=mv[r][:, :, 0], scalar=-1.0, in1=y, op0=ALU.mult, op1=ALU.mult).then_inc(nw.sem, 1)

            def wide(ap, shape):
                return ap.broadcast_to(shape)

            def iteration(n, r):
                o = 1 - r
                outs = p_kvo[:, :].rearrange("p (i c) -> p i c", i=TT)
                three, four = slice(0, TT), slice(TT, 2 * TT)
                if at(n, 0):
                    dve.wait_ge(uc_ready.sem, 2)
                    for q in range(PAIR):
                        dve.memset(mv[q][:, :, :], 1.0).then_inc(mv_set.sem, 1)
                    dve.wait_ge(mv_set.sem, PAIR)
                if active(n, 0):
                    dve.wait_ge(z_p.sem, z_p.at(n))
                    if h_s.due(n - PAIR):
                        dve.wait_ge(h_s.sem, h_s.at(n - PAIR))
                    dve.tensor_tensor(zs[r][:, :], p_h[:, 0:S], UC[:, :], ALU.add).then_inc(z_s.sem, 1)
                if active(n, 4):
                    b = n - 4
                    dve.wait_ge(nw.sem, nw.at(n - 1))
                    if sent.due(b - PAIR):
                        dve.wait_ge(sent.sem, sent.at(b - PAIR))
                    if res.due(b - PAIR):
                        dve.wait_ge(res.sem, res.at(b - PAIR))
                    dve.tensor_scalar(pay[r][0][:, 0, 0:D], X[:, 2 * b, :], mv[o][:, TT, 0:1], root[o][:, 0, TT:TT + 1],
                                      ALU.subtract, ALU.mult).then_inc(nm4.sem, 1)
                if active(n, 5):
                    b = n - 5
                    cur, nxt = nup[o], nup[r]
                    dve.wait_ge(rank_p.sem, rank_p.at(b))
                    if at(n, 5):
                        dve.wait_ge(t["count_set"].sem, 2)
                    ranks = p_r[:, 64:64 + TT * E].rearrange("p (i e) -> p i e", i=TT)
                    dve.tensor_tensor(place[:, :, :], ranks, wide(cur[:, :].rearrange("p (o e) -> p o e", o=1), [P, TT, E]), ALU.add)\
                        .then_inc(pos_s.sem, 1)
                    dve.tensor_tensor(nxt[:, :], p_r[:, 96:96 + E], cur[:, :], ALU.add).then_inc(pos_s.sem, 1)
                if active(n, 4):
                    b = n - 4
                    dve.tensor_scalar(pay[r][0][:, 1, 0:D], X[:, 2 * b + 1, :], mv[o][:, TT + 1, 0:1], root[o][:, 0, TT + 1:TT + 2],
                                      ALU.subtract, ALU.mult).then_inc(nm4.sem, 1)
                if active(n, 5):
                    b = n - 5
                    dve.wait_ge(pos_s.sem, pos_s.at(b, 2))
                    for i in range(TT):
                        dve.tensor_tensor(mine[:, i, :, :], hot[o][:, i, :, :],
                                          wide(place[:, i, :].rearrange("p (o e) -> p o e", o=1), [P, TOP, E]), ALU.mult).then_inc(pos_s.sem, 1)
                if active(n, 3):
                    b = n - 3
                    dve.wait_ge(o_p.sem, o_p.at(b))
                    if onT3_p.due(b - 1):
                        dve.wait_ge(onT3_p.sem, onT3_p.at(b - 1))
                    dve.tensor_scalar(den[:, :, :], outs[:, :, D:D + H], 1e-6, None, ALU.max).then_inc(o_s.sem, 1)
                if active(n, 5):
                    b = n - 5
                    dve.wait_ge(pos_s.sem, pos_s.at(b, 4))
                    dve.tensor_reduce(posf[:, :, :], mine[:, :, :, :], AX.X, ALU.add).then_inc(pos_s.sem, 1)
                if active(n, 3):
                    b = n - 3
                    dve.wait_ge(o_s.sem, o_s.at(b, 1))
                    dve.reciprocal(den[:, :, :], den[:, :, :]).then_inc(o_s.sem, 1)
                if active(n, 5):
                    b = n - 5
                    dve.wait_ge(pos_s.sem, pos_s.at(b, 5))
                    dve.tensor_copy(pos[o][:, :, :], posf[:, :, :]).then_inc(pos_s.sem, 1)
                if active(n, 3):
                    b = n - 3
                    dve.wait_ge(o_s.sem, o_s.at(b, 2))
                    dve.tensor_tensor(on3[:, :, :].rearrange("p i (h d) -> p i h d", d=HD), outs[:, :, 0:D].rearrange("p i (h d) -> p i h d", d=HD),
                                      wide(den[:, :, :].rearrange("p i (h o) -> p i h o", o=1), [P, TT, H, HD]), ALU.mult).then_inc(o_s.sem, 1)
                if active(n, 2):
                    b = n - 2
                    dve.wait_ge(el_s.sem, el_s.at(b))
                    if qfT_p.due(b - PAIR):
                        dve.wait_ge(qfT_p.sem, qfT_p.at(b - PAIR))
                    dve.scalar_tensor_tensor(out=feat[r][:, :, :], in0=ex[:, :, :], scalar=1.0, in1=rl[:, :, :], op0=ALU.min, op1=ALU.add)\
                        .then_inc(feat_s.sem, 1)
                if active(n, 0):
                    dve.wait_ge(hT_p.sem, hT_p.at(n))
                    dve.tensor_tensor(X[:, bass.ds(2 * n, 2), :], p_h[:, 0:S].rearrange("p (i d) -> p i d", i=TT), X[:, bass.ds(2 * n, 2), :], ALU.add)\
                        .then_inc(x2_s.sem, 1)
                if active(n, 0):
                    dve.wait_ge(x2_s.sem, x2_s.at(n))
                    steady(dve, t)
                    for i in range(TT):
                        dve.bn_stats(stats3[r][:, i, :], X[:, 2 * n + i, :]).then_inc(st3.sem, 1)
                if active(n, 0):
                    dve.wait_ge(st3.sem, st3.at(n, 2))
                    if nw.due(n - PAIR):
                        dve.wait_ge(nw.sem, nw.at(n - PAIR))
                    steady(dve, t)
                    for i in range(TT):
                        dve.bn_aggr(mv[r][:, i, :], stats3[r][:, i, :]).then_inc(st3.sem, 1)
                if active(n, 1):
                    b = n - 1
                    dve.wait_ge(qkv_p.sem, qkv_p.at(b))
                    if rot_s.due(b - 1):
                        dve.wait_ge(rot_s.sem, rot_s.at(b - 1))
                    qkp = p_qkv[:, :].rearrange("p (i c) -> p i c", i=TT)[:, :, 0:2 * D]
                    dve.tensor_tensor(t1[:, :, :], qkp, w["cosf"][:, :, :], ALU.mult).then_inc(t_s.sem, 1)
                    halves = [x.rearrange("p i (g a d) -> p i g a d", a=2, d=HD // 2) for x in (qkp, t2[:, :, :], w["sinf"][:, :, :])]
                    for a in range(2):
                        dve.tensor_tensor(halves[1][:, :, :, a, :], halves[0][:, :, :, 1 - a, :], halves[2][:, :, :, a, :], ALU.mult)\
                            .then_inc(t_s.sem, 1)
                if active(n, 4):
                    b = n - 4
                    dve.wait_ge(lg_p.sem, lg_p.at(b))
                    if ex4_s.due(b - 1):
                        dve.wait_ge(ex4_s.sem, ex4_s.at(b - 1))
                    dve.tensor_tensor(lg[:, :, :], p_r[:, 0:TT * E].rearrange("p (i e) -> p i e", i=TT),
                                      wide(w["br"][:, :].rearrange("p (o e) -> p o e", o=1), [P, TT, E]), ALU.add).then_inc(lg_s.sem, 1)
                if active(n, 3):
                    b = n - 3
                    dve.wait_ge(u_p.sem, u_p.at(b))
                    dve.wait_ge(nm3.sem, nm3.at(b))
                    dve.tensor_tensor(X[:, bass.ds(2 * b, 2), :], p_u[:, 0:S].rearrange("p (i d) -> p i d", i=TT), X[:, bass.ds(2 * b, 2), :], ALU.add)\
                        .then_inc(x3_s.sem, 1)
                if active(n, 4):
                    b = n - 4
                    dve.wait_ge(lg_s.sem, lg_s.at(b, 1))
                    dve.tensor_reduce(negtop[:, :], lg[:, :, :], AX.X, ALU.max, negate=True).then_inc(lg_s.sem, 1)
                if active(n, 3):
                    b = n - 3
                    dve.wait_ge(x3_s.sem, x3_s.at(b))
                    steady(dve, t)
                    for i in range(TT):
                        dve.bn_stats(stats4[o][:, i, :], X[:, 2 * b + i, :]).then_inc(st4.sem, 1)
                if active(n, 4):
                    b = n - 4
                    dve.wait_ge(lg_s.sem, lg_s.at(b, 2))
                    dve.tensor_tensor(lg[:, :, :], lg[:, :, :], wide(negtop[:, :].rearrange("p (i o) -> p i o", o=1), [P, TT, E]), ALU.add)\
                        .then_inc(lg_s.sem, 1)
                if active(n, 3):
                    b = n - 3
                    dve.wait_ge(st4.sem, st4.at(b, 2))
                    if nm4.due(b - PAIR):
                        dve.wait_ge(nm4.sem, nm4.at(b - PAIR))
                    steady(dve, t)
                    for i in range(TT):
                        dve.bn_aggr(mv[r][:, TT + i, :], stats4[o][:, i, :]).then_inc(st4.sem, 1)
                if active(n, 2):
                    b = n - 2
                    dve.wait_ge(kv_p.sem, kv_p.at(b))
                    if o_p.due(b - 1):
                        dve.wait_ge(o_p.sem, o_p.at(b - 1))
                    dve.tensor_tensor(KVm[:, 0:D], p_kvo[:, 0:D], w["block_mask"][:, :], ALU.mult).then_inc(kv_s.sem, 1)
                if active(n, 2):
                    dve.tensor_scalar(KVm[:, D:D + H], w["head_mask"][:, :], p_kvo[:, D:D + 1], None, ALU.mult).then_inc(kv_s.sem, 1)
                root_step(n, r, 0)
                if active(n, 4):
                    b = n - 4
                    dve.wait_ge(ex4_s.sem, ex4_s.at(b))
                    dve.tensor_reduce(z[:, :], probs4[:, :, :], AX.X, ALU.add).then_inc(pr_s.sem, 1)
                root_step(n, r, 1)
                if active(n, 4):
                    b = n - 4
                    dve.wait_ge(pr_s.sem, pr_s.at(b, 1))
                    dve.reciprocal(z[:, :], z[:, :]).then_inc(pr_s.sem, 1)
                root_step(n, r, 2)
                if active(n, 4):
                    b = n - 4
                    dve.wait_ge(pr_s.sem, pr_s.at(b, 2))
                    dve.tensor_tensor(probs4[:, :, :], probs4[:, :, :], wide(z[:, :].rearrange("p (i o) -> p i o", o=1), [P, TT, E]), ALU.mult)\
                        .then_inc(pr_s.sem, 1)
                root_step(n, r, 3)
                if active(n, 4):
                    b = n - 4
                    dve.wait_ge(pr_s.sem, pr_s.at(b, 3))
                    steady(dve, t)
                    for i in range(TT):
                        dve.max(best[:, i, :], probs4[:, i, :]).then_inc(top_s.sem, 1)
                root_step(n, r, 4)
                if active(n, 4):
                    b = n - 4
                    for i in range(TT):
                        dve.wait_ge(top_s.sem, top_s.at(b, 1 + i))
                        steady(dve, t)
                        dve.max_index(where[:, i, :], best[:, i, :], probs4[:, i, :]).then_inc(top_s.sem, 1)
                root_step(n, r, 5)
                if active(n, 4):
                    b = n - 4
                    if sent.due(b - PAIR):
                        dve.wait_ge(sent.sem, sent.at(b - PAIR))
                    dve.tensor_tensor(z[:, :], best[:, :, 0], best[:, :, 1], ALU.add).then_inc(pay_s.sem, 1)
                if active(n, 4):
                    b = n - 4
                    dve.wait_ge(top_s.sem, top_s.at(b))
                    dve.tensor_copy(wheref[:, :, :], where[:, :, 0:TOP]).then_inc(hot_s.sem, 1)
                root_step(n, r, 6)
                if active(n, 4):
                    b = n - 4
                    dve.wait_ge(pay_s.sem, pay_s.at(b, 1))
                    dve.tensor_scalar(z[:, :], z[:, :], 1e-9, None, ALU.max).then_inc(pay_s.sem, 1)
                if active(n, 4):
                    b = n - 4
                    dve.wait_ge(hot_s.sem, hot_s.at(b, 1))
                    for i in range(TT):
                        dve.tensor_tensor(hot[r][:, i, :, :], wide(w["iota_e"][:, :].rearrange("p (o e) -> p o e", o=1), [P, TOP, E]),
                                          wide(wheref[:, i, :].rearrange("p (k o) -> p k o", o=1), [P, TOP, E]), ALU.is_equal)\
                            .then_inc(hot_s.sem, 1)
                root_step(n, r, 7)
                if active(n, 4):
                    b = n - 4
                    dve.wait_ge(pay_s.sem, pay_s.at(b, 2))
                    dve.reciprocal(z[:, :], z[:, :]).then_inc(pay_s.sem, 1)
                root_step(n, r, 8)
                if active(n, 4):
                    b = n - 4
                    dve.wait_ge(hot_s.sem, hot_s.at(b))
                    if rank_p.due(b - PAIR):
                        dve.wait_ge(rank_p.sem, rank_p.at(b - PAIR))
                    dve.tensor_tensor(sel[r][:, :, :], hot[r][:, :, 0, :], hot[r][:, :, 1, :], ALU.add).then_inc(sel_s.sem, 1)
                root_step(n, r, 9)
                if active(n, 4):
                    b = n - 4
                    dve.wait_ge(pay_s.sem, pay_s.at(b, 3))
                    for k in range(TOP):
                        dve.tensor_tensor(pay[r][k][:, :, D], best[:, :, k], z[:, :], ALU.mult).then_inc(gate_in.sem, 1)
                root_step(n, r, 10)
                if active(n, 4):
                    b = n - 4
                    if at(n, 4):
                        dve.wait_ge(s2.sem, 4)
                    if ids_up.due(b - 1):
                        dve.wait_ge(ids_up.sem, ids_up.at(b - 1))
                    for k in range(TOP):
                        dve.tensor_copy(pay[r][k][:, :, D + 1], ids[:, :, k]).then_inc(pay_s.sem, 1)
                root_step(n, r, 11)
                if active(n, 4):
                    b = n - 4
                    dve.wait_ge(pay_s.sem, pay_s.at(b))
                    dve.tensor_scalar(ids[:, :, :], ids[:, :, :], float(TOP * S), None, ALU.add).then_inc(ids_up.sem, 1)
                root_step(n, r, 12)

            pipeline(dve, iteration)

        @block.scalar
        def _(act):
            act.wait_ge(uc_ready.sem, 1)
            act.activation(UC[:, :], p_u[:, 0:S], ACT.Identity, bias=w["bo"][:, 0:1]).then_inc(uc_ready.sem, 1)

            def iteration(n, r):
                o = 1 - r
                if active(n, 1):
                    b = n - 1
                    act.wait_ge(nw.sem, nw.at(b))
                    act.wait_ge(x2_s.sem, x2_s.at(b))
                    if x3T_p.due(b - PAIR):
                        act.wait_ge(x3T_p.sem, x3T_p.at(b - PAIR))
                    for i in range(TT):
                        act.activation(xn3[o][:, i, :], X[:, 2 * b + i, :], ACT.Identity, bias=root[o][:, 2, i:i + 1],
                                       scale=root[o][:, 0, i:i + 1]).then_inc(nm3.sem, 1)
                if active(n, 2):
                    b = n - 2
                    act.wait_ge(rot_s.sem, rot_s.at(b))
                    if feat_s.due(b - 1):
                        act.wait_ge(feat_s.sem, feat_s.at(b - 1))
                    act.activation(ex[:, :, :], rot[r][:, :, :], ACT.Exp).then_inc(el_s.sem, 1)
                    act.activation(rl[:, :, :], rot[r][:, :, :], ACT.Relu).then_inc(el_s.sem, 1)
                if active(n, 0):
                    act.wait_ge(z_s.sem, z_s.at(n))
                    if hT_p.due(n - PAIR):
                        act.wait_ge(hT_p.sem, hT_p.at(n - PAIR))
                    act.activation(hT[r][:, :], zs[r][:, :], ACT.Tanh).then_inc(h_s.sem, 1)
                if active(n, 1):
                    b = n - 1
                    act.wait_ge(x3T_p.sem, x3T_p.at(b))
                    if qkv_p.due(b - PAIR):
                        act.wait_ge(qkv_p.sem, qkv_p.at(b - PAIR))
                    act.activation(xn3T[o][:, :], p_ta[:, 0:S], ACT.Copy).then_inc(x3T_s.sem, 1)
                if active(n, 4):
                    b = n - 4
                    act.wait_ge(x4T_p.sem, x4T_p.at(b))
                    if lg_p.due(b - 1):
                        act.wait_ge(lg_p.sem, lg_p.at(b - 1))
                    act.activation(xn4T[:, :], p_tb[:, 0:S], ACT.Copy).then_inc(x4T_s.sem, 1)
                if active(n, 4):
                    b = n - 4
                    act.wait_ge(nm4.sem, nm4.at(b))
                    if sent.due(b - PAIR):
                        act.wait_ge(sent.sem, sent.at(b - PAIR))
                    act.activation(pay[r][1][:, :, 0:D], pay[r][0][:, :, 0:D], ACT.Copy).then_inc(pay1_s.sem, 1)
                if active(n, 3):
                    b = n - 3
                    act.wait_ge(onT3_p.sem, onT3_p.at(b))
                    if u_p.due(b - 1):
                        act.wait_ge(u_p.sem, u_p.at(b - 1))
                    act.activation(on3T[:, :], p_tb[:, 0:S], ACT.Copy).then_inc(onT3_s.sem, 1)
                if active(n, 4):
                    b = n - 4
                    act.wait_ge(lg_s.sem, lg_s.at(b))
                    if top_s.due(b - 1):
                        act.wait_ge(top_s.sem, top_s.at(b - 1))
                    act.activation(probs4[:, :, :], lg[:, :, :], ACT.Exp).then_inc(ex4_s.sem, 1)
                if active(n, 1):
                    b = n - 1
                    act.wait_ge(qkv_p.sem, qkv_p.at(b))
                    act.wait_ge(t_s.sem, t_s.at(b))
                    if kv_p.due(b - PAIR):
                        act.wait_ge(kv_p.sem, kv_p.at(b - PAIR))
                    if at(n, 1):
                        act.wait_ge(s2.sem, 4)
                    act.activation(KVones[o][:, :, 0:D], p_qkv[:, :].rearrange("p (i c) -> p i c", i=TT)[:, :, 2 * D:3 * D], ACT.Copy)\
                        .then_inc(v3_s.sem, 1)
                if active(n, 2):
                    act.wait_ge(qfT_p.sem, qfT_p.at(n - 2))
                    if o_p.due(n - 3):
                        act.wait_ge(o_p.sem, o_p.at(n - 3))
                    act.activation(qfT[:, :], p_ta[:, 0:S], ACT.Copy).then_inc(qfT_s.sem, 1)

            pipeline(act, iteration)

        @block.tensor
        def _(pe):
            if t["cell"].due(B - 1):
                pe.wait_ge(t["cell"].sem, t["cell"].at(B - 1))
            pe.wait_ge(s2.sem, 4)
            pe.wait_ge(w["loaded"].sem, w["loaded"].at(0))
            pe.matmul(p_u[:, 0:S], uoh[:, :], state[:, :], start=True, stop=True).then_inc(uc_ready.sem, 1)
            pe.wait_ge(uc_ready.sem, 2)
            pe.matmul(p_h[:, 0:S], w["wo"][:, :], XN2T[:, 0, :], start=True, stop=True).then_inc(z_p.sem, 1)

            def turn(dst, src):
                for i in range(TT):
                    mm = pe.transpose(dst[:, i * P:(i + 1) * P], src[:, i, 0:P], ident[:, :])
                return mm

            def iteration(n, r):
                o = 1 - r
                if active(n, 5):
                    b = n - 5
                    pe.wait_ge(sel_s.sem, sel_s.at(b))
                    pe.wait_ge(lg_s.sem, lg_s.at(b, 1))
                    tri, ones = w["before"], w["ones16"]
                    k0, k1 = sel[o][:, 0, :], sel[o][:, 1, :]
                    c = 64
                    pe.matmul(p_r[:, c:c + E], tri[:, :], k0, start=True, stop=True)
                    pe.matmul(p_r[:, c + E:c + 2 * E], tri[:, :], k1, start=True, stop=False)
                    pe.matmul(p_r[:, c + E:c + 2 * E], ones[:, :], k0, start=False, stop=True)
                    pe.matmul(p_r[:, c + 2 * E:c + 3 * E], ones[:, :], k0, start=True, stop=False)
                    pe.matmul(p_r[:, c + 2 * E:c + 3 * E], ones[:, :], k1, start=False, stop=True).then_inc(rank_p.sem, 1)
                if active(n, 3):
                    b = n - 3
                    pe.wait_ge(qfT_s.sem, qfT_s.at(b))
                    pe.wait_ge(kv_s.sem, kv_s.at(b))
                    for i in range(TT):
                        mm = pe.matmul(p_kvo[:, i * S:i * S + D + H], qfT[:, i * P:(i + 1) * P], KVm[:, :], start=True, stop=True)
                    mm.then_inc(o_p.sem, 1)
                if active(n, 1):
                    b = n - 1
                    pe.wait_ge(nm3.sem, nm3.at(b))
                    if active(n, 3):
                        pe.wait_ge(qfT_s.sem, qfT_s.at(n - 3))
                    turn(p_ta, xn3[o]).then_inc(x3T_p.sem, 1)
                if active(n, 4):
                    b = n - 4
                    pe.wait_ge(nm4.sem, nm4.at(b))
                    pe.wait_ge(onT3_s.sem, onT3_s.at(b))
                    turn(p_tb, pay[r][0]).then_inc(x4T_p.sem, 1)
                if active(n, 0):
                    pe.wait_ge(h_s.sem, h_s.at(n))
                    pe.wait_ge(z_s.sem, z_s.at(n))
                    turn(p_h, hT[r][:, :].rearrange("p (i d) -> p i d", i=TT)).then_inc(hT_p.sem, 1)
                if active(n, 1):
                    b = n - 1
                    pe.wait_ge(x3T_s.sem, x3T_s.at(b))
                    if t_s.due(b - 1):
                        pe.wait_ge(t_s.sem, t_s.at(b - 1))
                    if v3_s.due(b - 1):
                        pe.wait_ge(v3_s.sem, v3_s.at(b - 1))
                    for i in range(TT):
                        mm = pe.matmul(p_qkv[:, i * 512:i * 512 + Z2], xn3T[o][:, i * P:(i + 1) * P], w["Wqkv2"][:, :], start=True, stop=True)
                    mm.then_inc(qkv_p.sem, 1)
                if active(n, 3):
                    b = n - 3
                    pe.wait_ge(o_s.sem, o_s.at(b))
                    if active(n, 4):
                        pe.wait_ge(x4T_s.sem, x4T_s.at(n - 4))
                    turn(p_tb, on3).then_inc(onT3_p.sem, 1)
                if active(n, 4):
                    b = n - 4
                    pe.wait_ge(x4T_s.sem, x4T_s.at(b))
                    if pos_s.due(b - 1):
                        pe.wait_ge(pos_s.sem, pos_s.at(b - 1, 2))
                    for i in range(TT):
                        mm = pe.matmul(p_r[:, i * E:(i + 1) * E], xn4T[:, i * P:(i + 1) * P], w["Wr"][:, :], start=True, stop=True)
                    mm.then_inc(lg_p.sem, 1)
                if active(n, 3):
                    b = n - 3
                    pe.wait_ge(onT3_s.sem, onT3_s.at(b))
                    if x3_s.due(b - 1):
                        pe.wait_ge(x3_s.sem, x3_s.at(b - 1))
                    for i in range(TT):
                        mm = pe.matmul(p_u[:, i * P:(i + 1) * P], on3T[:, i * P:(i + 1) * P], w["Wout2"][:, :], start=True, stop=True)
                    mm.then_inc(u_p.sem, 1)
                if active(n, 2):
                    b = n - 2
                    pe.wait_ge(feat_s.sem, feat_s.at(b))
                    pe.wait_ge(v3_s.sem, v3_s.at(b))
                    if o_s.due(b - 1):
                        pe.wait_ge(o_s.sem, o_s.at(b - 1))
                    for i in range(TT):
                        mm = pe.matmul(p_kvo[:, 0:D + 2], feat[r][:, i, D:2 * D], KVones[r][:, i, :], start=(i == 0), stop=(i == 1))
                    mm.then_inc(kv_p.sem, 1)
                    if active(n, 1):
                        pe.wait_ge(x3T_s.sem, x3T_s.at(n - 1))
                    turn(p_ta, feat[r]).then_inc(qfT_p.sem, 1)
                if isinstance(n, int) and n + 1 >= B:
                    pass
                else:
                    pe.wait_ge(x2_s.sem, x2_s.at(n))
                    pe.matmul(p_h[:, 0:S], w["wo"][:, :], XN2T[:, n + 1, :], start=True, stop=True).then_inc(z_p.sem, 1)

            pipeline(pe, iteration)


def experts(nc, ctx, t):

    def sig(name, per=1):
        return Signal(nc, ctx, name, per)

    with ExitStack() as scope:
        def psum(name, cols=512):
            return scope.enter_context(nc.psum_tensor(name, [P, cols], F32))

        def tmp(name, shape, dt=F32):
            return scope.enter_context(nc.sbuf_tensor(name, shape, dt))

        w, X, ident, disp, back = t["w2"], t["X"], t["ident"], t["disp"], t["back"]
        count = t["count"]
        R3 = 4

        fill = tmp("fill", [P, ROW])
        counti, endi = tmp("counti", [P, E], I32), tmp("endi", [P, E], I32)
        full, tiles = tmp("full", [P, E]), [tmp(f"tiles{i}", [P, E]) for i in range(2)]
        passed, prev, eno, prevt, off = tmp("passed", [P, TILES, E]), tmp("prev", [P, TILES, E]), tmp("eno", [P, TILES]), tmp("prevt", [P, TILES]), tmp("off", [P, TILES])
        offi, enoi = tmp("offi", [P, TILES], I32), tmp("enoi", [P, TILES], I32)
        rows = [tmp(f"rows{r}", [P, ROW]) for r in range(R3)]
        xT = [tmp(f"xT{r}", [P, P]) for r in range(R3)]
        w1 = [tmp(f"w1_{r}", [P, HID + 2]) for r in range(R3)]
        hid = [tmp(f"hid{r}", [P, 2, P]) for r in range(R3)]
        y = [tmp(f"y{r}", [P, D]) for r in range(R3)]
        to = [tmp(f"to{r}", [P, 1], U32) for r in range(R3)]
        NB = 4
        yb = [tmp(f"yb{i}", [P, NB, TOP * D]) for i in range(2 * B // NB)]

        p_x = [psum(f"p_x{i}") for i in range(2)]
        p_hid = [psum(f"p_hid{i}") for i in range(2)]
        p_y = [psum(f"p_y{i}") for i in range(2)]

        fill_s, plan, table, pad = sig("fill_s"), sig("plan"), sig("table"), sig("pad")
        rows_in = [sig(f"rows_in{i}", 16) for i in range(R3)]
        x_p, x_s, w_s, hid_p, hid_s, y_p, y_s, to_s = sig("x_p"), sig("x_s"), sig("w_s"), sig("hid_p"), sig("hid_s", 2), sig("y_p"), sig("y_s"), sig("to_s")
        yout = [sig(f"yout{i}", 16) for i in range(R3)]
        yb_in = [sig(f"yb_in{i}", 16) for i in range(2 * B // NB)]
        sum_s, out_done = sig("sum_s", 2), sig("out_done")

        def pipeline(eng, step):
            for k in range(2):
                for r in range(R3):
                    step(k * R3 + r, k, r)
            with eng.Fori(2, TILES // R3, 1) as k:
                for r in range(R3):
                    step(k * R3 + r, k, r)
            for r in range(2):
                step(None, TILES // R3, r)

        def behind(i, k, r, lag):
            last = i is None
            i = TILES + r if last else i
            if isinstance(i, int) and (i < lag or i - lag >= TILES):
                return []
            return [(i - lag, (r - lag) % R3, k if r >= lag else k - 1)]

        block = scope.enter_context(nc.Block())

        @block.gpsimd
        def _(pool):
            pool.memset(fill[:, 0:D + 1], 0.0).then_inc(fill_s.sem, 1)
            pool.memset(fill[:, D + 1:ROW], NOWHERE).then_inc(fill_s.sem, 1)

            def step(i, k, r):
                if i is None:
                    return
                pool.wait_ge(y_s.sem, y_s.at(i))
                pool.wait_ge(to_s.sem, to_s.at(i))
                steady(pool, t)
                pool.indirect_dma_start(out=back, out_offset=bass.IndirectOffsetOnAxis(ap=to[r][:, 0:1], axis=0), in_=y[r][:, :],
                                        in_offset=None, bounds_check=TOP * TOKENS - 1, oob_is_err=False).then_inc(yout[r].sem, 16)

            pipeline(pool, step)

        @block.sync
        def _(sp):
            sp.wait_ge(fill_s.sem, 2)
            if t["sent"].due(B - 1):
                sp.wait_ge(t["sent"].sem, t["sent"].at(B - 1))
            sp.wait_ge(plan.sem, plan.at(0, 1))
            for e in range(E):
                end = sp.value_load(endi[0:1, e:e + 1], min_val=e * REGION, max_val=e * REGION + TOKENS)
                sp.dma_start(disp[bass.ds(end, P), :], fill[:, :]).then_inc(pad.sem, 16)
            sp.dma_start(disp[E * REGION:E * REGION + P, :], fill[:, :]).then_inc(pad.sem, 16)
            sp.wait_ge(pad.sem, 16 * (E + 1))
            sp.wait_ge(table.sem, 2)

            def step(i, k, r):
                if i is None:
                    return
                at = sp.value_load(offi[0:1, bass.ds(i, 1)], min_val=0, max_val=E * REGION)
                if x_p.due(i - R3):
                    sp.wait_ge(x_p.sem, x_p.at(i - R3))
                if to_s.due(i - R3):
                    sp.wait_ge(to_s.sem, to_s.at(i - R3))
                if y_s.due(i - R3):
                    sp.wait_ge(y_s.sem, y_s.at(i - R3))
                steady(sp, t)
                sp.dma_start(rows[r][:, :], disp[bass.ds(at, P), :]).then_inc(rows_in[r].sem, 16)

            pipeline(sp, step)
            for r in range(R3):
                if yout[r].due(TILES // R3 - 1):
                    sp.wait_ge(yout[r].sem, yout[r].at(TILES // R3 - 1))
            bv = back.rearrange("(n p k) d -> p n (k d)", p=P, k=TOP)
            ov = t["out"].rearrange("(n p) d -> p n d", p=P)
            for c in range(2 * B // NB):
                sp.dma_start(yb[c][:, :, :], bv[:, c * NB:(c + 1) * NB, :]).then_inc(yb_in[c].sem, 16)
            for c in range(2 * B // NB):
                sp.wait_ge(sum_s.sem, sum_s.at(c))
                sp.dma_start(ov[:, c * NB:(c + 1) * NB, :], X[:, c * NB:(c + 1) * NB, :]).then_inc(out_done.sem, 16)
            sp.wait_ge(out_done.sem, 16 * (2 * B // NB))

        @block.vector
        def _(dve):
            n = [0]

            def then(ins, mark=plan):
                n[0] += 1
                ins.then_inc(mark.sem, 1)
                dve.wait_ge(mark.sem, n[0])

            if t["pos_s"].due(B - 1):
                dve.wait_ge(t["pos_s"].sem, t["pos_s"].at(B - 1))
            then(dve.tensor_copy(endi[:, :], count[:, :]))
            then(dve.tensor_tensor(full[:, :], count[:, :], w["region"][:, :], ALU.subtract))
            then(dve.tensor_scalar(counti[:, :], full[:, :], float(P - 1), None, ALU.add))
            then(dve.tensor_scalar(counti[:, :], counti[:, :], 7, None, ALU.logical_shift_right))
            then(dve.tensor_copy(tiles[0][:, :], counti[:, :]))
            for j, s in enumerate((1, 2, 4, 8)):
                a, b = tiles[j % 2], tiles[(j + 1) % 2]
                then(dve.tensor_copy(b[:, 0:s], a[:, 0:s]))
                then(dve.tensor_tensor(b[:, s:E], a[:, s:E], a[:, 0:E - s], ALU.add))
            cum = tiles[0]
            shape = [P, TILES, E]
            cw = cum[:, :].rearrange("p (o e) -> p o e", o=1).broadcast_to(shape)
            then(dve.tensor_tensor(passed[:, :, :], w["iota_t"][:, :].rearrange("p (t o) -> p t o", o=1).broadcast_to(shape), cw, ALU.is_ge))
            then(dve.tensor_tensor(prev[:, :, :], passed[:, :, :], cw, ALU.mult))
            then(dve.tensor_reduce(eno[:, :], passed[:, :, :], AX.X, ALU.add))
            then(dve.tensor_reduce(prevt[:, :], prev[:, :, :], AX.X, ALU.max))
            then(dve.tensor_tensor(off[:, :], w["iota_t"][:, :], prevt[:, :], ALU.subtract))
            then(dve.tensor_scalar(off[:, :], off[:, :], float(P), None, ALU.mult))
            then(dve.scalar_tensor_tensor(out=off[:, :], in0=eno[:, :], scalar=float(REGION), in1=off[:, :], op0=ALU.mult, op1=ALU.add))
            then(dve.tensor_scalar(off[:, :], off[:, :], float(E * REGION), None, ALU.min))
            then(dve.tensor_scalar(eno[:, :], eno[:, :], float(E - 1), None, ALU.min))
            dve.tensor_copy(offi[:, :], off[:, :]).then_inc(table.sem, 1)
            dve.tensor_copy(enoi[:, :], eno[:, :]).then_inc(table.sem, 1)
            dve.wait_ge(table.sem, 2)

            def step(i, k, r):
                if i is not None:
                    e = dve.value_load(enoi[0:1, bass.ds(i, 1)], min_val=0, max_val=E - 1)
                    if hid_p.due(i - R3):
                        dve.wait_ge(hid_p.sem, hid_p.at(i - R3))
                    if hid_s.due(i - R3):
                        dve.wait_ge(hid_s.sem, hid_s.at(i - R3))
                    dve.tensor_copy(w1[r][:, :], w["W1"][:, bass.ds(e, 1), :].rearrange("p o c -> p (o c)")).then_inc(w_s.sem, 1)
                    dve.wait_ge(rows_in[r].sem, rows_in[r].at(k))
                    if yout[r].due(k - 1):
                        dve.wait_ge(yout[r].sem, yout[r].at(k - 1))
                    dve.tensor_copy(to[r][:, :], rows[r][:, D + 1:ROW]).then_inc(to_s.sem, 1)
                for j, q, kq in behind(i, k, r, 2):
                    dve.wait_ge(y_p.sem, y_p.at(j))
                    if yout[q].due(kq - 1):
                        dve.wait_ge(yout[q].sem, yout[q].at(kq - 1))
                    dve.tensor_scalar(y[q][:, :], p_y[q % 2][:, 0:D], rows[q][:, D:D + 1], None, ALU.mult).then_inc(y_s.sem, 1)

            pipeline(dve, step)
            for c in range(2 * B // NB):
                sl = X[:, c * NB:(c + 1) * NB, :]
                dve.wait_ge(yb_in[c].sem, yb_in[c].at(0))
                dve.tensor_tensor(sl, sl, yb[c][:, :, 0:D], ALU.add).then_inc(sum_s.sem, 1)
                dve.wait_ge(sum_s.sem, sum_s.at(c, 1))
                dve.tensor_tensor(sl, sl, yb[c][:, :, D:2 * D], ALU.add).then_inc(sum_s.sem, 1)

        @block.scalar
        def _(act):
            def step(i, k, r):
                if i is not None:
                    act.wait_ge(x_p.sem, x_p.at(i))
                    if hid_p.due(i - R3):
                        act.wait_ge(hid_p.sem, hid_p.at(i - R3))
                    act.activation(xT[r][:, :], p_x[r % 2][:, 0:P], ACT.Copy).then_inc(x_s.sem, 1)
                for j, q, _ in behind(i, k, r, 1):
                    act.wait_ge(hid_p.sem, hid_p.at(j))
                    act.wait_ge(w_s.sem, w_s.at(j))
                    if y_p.due(j - R3):
                        act.wait_ge(y_p.sem, y_p.at(j - R3))
                    for c in range(2):
                        act.activation(hid[q][:, c, :], p_hid[q % 2][:, c * P:(c + 1) * P], ACT.Gelu, bias=w1[q][:, HID + c:HID + c + 1])\
                            .then_inc(hid_s.sem, 1)

            pipeline(act, step)

        @block.tensor
        def _(pe):
            pe.wait_ge(table.sem, 2)

            def step(i, k, r):
                if i is not None:
                    pe.wait_ge(rows_in[r].sem, rows_in[r].at(k))
                    if x_s.due(i - 2):
                        pe.wait_ge(x_s.sem, x_s.at(i - 2))
                    pe.transpose(p_x[r % 2][:, 0:P], rows[r][:, 0:D], ident[:, :]).then_inc(x_p.sem, 1)
                for j, q, _ in behind(i, k, r, 1):
                    pe.wait_ge(x_s.sem, x_s.at(j))
                    pe.wait_ge(w_s.sem, w_s.at(j))
                    if hid_s.due(j - 2):
                        pe.wait_ge(hid_s.sem, hid_s.at(j - 2))
                    for c in range(2):
                        mm = pe.matmul(p_hid[q % 2][:, c * P:(c + 1) * P], w1[q][:, c * P:(c + 1) * P], xT[q][:, :], start=True, stop=True)
                    mm.then_inc(hid_p.sem, 1)
                for j, q, _ in behind(i, k, r, 2):
                    e = pe.value_load(enoi[0:1, bass.ds(j, 1)], min_val=0, max_val=E - 1)
                    if y_s.due(j - 2):
                        pe.wait_ge(y_s.sem, y_s.at(j - 2))
                    pe.matmul(p_y[q % 2][:, 0:D], w["one_row"][:, :], w["b2"][0:1, bass.ds(e, 1), :].rearrange("p o c -> p (o c)"),
                              start=True, stop=False)
                    pe.wait_ge(hid_s.sem, hid_s.at(j))
                    for c in range(2):
                        mm = pe.matmul(p_y[q % 2][:, 0:D], hid[q][:, c, :], w["W2"][:, bass.ds(e, 1), c, :].rearrange("p o c -> p (o c)"),
                                       start=False, stop=(c == 1))
                    mm.then_inc(y_p.sem, 1)

            pipeline(pe, step)


def program(nc, x, Wqkv, bqk, bv, Wout, bout, gates_w, gates_u, gates_b, in_c, wo, uo, bo, Wqkv2, Wout2, Wr, br, W1, W2, b2, cosf, sinf, out):
    with ExitStack() as ctx:
        def sb(name, shape, dt=F32):
            return ctx.enter_context(nc.sbuf_tensor(name, shape, dt))

        t = dict(x_dram=x, Wqkv=Wqkv, bqk=bqk, bv=bv, Wout=Wout, bout=bout, gates_w=gates_w, gates_u=gates_u, gates_b=gates_b,
                 in_c=in_c, out=out)
        t["X"], t["XN2T"], t["state"] = sb("X", [P, 2 * B, D]), sb("XN2T", [P, B, S]), sb("state", [P, S])
        t["ident"], t["ident16"] = sb("ident", [P, P]), sb("ident16", [P, P], BF16)
        t["disp"] = nc.dram_tensor("disp", [E * REGION + P, ROW], F32).ap()
        t["back"] = nc.dram_tensor("back", [TOP * TOKENS, D], F32).ap()
        t["count"] = sb("count", [P, E])
        w = t["w2"] = dict(wo=sb("wo", [P, D]), uo=sb("uo", [P, D]), bo=sb("bo2", [P, 1]), Wqkv2=sb("Wqkv2", [P, 3 * D]),
                           Wout2=sb("Wout2", [P, D]), Wr=sb("Wr", [P, E]), br=sb("br", [P, E]), cosf=sb("cosf", [P, TT, 2 * D]),
                           sinf=sb("sinf", [P, TT, 2 * D]), W1=sb("W1", [P, E, HID + 2]), W2=sb("W2", [P, E, 2, D]),
                           b2=sb("b2", [1, E, D]), block_mask=sb("block_mask", [P, D]), head_mask=sb("head_mask", [P, H]),
                           before=sb("before", [P, P], BF16), ones16=sb("ones16", [P, P], BF16), iota_e=sb("iota_e", [P, E]),
                           iota_t=sb("iota_t", [P, TILES]), region=sb("region", [P, E]), one_row=sb("one_row", [1, P]),
                           loaded=Signal(nc, ctx, "loaded", 16 * 12))
        for name in ("consts", "v_set", "count_set", "const_steps"):
            t[name] = Signal(nc, ctx, name)

        with nc.Block() as block:
            @block.gpsimd
            def _(pool):
                n = 0
                fills = [(t["ident"], 0.0), (t["ident16"], 0.0), (w["block_mask"], 1.0), (w["head_mask"], 1.0), (w["before"], 1.0),
                         (w["ones16"], 1.0), (w["one_row"], 1.0)]
                for m, value in fills:
                    pool.memset(m[:, :], value).then_inc(t["const_steps"].sem, 1)
                n += len(fills)
                pool.iota(w["iota_e"][:, :], pattern=[[1, E]], base=0, channel_multiplier=0, allow_small_or_imprecise_dtypes=True)\
                    .then_inc(t["const_steps"].sem, 1)
                pool.iota(w["iota_t"][:, :], pattern=[[1, TILES]], base=0, channel_multiplier=0, allow_small_or_imprecise_dtypes=True)\
                    .then_inc(t["const_steps"].sem, 1)
                n += 2
                for m in (w["region"], t["count"]):
                    pool.iota(m[:, :], pattern=[[REGION, E]], base=0, channel_multiplier=0, allow_small_or_imprecise_dtypes=True)\
                        .then_inc(t["count_set"].sem, 1)
                pool.wait_ge(t["const_steps"].sem, n)
                for m in (t["ident"], t["ident16"]):
                    pool.affine_select(out=m[:, :], in_=m[:, :], compare_op=ALU.not_equal, fill=1.0, base=0, pattern=[[-1, P]],
                                       channel_multiplier=1).then_inc(t["consts"].sem, 1)
                pool.affine_select(out=w["before"][:, :], in_=w["before"][:, :], compare_op=ALU.is_gt, fill=0.0, base=0,
                                   pattern=[[1, P]], channel_multiplier=-1).then_inc(t["consts"].sem, 1)
                for step, (op, base, sign) in enumerate(((ALU.is_ge, 0, 1), (ALU.is_ge, HD - 1, -1))):
                    m = w["block_mask"][:, :].rearrange("p (h d) -> p h d", d=HD)
                    pool.affine_select(out=m, in_=m, compare_op=op, fill=0.0, base=base, pattern=[[-HD * sign, H], [0, HD]],
                                       channel_multiplier=sign).then_inc(t["consts"].sem, 1)
                    pool.affine_select(out=w["head_mask"][:, :], in_=w["head_mask"][:, :], compare_op=op, fill=0.0, base=base,
                                       pattern=[[-HD * sign, H]], channel_multiplier=sign).then_inc(t["consts"].sem, 1)
                    pool.wait_ge(t["consts"].sem, 5 + 2 * step)
        t["n_consts"] = 7
        t["w2_loads"] = [(w["wo"], wo), (w["uo"], uo), (w["bo"], bo), (w["Wqkv2"], Wqkv2), (w["Wout2"], Wout2), (w["Wr"], Wr),
                         (w["br"], br.partition_broadcast(P)), (w["cosf"], cosf), (w["sinf"], sinf), (w["W1"], W1), (w["W2"], W2), (w["b2"], b2)]
        attention_and_recurrence(nc, ctx, t)
        linear_attention_and_routing(nc, ctx, t)
        experts(nc, ctx, t)


def kernel(**inputs):
    import numpy as np
    import concourse.bacc as bacc
    from concourse.bass_utils import run_bass_kernel_spmd

    g = {k: np.asarray(v) for k, v in inputs.items()}
    ffn = lambda name: g["L0_ffn_" + name]
    bqkv = g["L0_attn_bqkv"]
    angle = np.arange(S, dtype=np.float32)[:, None] * (1.0 / 10000.0 ** (np.arange(0, HD, 2, dtype=np.float32) / HD))[None, :]
    cos, sin = np.cos(angle), np.sin(angle)
    factors = np.array([SCALE, 1.0], np.float32)[None, :, None, None, None]
    full = lambda lo, hi: np.broadcast_to(factors * np.stack([lo, hi], 1)[:, None, None], (S, 2, H, 2, HD // 2))
    table = lambda a: np.ascontiguousarray(a.reshape(TT, P, 2 * D).transpose(1, 0, 2)).astype(np.float32)
    b1 = g["L1_ffn_b1"].reshape(E, 2, P).transpose(2, 0, 1)
    laid = {
        "x": g["L0_attn_x"].reshape(TOKENS, D),
        "Wqkv": g["L0_attn_Wqkv"], "bqk": bqkv[:2 * D].reshape(2, P).T, "bv": bqkv[2 * D:],
        "Wout": g["L0_attn_Wout"], "bout": g["L0_attn_bout"],
        "gates_w": np.stack([ffn("wf").T, ffn("wi").T, ffn("wc").T], 1),
        "gates_u": np.stack([ffn("uf").T, ffn("ui").T, ffn("uc").T], 1),
        "gates_b": np.stack([ffn("bf"), ffn("bi"), ffn("bc")], 1),
        "in_c": ffn("in_c").reshape(P, 1),
        "wo": ffn("wo").T, "uo": ffn("uo").T, "bo": ffn("bo").reshape(P, 1),
        "Wqkv2": g["L1_attn_w_qkv"].T, "Wout2": g["L1_attn_w_out"].T,
        "Wr": g["L1_ffn_Wr"], "br": g["L1_ffn_br"],
        "W1": np.concatenate([g["L1_ffn_W1"].transpose(1, 0, 2), b1], 2),
        "W2": g["L1_ffn_W2"].reshape(E, 2, P, D).transpose(2, 0, 1, 3),
        "b2": g["L1_ffn_b2"].reshape(1, E, D),
        "cosf": table(full(cos, cos)), "sinf": table(full(-sin, sin)),
    }
    nc = bacc.Bacc("TRN2", target_bir_lowering=False, num_devices=1)
    arrays, args = {}, []
    for name, a in laid.items():
        a = np.ascontiguousarray(a)
        arrays[f"in_{name}_dram"] = a
        args.append(nc.dram_tensor(f"in_{name}_dram", a.shape, mybir.dt.from_np(a.dtype), kind="ExternalInput").ap())
    args.append(nc.dram_tensor("out_dram", (TOKENS, D), F32, kind="ExternalOutput").ap())
    program(nc, *args)
    result = run_bass_kernel_spmd(nc, [arrays], core_ids=[0])
    return result.results[0]["out_dram"].reshape(B, S, D)
```

```python
from contextlib import ExitStack

import concourse.bass as bass
from concourse import mybir

F32 = mybir.dt.float32
BF16 = mybir.dt.bfloat16
I32 = mybir.dt.int32
U32 = mybir.dt.uint32
ALU = mybir.AluOpType
ACT = mybir.ActivationFunctionType
AX = mybir.AxisListType

P = 128
B = 16
S = 256
D = 128
H = 16
HD = D // H
TT = S // P
EPS = 1e-5
NG = 4
RING = 3
PARTS = 3
PAIRS = 6 * HD
SCALE = HD ** -0.5
MAX_BEFORE = range(3)
MAX_AT = [range(a, b) for a, b in ((3, 5), (5, 7), (7, 9), (9, 11), (11, 14), (14, 16), (16, 16), (16, 16))]
MAGIC = 0x5F3759DF
NEWTON = 3
TWO_ONES = 1.0 + 0x3F80 / 2 ** 23


class Signal:

    def __init__(self, nc, ctx, name, per=1):
        self.sem = ctx.enter_context(nc.semaphore(name))
        self.per = per

    def at(self, b, part=None):
        value = b * self.per + (self.per if part is None else part)
        assert not isinstance(value, int) or value > 0
        return value

    def due(self, b, part=None):
        value = b * self.per + (self.per if part is None else part)
        return not isinstance(value, int) or value > 0


def steady(eng, t):
    eng.nop(nofuse=True)


def newton_steps(t, pool, root, mark, b):
    y, u, v = root[:, 0, :], root[:, 1, :], root[:, 3, :]
    j = 0
    for _ in range(NEWTON):
        if j:
            pool.wait_ge(mark.sem, mark.at(b, j))
        pool.tensor_tensor(u, y, y, ALU.mult).then_inc(mark.sem, 1)
        pool.wait_ge(mark.sem, mark.at(b, j + 1))
        pool.tensor_tensor(u, u, v, ALU.mult).then_inc(mark.sem, 1)
        pool.wait_ge(mark.sem, mark.at(b, j + 2))
        steady(pool, t)
        pool.tensor_scalar(u, u, -0.5, 1.5, ALU.mult, ALU.add).then_inc(mark.sem, 1)
        pool.wait_ge(mark.sem, mark.at(b, j + 3))
        pool.tensor_tensor(y, y, u, ALU.mult).then_inc(mark.sem, 1)
        j += 4


def constants(pool, t, w):
    n = 0
    fills = [(t["ident"], 0.0), (t["ident16"], 0.0), (w["kv_mask"], 1.0), (w["before"], 1.0),
             (w["ones16"], 1.0), (w["one_row"], 1.0)]
    for m, value in fills:
        pool.memset(m[:, :], value).then_inc(t["const_steps"].sem, 1)
    n += len(fills)
    pool.iota(w["iota_e"][:, :], pattern=[[1, E]], base=0, channel_multiplier=0, allow_small_or_imprecise_dtypes=True)\
        .then_inc(t["const_steps"].sem, 1)
    pool.iota(w["iota_t"][:, :], pattern=[[0, 1]], base=0, channel_multiplier=1, allow_small_or_imprecise_dtypes=True)\
        .then_inc(t["const_steps"].sem, 1)
    n += 2
    for m in (w["region"], t["count"]):
        pool.iota(m[:, :], pattern=[[REGION, E]], base=0, channel_multiplier=0, allow_small_or_imprecise_dtypes=True)\
            .then_inc(t["count_set"].sem, 1)
    pool.wait_ge(t["const_steps"].sem, n)
    for m in (t["ident"], t["ident16"]):
        pool.affine_select(out=m[:, :], in_=m[:, :], compare_op=ALU.not_equal, fill=1.0, base=0, pattern=[[-1, P]],
                           channel_multiplier=1).then_inc(t["consts"].sem, 1)
    pool.affine_select(out=w["before"][:, :], in_=w["before"][:, :], compare_op=ALU.is_gt, fill=0.0, base=0,
                       pattern=[[1, P]], channel_multiplier=-1).then_inc(t["consts"].sem, 1)
    for step, (op, base, sign) in enumerate(((ALU.is_ge, 0, 1), (ALU.is_ge, HD - 1, -1))):
        m = w["kv_mask"][:, 0:D].rearrange("p (h d) -> p h d", d=HD)
        pool.affine_select(out=m, in_=m, compare_op=op, fill=0.0, base=base, pattern=[[-HD * sign, H], [0, HD]],
                           channel_multiplier=sign).then_inc(t["consts"].sem, 1)
        pool.affine_select(out=w["kv_mask"][:, D:D + H], in_=w["kv_mask"][:, D:D + H], compare_op=op, fill=0.0, base=base,
                           pattern=[[-HD * sign, H]], channel_multiplier=sign).then_inc(t["consts"].sem, 1)
        pool.wait_ge(t["consts"].sem, 5 + 2 * step)


def attention_and_recurrence(nc, ctx, t):

    def sb(name, shape, dt=F32):
        return ctx.enter_context(nc.sbuf_tensor(name, shape, dt))

    def sig(name, per=1):
        return Signal(nc, ctx, name, per)

    with ExitStack() as scope:
        def psum(name, cols=512):
            return scope.enter_context(nc.psum_tensor(name, [P, cols], F32))

        def tmp(name, shape, dt=F32):
            return scope.enter_context(nc.sbuf_tensor(name, shape, dt))

        X, XN2T, state = t["X"], t["XN2T"], t["state"]
        ident, ident16 = t["ident"], t["ident16"]

        Wqkv, Wout = tmp("Wqkv", [P, 3 * D]), tmp("Wout", [P, D])
        bqk, bqk_s = tmp("bqk", [P, 2]), tmp("bqk_s", [P, 2])
        bv, bo = tmp("bv", [P, D]), tmp("bo", [P, D])
        gates_w, gates_u, gates_uh = tmp("gates_w", [P, 3, D]), tmp("gates_u", [P, 3, D]), tmp("gates_uh", [P, 3, D])
        gates_b, gates_bh = tmp("gates_b", [P, 3]), tmp("gates_bh", [P, 3])
        c_start, zeros = tmp("c_start", [P, 1]), tmp("zeros", [P, S])

        stats1, mv1 = [tmp(f"stats1_{r}", [P, TT, 6]) for r in range(RING)], [tmp(f"mv1_{r}", [P, TT, 2]) for r in range(RING)]
        stats2, mv2 = [tmp(f"stats2_{r}", [P, TT, 6]) for r in range(RING)], [tmp(f"mv2_{r}", [P, TT, 2]) for r in range(RING)]
        root1, root2 = [tmp(f"root1_{r}", [P, 5, TT]) for r in range(RING)], [tmp(f"root2_{r}", [P, 5, TT]) for r in range(RING)]
        xn1 = [tmp(f"xn1_{r}", [P, TT, D]) for r in range(RING)]
        xn1T = [tmp(f"xn1T_{r}", [P, S]) for r in range(RING)]
        qk = [tmp(f"qk_{r}", [P, 2, S]) for r in range(RING)]
        part = tmp("part", [P, PARTS, 2, S], BF16)
        rest = tmp("rest", [P, 2, S])
        QS = [tmp(f"QS_{r}", [PAIRS + PARTS, H, S], BF16) for r in range(RING)]
        KS = [tmp(f"KS_{r}", [PAIRS + PARTS, H, S], BF16) for r in range(RING)]
        V = [tmp(f"V_{r}", [P, TT, H, 32]) for r in range(RING)]
        negmax = tmp("negmax", [P, TT, H])
        maxrest = tmp("maxrest", [P, TT, H])
        maxpart = tmp("maxpart", [P, TT, PARTS, H], BF16)
        maxT = tmp("maxT", [PARTS * H, S], BF16)
        probs = [tmp(f"probs_{r}", [P, 4, S]) for r in range(2)]
        OT = [tmp(f"OT_{r}", [P, NG, S]) for r in range(RING)]
        rz = tmp("rz", [P, TT, H])
        on = tmp("on", [P, TT, D])
        onT = tmp("onT", [P, S])
        xb = [tmp(f"xb_{r}", [P, TT, D]) for r in range(RING)]
        xn2 = [tmp(f"xn2_{r}", [P, TT, D]) for r in range(RING)]
        xn2T = tmp("xn2T", [P, S])
        gate = tmp("gate", [P, 3, S])
        ca, cb = tmp("ca", [P, S]), tmp("cb", [P, S])

        p_exp = [psum(f"p_exp{i}", 1024) for i in range(2)]
        p_max = [psum(f"p_max{i}") for i in range(2)]
        p_out = psum("p_out")
        p_misc = psum("p_misc")

        scratch = [nc.dram_tensor(f"scratch_{r}", [2, PARTS, HD, H, S], BF16).ap() for r in range(RING)]

        x_in = [sig(f"x_in{i}") for i in range(3)]
        w_in = sig("w_in")
        consts = t["consts"]
        setup_done, ones_set = sig("setup_done", 5), sig("ones_set", RING)
        stats_a = sig("stats_a", 4)
        seed_a = sig("seed_a", 3)
        newton_a = sig("newton_a", 4 * NEWTON)
        norm_a = sig("norm_a", 2)
        xnT_p = sig("xnT_p")
        xnT_s = sig("xnT_s")
        qk_p = sig("qk_p")
        qk_s = sig("qk_s", 4)
        v_p = sig("v_p")
        v_s = sig("v_s")
        split = sig("split", 3)
        parts_out = sig("parts_out", 16 * 2 * PARTS)
        stack_in = sig("stack_in", 16 * 6)
        max_p = sig("max_p", 16)
        max_s = sig("max_s", 16)
        msplit = sig("msplit", 5)
        maxT_p = sig("maxT_p")
        maxT_s = sig("maxT_s")
        maxrow_in = sig("maxrow_in", 16 * PARTS)
        score_p = sig("score_p", 8)
        prob_s = sig("prob_s", 8)
        pv_p = sig("pv_p", 8)
        OT_s = sig("OT_s", 4)
        xb_s = sig("xb_s")
        OQ_p = sig("OQ_p", 2)
        rz_s = sig("rz_s", 2)
        on_s = sig("on_s", 2)
        onT_p = sig("onT_p")
        onT_s = sig("onT_s")
        proj_p = sig("proj_p")
        x1_s = sig("x1_s")
        stats_b = sig("stats_b", 4)
        seed_b = sig("seed_b", 3)
        newton_b = sig("newton_b", 4 * NEWTON)
        norm_b = sig("norm_b", 2)
        xn2T_p = sig("xn2T_p")
        xn2T_s = sig("xn2T_s")
        xn2T_k = sig("xn2T_k")
        gfi_p = sig("gfi_p")
        gfi_s = sig("gfi_s", 2)
        gc_p = sig("gc_p")
        gc_s = sig("gc_s")
        cell = sig("cell", 3)
        t["cell"] = cell

        LAST = B + 5
        PEEL = 6

        def pipeline(eng, iteration):
            for n in range(-1, PEEL):
                iteration(n, n % RING)
            with eng.Fori(0, (B - 1 - PEEL) // RING, 1) as k:
                for c in range(RING):
                    iteration(k * RING + (PEEL + c), (PEEL + c) % RING)
            for n in range(B - 1, LAST):
                iteration(n, n % RING)

        def active(n, lag):
            return not isinstance(n, int) or 0 <= n - lag < B

        def at(n, first):
            return isinstance(n, int) and n == first

        block = scope.enter_context(nc.Block())

        @block.sync
        def _(sp):
            xv = t["x_dram"].rearrange("(n p) d -> p n d", p=P)
            sp.dma_start(X[:, 0:2, :], xv[:, 0:2, :]).then_inc(x_in[0].sem, 16)
            sp.dma_start(Wqkv[:, :], t["Wqkv"]).then_inc(w_in.sem, 16)
            sp.dma_start(bqk[:, :], t["bqk"]).then_inc(w_in.sem, 16)
            sp.dma_start(bv[:, :], t["bv"].partition_broadcast(P)).then_inc(w_in.sem, 16)
            sp.dma_start(bo[:, :], t["bout"].partition_broadcast(P)).then_inc(w_in.sem, 16)
            sp.dma_start(X[:, 2:4, :], xv[:, 2:4, :]).then_inc(x_in[1].sem, 16)
            sp.dma_start(Wout[:, :], t["Wout"]).then_inc(w_in.sem, 16)
            sp.dma_start(gates_w[:, :, :], t["gates_w"]).then_inc(w_in.sem, 16)
            sp.dma_start(gates_u[:, :, :], t["gates_u"]).then_inc(w_in.sem, 16)
            sp.dma_start(gates_b[:, :], t["gates_b"]).then_inc(w_in.sem, 16)
            sp.dma_start(c_start[:, :], t["in_c"]).then_inc(w_in.sem, 16)
            sp.dma_start(X[:, 4:2 * B, :], xv[:, 4:2 * B, :]).then_inc(x_in[2].sem, 16)

            def iteration(n, r):
                for step in range(5):
                    for dst, src in t["w2_loads"][2 * step:2 * step + 2] if at(n, step + 1) else []:
                        sp.dma_start(dst[tuple(slice(None) for _ in dst.shape)], src).then_inc(t["w2"]["loaded"].sem, 16)
                if active(n, 0):
                    b = n
                    if stack_in.due(b - 1):
                        sp.wait_ge(stack_in.sem, stack_in.at(b - 1))
                    for i in range(PARTS):
                        if i == 0:
                            sp.wait_ge(qk_s.sem, qk_s.at(b))
                        else:
                            sp.wait_ge(split.sem, split.at(b, 1 + i))
                        for j in range(2):
                            sp.dma_start(scratch[r][j, i].rearrange("d h t -> h d t"), part[:, i, j, :])\
                                .then_inc(parts_out.sem, 16)
                    sp.wait_ge(parts_out.sem, parts_out.at(b))
                    if isinstance(n, int) and n < RING:
                        sp.wait_ge(ones_set.sem, n + 1)
                    if score_p.due(b - RING):
                        sp.wait_ge(score_p.sem, score_p.at(b - RING))
                    first = 0
                    for i in range(PARTS):
                        k = PARTS - i
                        src = scratch[r][0, i].rearrange("(o d) h t -> o d (h t)", o=1)
                        sp.dma_start(QS[r][first:first + k * HD, :, :], src.broadcast_to([k, HD, H * S])).then_inc(stack_in.sem, 16)
                        sp.dma_start(KS[r][first:first + k * HD, :, :], scratch[r][1, 0:k].rearrange("k d h t -> (k d) (h t)"))\
                            .then_inc(stack_in.sem, 16)
                        first += k * HD
                if active(n, 1):
                    b, q = n - 1, (r - 1) % RING
                    sp.wait_ge(maxT_s.sem, maxT_s.at(b))
                    sp.wait_ge(stack_in.sem, stack_in.at(b))
                    for i in range(PARTS):
                        sp.dma_start(QS[q][PAIRS + i:PAIRS + i + 1, :, :], maxT[i * H:(i + 1) * H, :])\
                            .then_inc(maxrow_in.sem, 16)
                    sp.wait_ge(maxrow_in.sem, maxrow_in.at(b))
                    steady(sp, t)

            pipeline(sp, iteration)

        @block.gpsimd
        def _(pool):
            constants(pool, t, t["w2"])

            def setup():
                pool.wait_ge(w_in.sem, w_in.at(0, 16 * 9))
                pool.tensor_scalar(bqk_s[:, :], bqk[:, :], SCALE, None, ALU.mult).then_inc(setup_done.sem, 1)
                pool.memset(zeros[:, :], 0.0).then_inc(setup_done.sem, 1)
                pool.tensor_scalar(gates_uh[:, :, :], gates_u[:, :, :], 0.5, None, ALU.mult).then_inc(setup_done.sem, 1)
                pool.tensor_scalar(gates_bh[:, :], gates_b[:, :], 0.5, None, ALU.mult).then_inc(setup_done.sem, 1)
                pool.wait_ge(setup_done.sem, 4)
                pool.tensor_scalar(state[:, :], zeros[:, :], c_start[:, 0:1], 2.0, ALU.add, ALU.mult)\
                    .then_inc(setup_done.sem, 1)

            newton = lambda root, mark, b: newton_steps(t, pool, root, mark, b)

            def iteration(n, r):
                if at(n, 0):
                    setup()
                if active(n, 0):
                    pool.wait_ge(split.sem, split.at(n, 2))
                    if parts_out.due(n - 1):
                        pool.wait_ge(parts_out.sem, parts_out.at(n - 1))
                    pool.tensor_tensor(part[:, 2, :, :], rest[:, :, :], part[:, 1, :, :], ALU.subtract).then_inc(split.sem, 1)
                if active(n, -1):
                    pool.wait_ge(seed_a.sem, seed_a.at(n + 1))
                    newton(root1[(r + 1) % RING], newton_a, n + 1)
                if active(n, 2):
                    b, q = n - 2, (r - 2) % RING
                    if x1_s.due(b - RING):
                        pool.wait_ge(x1_s.sem, x1_s.at(b - RING))
                    steady(pool, t)
                    pool.tensor_tensor(xb[q][:, :, :], X[:, bass.ds(2 * b, 2), :],
                                       bo[:, :].rearrange("p (o d) -> p o d", o=1).broadcast_to([P, TT, D]), ALU.add)\
                        .then_inc(xb_s.sem, 1)
                if active(n, 3):
                    b, q = n - 3, (r - 3) % RING
                    pool.wait_ge(seed_b.sem, seed_b.at(b))
                    newton(root2[q], newton_b, b)

            pipeline(pool, iteration)

        @block.vector
        def _(dve):
            for r in range(RING):
                dve.memset(V[r][:, :, :, :], 0.0).then_inc(t["v_set"].sem, 1)
            dve.wait_ge(t["v_set"].sem, 3)
            for r in range(RING):
                dve.memset(V[r][:, :, :, HD:HD + 1], 1.0).then_inc(t["v_set"].sem, 1)
            dve.wait_ge(t["v_set"].sem, 6)

            def layer_stats(b, stats, mv, root, st, sd, prev_norm):
                steady(dve, t)
                for i in range(TT):
                    dve.bn_stats(stats[:, i, :], X[:, 2 * b + i, :]).then_inc(st.sem, 1)
                if prev_norm.due(b - RING):
                    dve.wait_ge(prev_norm.sem, prev_norm.at(b - RING))
                for i in range(TT):
                    dve.wait_ge(st.sem, st.at(b, 1 + i))
                    steady(dve, t)
                    dve.bn_aggr(mv[:, i, :], stats[:, i, :]).then_inc(st.sem, 1)
                dve.wait_ge(st.sem, st.at(b))
                dve.tensor_scalar(root[:, 3, :], mv[:, :, 1], EPS, None, ALU.add).then_inc(sd.sem, 1)
                dve.wait_ge(sd.sem, sd.at(b, 1))
                dve.tensor_scalar(root[:, 4, :].bitcast(U32), root[:, 3, :].bitcast(U32), 1, None, ALU.logical_shift_right)\
                    .then_inc(sd.sem, 1)
                dve.wait_ge(sd.sem, sd.at(b, 2))
                dve.tensor_scalar(root[:, 0, :].bitcast(I32), root[:, 4, :].bitcast(I32), -1.0, float(MAGIC), ALU.mult, ALU.add)\
                    .then_inc(sd.sem, 1)

            def layer_norm(b, mv, root, dst, nw, nm):
                dve.wait_ge(nw.sem, nw.at(b))
                for i in range(TT):
                    dve.tensor_scalar(dst[:, i, :], X[:, 2 * b + i, :], mv[:, i, 0:1], root[:, 0, i:i + 1], ALU.subtract, ALU.mult)\
                        .then_inc(nm.sem, 1)

            def row_max(b, u):
                i, hp = u // 8, u % 8
                dve.wait_ge(max_p.sem, max_p.at(b, u + 1))
                if u == 0:
                    if msplit.due(b - 1):
                        dve.wait_ge(msplit.sem, msplit.at(b - 1))
                dve.tensor_reduce(negmax[:, i, 2 * hp:2 * hp + 2], p_max[u % 2][:, :].rearrange("p (h k) -> p h k", h=2),
                                  AX.X, ALU.max, negate=True).then_inc(max_s.sem, 1)

            def split_max(b):
                dve.wait_ge(max_s.sem, max_s.at(b))
                if maxT_p.due(b - 1):
                    dve.wait_ge(maxT_p.sem, maxT_p.at(b - 1))
                hs = [maxpart[:, :, i, :] for i in range(PARTS)]
                dve.tensor_copy(hs[0], negmax[:, :, :]).then_inc(msplit.sem, 1)
                dve.wait_ge(msplit.sem, msplit.at(b, 1))
                dve.tensor_tensor(maxrest[:, :, :], negmax[:, :, :], hs[0], ALU.subtract).then_inc(msplit.sem, 1)
                dve.wait_ge(msplit.sem, msplit.at(b, 2))
                dve.tensor_copy(hs[1], maxrest[:, :, :]).then_inc(msplit.sem, 1)
                dve.wait_ge(msplit.sem, msplit.at(b, 3))
                dve.tensor_tensor(hs[2], maxrest[:, :, :], hs[1], ALU.subtract).then_inc(msplit.sem, 2)

            def step_cell(b):
                dve.wait_ge(gfi_s.sem, gfi_s.at(b))
                if at(b, 0):
                    dve.wait_ge(setup_done.sem, 5)
                dve.scalar_tensor_tensor(out=ca[:, :], in0=gate[:, 0, :], scalar=1.0, in1=state[:, :], op0=ALU.add, op1=ALU.mult)\
                    .then_inc(cell.sem, 1)
                dve.wait_ge(gc_s.sem, gc_s.at(b))
                dve.scalar_tensor_tensor(out=cb[:, :], in0=gate[:, 1, :], scalar=1.0, in1=gate[:, 2, :], op0=ALU.add, op1=ALU.mult)\
                    .then_inc(cell.sem, 1)
                dve.wait_ge(cell.sem, cell.at(b, 2))
                dve.scalar_tensor_tensor(out=state[:, :], in0=ca[:, :], scalar=0.5, in1=cb[:, :], op0=ALU.mult, op1=ALU.add)\
                    .then_inc(cell.sem, 1)

            def quotient(b, i):
                dve.wait_ge(OQ_p.sem, OQ_p.at(b, i + 1))
                if onT_p.due(b - 1):
                    dve.wait_ge(onT_p.sem, onT_p.at(b - 1))
                heads = p_misc[:, :].rearrange("p (h c) -> p h c", c=32)
                dve.reciprocal(rz[:, i, :], heads[:, :, HD]).then_inc(rz_s.sem, 1)
                dve.wait_ge(rz_s.sem, rz_s.at(b, i + 1))
                dve.tensor_tensor(on[:, i, :].rearrange("p (h d) -> p h d", d=HD), heads[:, :, 0:HD],
                                  rz[:, i, :].rearrange("p (h o) -> p h o", o=1).broadcast_to([P, H, HD]), ALU.mult)\
                    .then_inc(on_s.sem, 1)

            def iteration(n, r):
                for i in range(3):
                    if at(n, i - 1):
                        dve.wait_ge(x_in[i].sem, 16)
                for q in range(RING):
                    if at(n, q):
                        dve.memset(KS[q][32:, :, :].bitcast(F32), TWO_ONES).then_inc(ones_set.sem, 1)
                for s in range(8):
                    units = [lambda u=u: row_max(n - 1, u) for u in MAX_AT[s]] if active(n, 1) else []
                    if s == 7 and active(n, 0):
                        units = [lambda u=u: row_max(n, u) for u in MAX_BEFORE]
                    units += [lambda: None] * (3 - len(units))
                    units[0]()
                    if s == 2 and active(n, 0):
                        dve.wait_ge(v_p.sem, v_p.at(n))
                        if pv_p.due(n - RING):
                            dve.wait_ge(pv_p.sem, pv_p.at(n - RING))
                        dve.tensor_tensor(V[r][:, :, :, 0:HD], p_misc[:, 0:S].rearrange("p (i h d) -> p i h d", i=TT, d=HD),
                                          bv[:, :].rearrange("p (o h d) -> p o h d", o=1, d=HD).broadcast_to([P, TT, H, HD]), ALU.add)\
                            .then_inc(v_s.sem, 1)
                    if s == 3 and active(n, 3):
                        quotient(n - 3, 0)
                    units[1]()
                    units[2]()
                    if s == 4 and active(n, 3):
                        b, q = n - 3, (r - 3) % RING
                        dve.wait_ge(proj_p.sem, proj_p.at(b))
                        dve.wait_ge(xb_s.sem, xb_s.at(b))
                        dve.tensor_tensor(X[:, bass.ds(2 * b, 2), :], p_misc[:, 0:S].rearrange("p (i d) -> p i d", i=TT), xb[q][:, :, :], ALU.add)\
                            .then_inc(x1_s.sem, 1)
                    if s == 5 and active(n, 1):
                        split_max(n - 1)
                    if s == 5 and active(n, 3):
                        b, q = n - 3, (r - 3) % RING
                        dve.wait_ge(x1_s.sem, x1_s.at(b))
                        layer_stats(b, stats2[q], mv2[q], root2[q], stats_b, seed_b, norm_b)
                    if s == 3 and active(n, 3):
                        quotient(n - 3, 1)
                    if s == 0 and active(n, 5):
                        step_cell(n - 5)
                    if s == 1 and active(n, -1):
                        q = (r + 1) % RING
                        layer_stats(n + 1, stats1[q], mv1[q], root1[q], stats_a, seed_a, norm_a)
                    if s == 2 and active(n, 0):
                        dve.wait_ge(qk_s.sem, qk_s.at(n))
                        if split.due(n - 1):
                            dve.wait_ge(split.sem, split.at(n - 1))
                        if parts_out.due(n - 1):
                            dve.wait_ge(parts_out.sem, parts_out.at(n - 1))
                        dve.tensor_tensor(rest[:, :, :], qk[r][:, :, :], part[:, 0, :, :], ALU.subtract).then_inc(split.sem, 1)
                        dve.wait_ge(split.sem, split.at(n, 1))
                        dve.tensor_copy(part[:, 1, :, :], rest[:, :, :]).then_inc(split.sem, 1)
                    if s == 6 and active(n, -1):
                        q = (r + 1) % RING
                        if xnT_p.due(n + 1 - RING):
                            dve.wait_ge(xnT_p.sem, xnT_p.at(n + 1 - RING))
                        layer_norm(n + 1, mv1[q], root1[q], xn1[q], newton_a, norm_a)
                    if s == 7 and active(n, 3):
                        b, q = n - 3, (r - 3) % RING
                        if xn2T_p.due(b - RING):
                            dve.wait_ge(xn2T_p.sem, xn2T_p.at(b - RING))
                        layer_norm(b, mv2[q], root2[q], xn2[q], newton_b, norm_b)

            pipeline(dve, iteration)

        @block.scalar
        def _(act):
            def iteration(n, r):
                for s in range(8):
                    if s == 0 and active(n, 0):
                        act.wait_ge(xnT_p.sem, xnT_p.at(n))
                        if v_p.due(n - RING):
                            act.wait_ge(v_p.sem, v_p.at(n - RING))
                        act.activation(xn1T[r][:, :], p_misc[:, 0:S], ACT.Copy).then_inc(xnT_s.sem, 1)
                    if s == 1 and active(n, 0):
                        act.wait_ge(qk_p.sem, qk_p.at(n))
                        if parts_out.due(n - 1):
                            act.wait_ge(parts_out.sem, parts_out.at(n - 1))
                        if split.due(n - 1):
                            act.wait_ge(split.sem, split.at(n - 1))
                        if at(n, 0):
                            act.wait_ge(setup_done.sem, 1)
                        for j, sc in enumerate((SCALE, 1.0)):
                            for dst in (qk[r][:, j, :], part[:, 0, j, :]):
                                act.activation(dst, p_misc[:, j * S:(j + 1) * S], ACT.Identity,
                                               bias=(bqk_s if j == 0 else bqk)[:, j:j + 1], scale=sc).then_inc(qk_s.sem, 1)
                    if s == 4 and active(n, 3):
                        b = n - 3
                        act.wait_ge(onT_p.sem, onT_p.at(b))
                        if proj_p.due(b - 1):
                            act.wait_ge(proj_p.sem, proj_p.at(b - 1))
                        act.activation(onT[:, :], p_misc[:, 0:S], ACT.Copy).then_inc(onT_s.sem, 1)
                    if s == 5 and active(n, 4):
                        b = n - 4
                        act.wait_ge(xn2T_p.sem, xn2T_p.at(b))
                        if gc_p.due(b - 1):
                            act.wait_ge(gc_p.sem, gc_p.at(b - 1))
                        act.activation(xn2T[:, :], p_misc[:, 0:S], ACT.Copy).then_inc(xn2T_s.sem, 1)
                        act.activation(XN2T[:, b, :], p_misc[:, 0:S], ACT.Copy).then_inc(xn2T_k.sem, 1)
                    if s == 6 and active(n, 1):
                        b = n - 1
                        act.wait_ge(maxT_p.sem, maxT_p.at(b))
                        if maxrow_in.due(b - 1):
                            act.wait_ge(maxrow_in.sem, maxrow_in.at(b - 1))
                        act.activation(maxT[:, :], p_misc[0:PARTS * H, 0:S // 2].bitcast(BF16), ACT.Copy).then_inc(maxT_s.sem, 1)
                    if s == 7 and active(n, 4):
                        b = n - 4
                        act.wait_ge(gfi_p.sem, gfi_p.at(b))
                        if cell.due(b - 1):
                            act.wait_ge(cell.sem, cell.at(b - 1))
                        for j in range(2):
                            act.activation(gate[:, j, :], p_misc[:, j * S:(j + 1) * S], ACT.Tanh, bias=gates_bh[:, j:j + 1], scale=0.5)\
                                .then_inc(gfi_s.sem, 1)
                    if active(n, 2):
                        b = n - 2
                        if score_p.due(b, s + 1):
                            act.wait_ge(score_p.sem, score_p.at(b, s + 1))
                        if pv_p.due(b, s - 1):
                            act.wait_ge(pv_p.sem, pv_p.at(b, s - 1))
                        act.activation(probs[s % 2][:, :, :].rearrange("p j q -> p (j q)"), p_exp[s % 2][:, :], ACT.Exp)\
                            .then_inc(prob_s.sem, 1)
                        if s % 2 == 0 and s > 0:
                            copy_out(n - 2, (r - 2) % RING, s // 2 - 1)
                    if s == 0 and active(n, 3):
                        copy_out(n - 3, r, 3)
                    if s == 7 and active(n, 4):
                        b = n - 4
                        act.wait_ge(gc_p.sem, gc_p.at(b))
                        act.activation(gate[:, 2, :], p_misc[:, 0:S], ACT.Tanh, bias=gates_b[:, 2:3]).then_inc(gc_s.sem, 1)

            def copy_out(b, q, g):
                act.wait_ge(pv_p.sem, pv_p.at(b, 2 * g + 2))
                if g == 0:
                    if OQ_p.due(b - RING):
                        act.wait_ge(OQ_p.sem, OQ_p.at(b - RING))
                act.activation(OT[q][:, g, :], p_out[:, 0:S], ACT.Copy).then_inc(OT_s.sem, 1)

            pipeline(act, iteration)

        @block.tensor
        def _(pe):
            def scores(b, q, s):
                g, kt = s // 2, s % 2
                if prob_s.due(b, s - 1):
                    pe.wait_ge(prob_s.sem, prob_s.at(b, s - 1))
                for j in range(4):
                    h = 4 * g + j
                    mm = pe.matmul(p_exp[s % 2][:, j * S:(j + 1) * S], KS[q][:, h, kt * P:(kt + 1) * P], QS[q][:, h, :],
                                   start=True, stop=True)
                mm.then_inc(score_p.sem, 1)

            def weigh(b, q, s):
                g, kt = s // 2, s % 2
                if prob_s.due(b, s + 1):
                    pe.wait_ge(prob_s.sem, prob_s.at(b, s + 1))
                if s == 0:
                    pe.wait_ge(v_s.sem, v_s.at(b))
                if kt == 0:
                    if OT_s.due(b, g):
                        pe.wait_ge(OT_s.sem, OT_s.at(b, g))
                for j in range(4):
                    mm = pe.matmul(p_out[32 * j:32 * j + 32, 0:S], V[q][:, kt, 4 * g + j, :], probs[s % 2][:, j, :],
                                   start=(kt == 0), stop=(kt == 1))
                mm.then_inc(pv_p.sem, 1)

            def maxima(b, q, u):
                i, hp = u // 8, u % 8
                if max_s.due(b, u - 1):
                    pe.wait_ge(max_s.sem, max_s.at(b, u - 1))
                for j in range(2):
                    h = 2 * hp + j
                    mm = pe.matmul(p_max[u % 2][:, j * S:(j + 1) * S], QS[q][0:PAIRS, h, i * P:(i + 1) * P], KS[q][0:PAIRS, h, :],
                                   start=True, stop=True)
                mm.then_inc(max_p.sem, 1)

            def turn(src, n_tiles=TT):
                for i in range(n_tiles):
                    mm = pe.transpose(p_misc[:, i * P:(i + 1) * P], src[:, i, :], ident[:, :])
                return mm

            def misc(n, r, at_slot):
                b3, b4, q3, q4 = n - 3, n - 4, (r - 3) % RING, (r - 4) % RING
                if at_slot == "0" and active(n, 0):
                    pe.wait_ge(norm_a.sem, norm_a.at(n))
                    if active(n, 5):
                        if gc_s.due(n - 5):
                            pe.wait_ge(gc_s.sem, gc_s.at(n - 5))
                    elif active(n, 2):
                        if maxT_s.due(n - 2):
                            pe.wait_ge(maxT_s.sem, maxT_s.at(n - 2))
                    elif active(n, 1):
                        if v_s.due(n - 1):
                            pe.wait_ge(v_s.sem, v_s.at(n - 1))
                    turn(xn1[r]).then_inc(xnT_p.sem, 1)
                if at_slot == "1" and active(n, 0):
                    pe.wait_ge(xnT_s.sem, xnT_s.at(n))
                    for j in range(2):
                        mm = pe.matmul(p_misc[:, j * S:(j + 1) * S], Wqkv[:, j * D:(j + 1) * D], xn1T[r][:, :], start=True, stop=True)
                    mm.then_inc(qk_p.sem, 1)
                if at_slot == "2" and active(n, 0):
                    pe.wait_ge(qk_s.sem, qk_s.at(n))
                    for i in range(TT):
                        mm = pe.matmul(p_misc[:, i * P:(i + 1) * P], xn1T[r][:, i * P:(i + 1) * P], Wqkv[:, 2 * D:3 * D], start=True, stop=True)
                    mm.then_inc(v_p.sem, 1)
                if at_slot in ("3", "3b") and active(n, 3):
                    i = ("3", "3b").index(at_slot)
                    if i:
                        pe.wait_ge(on_s.sem, on_s.at(b3, 1))
                    else:
                        pe.wait_ge(OT_s.sem, OT_s.at(b3))
                        if active(n, 0):
                            pe.wait_ge(v_s.sem, v_s.at(n))
                        elif active(n, 5):
                            if gc_s.due(n - 5):
                                pe.wait_ge(gc_s.sem, gc_s.at(n - 5))
                    for g in range(NG):
                        mm = pe.transpose(p_misc[:, g * P:(g + 1) * P], OT[q3][:, g, i * P:(i + 1) * P], ident[:, :])
                    mm.then_inc(OQ_p.sem, 1)
                if at_slot == "4" and active(n, 3):
                    pe.wait_ge(on_s.sem, on_s.at(b3))
                    turn(on).then_inc(onT_p.sem, 1)
                if at_slot == "4b" and active(n, 3):
                    pe.wait_ge(onT_s.sem, onT_s.at(b3))
                    for i in range(TT):
                        mm = pe.matmul(p_misc[:, i * P:(i + 1) * P], onT[:, i * P:(i + 1) * P], Wout[:, :], start=True, stop=True)
                    mm.then_inc(proj_p.sem, 1)
                if at_slot == "5" and active(n, 4):
                    pe.wait_ge(norm_b.sem, norm_b.at(b4))
                    if active(n, 3):
                        pe.wait_ge(x1_s.sem, x1_s.at(b3))
                    else:
                        if gc_s.due(n - 5):
                            pe.wait_ge(gc_s.sem, gc_s.at(n - 5))
                    turn(xn2[q4]).then_inc(xn2T_p.sem, 1)
                if at_slot == "6" and active(n, 1):
                    if msplit.due(n - 1):
                        pe.wait_ge(msplit.sem, msplit.at(n - 1))
                    if active(n, 4):
                        pe.wait_ge(xn2T_s.sem, xn2T_s.at(b4))
                        pe.wait_ge(xn2T_k.sem, xn2T_k.at(b4))
                    elif active(n, 3):
                        pe.wait_ge(x1_s.sem, x1_s.at(b3))
                    else:
                        pe.wait_ge(v_s.sem, v_s.at(n))
                    steady(pe, t)
                    for i in range(TT):
                        mm = pe.transpose(p_misc[0:PARTS * H, i * P // 2:(i + 1) * P // 2].bitcast(BF16),
                                          maxpart[:, i, :, :].rearrange("p k h -> p (k h)"), ident16[:, :])
                    mm.then_inc(maxT_p.sem, 1)
                if at_slot == "6b" and active(n, 4):
                    pe.wait_ge(xn2T_s.sem, xn2T_s.at(b4))
                    pe.wait_ge(xn2T_k.sem, xn2T_k.at(b4))
                    if active(n, 1):
                        pe.wait_ge(maxT_s.sem, maxT_s.at(n - 1))
                    if cell.due(b4 - 1):
                        pe.wait_ge(cell.sem, cell.at(b4 - 1))
                    for j in range(2):
                        pe.matmul(p_misc[:, j * S:(j + 1) * S], gates_w[:, j, :], xn2T[:, :], start=True, stop=False)
                        mm = pe.matmul(p_misc[:, j * S:(j + 1) * S], gates_uh[:, j, :], state[:, :], start=False, stop=True)
                    mm.then_inc(gfi_p.sem, 1)
                if at_slot == "7b" and active(n, 4):
                    pe.wait_ge(gfi_s.sem, gfi_s.at(b4))
                    pe.matmul(p_misc[:, 0:S], gates_w[:, 2, :], xn2T[:, :], start=True, stop=False)
                    pe.matmul(p_misc[:, 0:S], gates_uh[:, 2, :], state[:, :], start=False, stop=True).then_inc(gc_p.sem, 1)

            def iteration(n, r):
                q1, q2 = (r - 1) % RING, (r - 2) % RING
                if at(n, -1):
                    pe.wait_ge(w_in.sem, w_in.at(0, 16 * 9))
                    pe.wait_ge(consts.sem, t["n_consts"])
                if at(n, 1):
                    pe.wait_ge(setup_done.sem, 5)
                    pe.wait_ge(t["v_set"].sem, 6)
                for s in range(8):
                    units = [lambda u=u: maxima(n - 1, q1, u) for u in MAX_AT[s]] if active(n, 1) else []
                    if s == 7 and active(n, 0):
                        pe.wait_ge(stack_in.sem, stack_in.at(n))
                        units = [lambda u=u: maxima(n, r, u) for u in MAX_BEFORE]
                    units += [lambda: None] * (3 - len(units))
                    units[0]()
                    if active(n, 2):
                        if s == 0:
                            if maxrow_in.due(n - 2):
                                pe.wait_ge(maxrow_in.sem, maxrow_in.at(n - 2))
                        scores(n - 2, q2, s)
                    misc(n, r, str(s))
                    units[1]()
                    if s == 0 and active(n, 3):
                        weigh(n - 3, r, 7)
                    if s and active(n, 2):
                        weigh(n - 2, q2, s - 1)
                    units[2]()
                    misc(n, r, str(s) + "b")

            pipeline(pe, iteration)


E = 16
HID = 256
TOP = 2
TOKENS = B * S
REGION = TOKENS + P
TILES = 80
ROW = D + 2
NOWHERE = float(4 * TOKENS)
PAIR = 2
Z2 = 3 * D


def linear_attention_and_routing(nc, ctx, t):

    def sig(name, per=1):
        return Signal(nc, ctx, name, per)

    with ExitStack() as scope:
        def psum(name, cols=512):
            return scope.enter_context(nc.psum_tensor(name, [P, cols], F32))

        def tmp(name, shape, dt=F32):
            return scope.enter_context(nc.sbuf_tensor(name, shape, dt))

        X, XN2T, state, ident = t["X"], t["XN2T"], t["state"], t["ident"]
        w = t["w2"]
        count = t["count"]
        disp = t["disp"]

        UC = tmp("UC", [P, S])
        uoh = tmp("uoh", [P, D])
        KVones = [tmp(f"KVones_{r}", [P, TT, D + H]) for r in range(PAIR)]
        zs = [tmp(f"zs_{r}", [P, S]) for r in range(PAIR)]
        hT = [tmp(f"hT_{r}", [P, S]) for r in range(PAIR)]
        stats3, stats4 = [tmp(f"stats3_{r}", [P, TT, 6]) for r in range(PAIR)], [tmp(f"stats4_{r}", [P, TT, 6]) for r in range(PAIR)]
        mv, root = [tmp(f"mv_{r}", [P, 2 * TT, 2]) for r in range(PAIR)], [tmp(f"root_{r}", [P, 4, 2 * TT]) for r in range(PAIR)]
        xn3 = [tmp(f"xn3_{r}", [P, TT, D]) for r in range(PAIR)]
        xn3T = [tmp(f"xn3T_{r}", [P, S]) for r in range(PAIR)]
        t1, t2 = tmp("t1", [P, TT, 2 * D]), tmp("t2", [P, TT, 2 * D])
        rot = [tmp(f"rot_{r}", [P, TT, 2 * D]) for r in range(PAIR)]
        ex, rl = tmp("ex", [P, TT, 2 * D]), tmp("rl", [P, TT, 2 * D])
        feat = [tmp(f"feat_{r}", [P, TT, 2 * D]) for r in range(PAIR)]
        KVm = tmp("KVm", [P, D + H])
        qfT = tmp("qfT", [P, S])
        den, on3, on3T = tmp("den", [P, TT, H]), tmp("on3", [P, TT, D]), tmp("on3T", [P, S])
        pay = [tmp(f"pay_{r}", [P, TOP, TT, ROW]) for r in range(PAIR)]
        xn4T = tmp("xn4T", [P, S])
        negtop, probs4, sums, z = tmp("negtop", [P, TT]), tmp("probs4", [P, TT, E]), tmp("sums", [P, TT]), tmp("z", [P, TT])
        best = tmp("best", [P, TT, 8])
        where = tmp("where", [P, TT, 8], U32)
        wheref = tmp("wheref", [P, TT, TOP])
        hot = [tmp(f"hot_{r}", [P, TT, TOP, E]) for r in range(PAIR)]
        sel = [tmp(f"sel_{r}", [P, TT, E], BF16) for r in range(PAIR)]
        place, mine, posf = tmp("place", [P, TT, E]), tmp("mine", [P, TT, TOP, E]), tmp("posf", [P, TT, TOP])
        pos = [tmp(f"pos_{r}", [P, TT, TOP], U32) for r in range(PAIR)]
        nup = [count, tmp("count_b", [P, E])]

        p_h, p_ta, p_tb, p_qkv = psum("p_h"), psum("p_ta"), psum("p_tb"), psum("p_qkv", 1024)
        p_kvo, p_u, p_r = psum("p_kvo"), psum("p_u"), psum("p_r")

        uc_ready = sig("uc_ready", 2)
        s2 = sig("setup2")
        z_p, z_s, h_s, hT_p, x2_s = sig("z_p"), sig("z_s"), sig("h_s"), sig("hT_p"), sig("x2_s")
        st3, sd, nw, nm3 = sig("st3", 4), sig("sd", 3), sig("nw", 3 * NEWTON + 1), sig("nm3", 2)
        x3T_p, x3T_s, qkv_p = sig("x3T_p"), sig("x3T_s"), sig("qkv_p")
        v3_s, t_s, rot_s, el_s, feat_s = sig("v3_s"), sig("t_s", 3), sig("rot_s"), sig("el_s", 2), sig("feat_s")
        kv_p, kv_s, qfT_p, qfT_s, o_p = sig("kv_p"), sig("kv_s"), sig("qfT_p"), sig("qfT_s"), sig("o_p")
        o_s, onT3_p, onT3_s, u_p, x3_s = sig("o_s", 3), sig("onT3_p"), sig("onT3_s"), sig("u_p"), sig("x3_s")
        st4, nm4, res, mv_set = sig("st4", 4), sig("nm4", 2), sig("res"), sig("mv_set")
        x4T_p, x4T_s, lg_p, lg_s, ex4_s = sig("x4T_p"), sig("x4T_s"), sig("lg_p"), sig("lg_s"), sig("ex4_s", TT)
        pr_s, top_s, hot_s, pay_s = sig("pr_s", 2), sig("top_s", 4), sig("hot_s", 2), sig("pay_s", 3)
        rank_p, pos_s, sent = sig("rank_p"), sig("pos_s", 5), sig("sent", 16 * TT * TOP)
        t["pos_s"], t["sent"], t["res"], t["rank_p"] = pos_s, sent, res, rank_p
        sel_s, gate_in, ids_up = sig("sel_s"), sig("gate_in"), sig("ids_up")

        LAST, PEEL = B + 5, 7

        def active(n, lag):
            return not isinstance(n, int) or 0 <= n - lag < B

        def at(n, first):
            return isinstance(n, int) and n == first

        def pipeline(eng, iteration):
            for n in range(PEEL):
                iteration(n, n % PAIR)
            with eng.Fori(0, (B - 1 - PEEL) // PAIR, 1) as k:
                for c in range(PAIR):
                    iteration(k * PAIR + (PEEL + c), (PEEL + c) % PAIR)
            for n in range(B - 1, LAST):
                iteration(n, n % PAIR)

        block = scope.enter_context(nc.Block())

        @block.sync
        def _(sp):
            for dst, src in t["w3_loads"]:
                sp.dma_start(dst[tuple(slice(None) for _ in dst.shape)], src).then_inc(w["loaded3"].sem, 16)

        @block.gpsimd
        def _(pool):
            pool.wait_ge(w["loaded"].sem, w["loaded"].at(0))
            pool.tensor_scalar(uoh[:, :], w["uo"][:, :], 0.5, None, ALU.mult).then_inc(s2.sem, 1)
            for r in range(PAIR):
                pool.memset(KVones[r][:, :, D:D + H], 1.0).then_inc(s2.sem, 1)
            for r in range(PAIR):
                pool.iota(pay[r][:, :, :, D + 1], pattern=[[1, TOP], [2 * P, TT]], base=r * TOP * S, channel_multiplier=2,
                          allow_small_or_imprecise_dtypes=True).then_inc(s2.sem, 1)

            def iteration(n, r):
                o = 1 - r
                if active(n, 5):
                    b = n - 5
                    pool.wait_ge(pos_s.sem, pos_s.at(b))
                    if ids_up.due(b - PAIR, 1):
                        pool.wait_ge(ids_up.sem, ids_up.at(b - PAIR))
                    pool.wait_ge(gate_in.sem, gate_in.at(b))
                    pool.wait_ge(nm4.sem, nm4.at(b))
                    if sent.due(b - 1):
                        pool.wait_ge(sent.sem, sent.at(b - 1))
                    steady(pool, t)
                    for i in range(TT):
                        for k in range(TOP):
                            pool.indirect_dma_start(out=disp, out_offset=bass.IndirectOffsetOnAxis(ap=pos[o][:, i, k:k + 1], axis=0),
                                                    in_=pay[o][:, k, i, :], in_offset=None).then_inc(sent.sem, 16)
                if active(n, 4) and not (isinstance(n, int) and n - 4 < PAIR):
                    b = n - 4
                    pool.wait_ge(sent.sem, sent.at(b - PAIR))
                    steady(pool, t)
                    pool.tensor_scalar(pay[r][:, :, :, D + 1], pay[r][:, :, :, D + 1], float(PAIR * TOP * S), None, ALU.add)\
                        .then_inc(ids_up.sem, 1)
                if active(n, 4):
                    b = n - 4
                    pool.wait_ge(nm4.sem, nm4.at(b))
                    steady(pool, t)
                    pool.tensor_tensor(X[:, bass.ds(2 * b, 2), :], X[:, bass.ds(2 * b, 2), :], pay[r][:, 0, :, 0:D], ALU.add)\
                        .then_inc(res.sem, 1)
                if active(n, 1):
                    b = n - 1
                    pool.wait_ge(t_s.sem, t_s.at(b))
                    if el_s.due(b - PAIR):
                        pool.wait_ge(el_s.sem, el_s.at(b - PAIR))
                    pool.tensor_tensor(rot[o][:, :, :], t1[:, :, :], t2[:, :, :], ALU.add).then_inc(rot_s.sem, 1)

            pipeline(pool, iteration)

        @block.vector
        def _(dve):
            def root_step(m, r, step):
                if not (active(m, 0) or active(m, 3)):
                    return
                y, u, shift, v = (root[r][:, j, :] for j in range(4))
                newton = step - 3
                if step == 0:
                    if active(m, 0):
                        dve.wait_ge(st3.sem, st3.at(m))
                    if active(m, 3):
                        dve.wait_ge(st4.sem, st4.at(m - 3))
                    if active(m, PAIR):
                        dve.wait_ge(nm3.sem, nm3.at(m - PAIR))
                    if nm4.due(m - 3 - PAIR):
                        dve.wait_ge(nm4.sem, nm4.at(m - 3 - PAIR))
                    dve.tensor_scalar(v, mv[r][:, :, 1], EPS, None, ALU.add).then_inc(sd.sem, 1)
                elif step == 1:
                    dve.wait_ge(sd.sem, sd.at(m, 1))
                    dve.tensor_scalar(u.bitcast(U32), v.bitcast(U32), 1, None, ALU.logical_shift_right).then_inc(sd.sem, 1)
                elif step == 2:
                    dve.wait_ge(sd.sem, sd.at(m, 2))
                    dve.tensor_scalar(y.bitcast(I32), u.bitcast(I32), -1.0, float(MAGIC), ALU.mult, ALU.add).then_inc(sd.sem, 1)
                elif newton < 3 * NEWTON:
                    if newton:
                        dve.wait_ge(nw.sem, nw.at(m, newton))
                    else:
                        dve.wait_ge(sd.sem, sd.at(m))
                    if newton % 3 == 0:
                        dve.tensor_tensor(u, y, y, ALU.mult).then_inc(nw.sem, 1)
                    elif newton % 3 == 1:
                        dve.scalar_tensor_tensor(out=u, in0=u, scalar=-0.5, in1=v, op0=ALU.mult, op1=ALU.mult).then_inc(nw.sem, 1)
                    else:
                        dve.scalar_tensor_tensor(out=y, in0=u, scalar=1.5, in1=y, op0=ALU.add, op1=ALU.mult).then_inc(nw.sem, 1)
                else:
                    dve.wait_ge(nw.sem, nw.at(m, 3 * NEWTON))
                    dve.scalar_tensor_tensor(out=shift, in0=mv[r][:, :, 0], scalar=-1.0, in1=y, op0=ALU.mult, op1=ALU.mult).then_inc(nw.sem, 1)

            def wide(ap, shape):
                return ap.broadcast_to(shape)

            def iteration(n, r):
                o = 1 - r
                outs = p_kvo[:, :].rearrange("p (i c) -> p i c", i=TT)
                three, four = slice(0, TT), slice(TT, 2 * TT)
                if at(n, 0):
                    dve.wait_ge(uc_ready.sem, 2)
                    for q in range(PAIR):
                        dve.memset(mv[q][:, :, :], 1.0).then_inc(mv_set.sem, 1)
                    dve.wait_ge(mv_set.sem, PAIR)
                if active(n, 0):
                    dve.wait_ge(z_p.sem, z_p.at(n))
                    if h_s.due(n - PAIR):
                        dve.wait_ge(h_s.sem, h_s.at(n - PAIR))
                    dve.tensor_tensor(zs[r][:, :], p_h[:, 0:S], UC[:, :], ALU.add).then_inc(z_s.sem, 1)
                if active(n, 5):
                    b = n - 5
                    cur, nxt = nup[o], nup[r]
                    dve.wait_ge(rank_p.sem, rank_p.at(b))
                    if at(n, 5):
                        dve.wait_ge(t["count_set"].sem, 2)
                    ranks = p_r[:, 64:64 + TT * E].rearrange("p (i e) -> p i e", i=TT)
                    dve.tensor_tensor(place[:, :, :], ranks, wide(cur[:, :].rearrange("p (o e) -> p o e", o=1), [P, TT, E]), ALU.add)\
                        .then_inc(pos_s.sem, 1)
                    dve.tensor_tensor(nxt[:, :], p_r[:, 96:96 + E], cur[:, :], ALU.add).then_inc(pos_s.sem, 1)
                if active(n, 5):
                    b = n - 5
                    dve.wait_ge(pos_s.sem, pos_s.at(b, 2))
                    dve.tensor_tensor(mine[:, :, :, :], hot[o][:, :, :, :],
                                      wide(place[:, :, :].rearrange("p i (o e) -> p i o e", o=1), [P, TT, TOP, E]), ALU.mult).then_inc(pos_s.sem, 1)
                if active(n, 5):
                    b = n - 5
                    dve.wait_ge(pos_s.sem, pos_s.at(b, 3))
                    dve.tensor_reduce(posf[:, :, :], mine[:, :, :, :], AX.X, ALU.add).then_inc(pos_s.sem, 1)
                if active(n, 0):
                    dve.wait_ge(hT_p.sem, hT_p.at(n))
                    dve.tensor_tensor(X[:, bass.ds(2 * n, 2), :], p_h[:, 0:S].rearrange("p (i d) -> p i d", i=TT), X[:, bass.ds(2 * n, 2), :], ALU.add)\
                        .then_inc(x2_s.sem, 1)
                if active(n, 3):
                    b = n - 3
                    dve.wait_ge(u_p.sem, u_p.at(b))
                    dve.wait_ge(nm3.sem, nm3.at(b))
                    dve.tensor_tensor(X[:, bass.ds(2 * b, 2), :], p_u[:, 0:S].rearrange("p (i d) -> p i d", i=TT), X[:, bass.ds(2 * b, 2), :], ALU.add)\
                        .then_inc(x3_s.sem, 1)
                if active(n, 5):
                    b = n - 5
                    dve.wait_ge(pos_s.sem, pos_s.at(b, 4))
                    dve.tensor_copy(pos[o][:, :, :], posf[:, :, :]).then_inc(pos_s.sem, 1)
                if active(n, 0):
                    dve.wait_ge(x2_s.sem, x2_s.at(n))
                    steady(dve, t)
                    for i in range(TT):
                        dve.bn_stats(stats3[r][:, i, :], X[:, 2 * n + i, :]).then_inc(st3.sem, 1)
                if active(n, 3):
                    b = n - 3
                    dve.wait_ge(x3_s.sem, x3_s.at(b))
                    steady(dve, t)
                    for i in range(TT):
                        dve.bn_stats(stats4[o][:, i, :], X[:, 2 * b + i, :]).then_inc(st4.sem, 1)
                if active(n, 0):
                    dve.wait_ge(st3.sem, st3.at(n, 2))
                    if nw.due(n - PAIR):
                        dve.wait_ge(nw.sem, nw.at(n - PAIR))
                    steady(dve, t)
                    for i in range(TT):
                        dve.bn_aggr(mv[r][:, i, :], stats3[r][:, i, :]).then_inc(st3.sem, 1)
                if active(n, 3):
                    b = n - 3
                    dve.wait_ge(st4.sem, st4.at(b, 2))
                    if nm4.due(b - PAIR):
                        dve.wait_ge(nm4.sem, nm4.at(b - PAIR))
                    steady(dve, t)
                    for i in range(TT):
                        dve.bn_aggr(mv[r][:, TT + i, :], stats4[o][:, i, :]).then_inc(st4.sem, 1)
                root_step(n, r, 0)
                if active(n, 2):
                    b = n - 2
                    dve.wait_ge(el_s.sem, el_s.at(b))
                    if qfT_p.due(b - PAIR):
                        dve.wait_ge(qfT_p.sem, qfT_p.at(b - PAIR))
                    dve.scalar_tensor_tensor(out=feat[r][:, :, :], in0=ex[:, :, :], scalar=1.0, in1=rl[:, :, :], op0=ALU.min, op1=ALU.add)\
                        .then_inc(feat_s.sem, 1)
                root_step(n, r, 1)
                root_step(n, r, 2)
                root_step(n, r, 3)
                if active(n, 1):
                    b = n - 1
                    dve.wait_ge(qkv_p.sem, qkv_p.at(b))
                    if rot_s.due(b - 1):
                        dve.wait_ge(rot_s.sem, rot_s.at(b - 1))
                    qkp = p_qkv[:, :].rearrange("p (i c) -> p i c", i=TT)[:, :, 0:2 * D]
                    dve.tensor_tensor(t1[:, :, :], qkp, w["cosf"][:, :, :], ALU.mult).then_inc(t_s.sem, 1)
                root_step(n, r, 4)
                if active(n, 1):
                    qkp = p_qkv[:, :].rearrange("p (i c) -> p i c", i=TT)[:, :, 0:2 * D]
                    halves = [x.rearrange("p i (g a d) -> p i g a d", a=2, d=HD // 2) for x in (qkp, t2[:, :, :], w["sinf"][:, :, :])]
                    dve.tensor_tensor(halves[1][:, :, :, 0, :], halves[0][:, :, :, 1, :], halves[2][:, :, :, 0, :], ALU.mult)\
                        .then_inc(t_s.sem, 1)
                root_step(n, r, 5)
                if active(n, 1):
                    qkp = p_qkv[:, :].rearrange("p (i c) -> p i c", i=TT)[:, :, 0:2 * D]
                    halves = [x.rearrange("p i (g a d) -> p i g a d", a=2, d=HD // 2) for x in (qkp, t2[:, :, :], w["sinf"][:, :, :])]
                    dve.tensor_tensor(halves[1][:, :, :, 1, :], halves[0][:, :, :, 0, :], halves[2][:, :, :, 1, :], ALU.mult)\
                        .then_inc(t_s.sem, 1)
                root_step(n, r, 6)
                if active(n, 4):
                    b = n - 4
                    dve.wait_ge(lg_p.sem, lg_p.at(b))
                    if ex4_s.due(b - 1):
                        dve.wait_ge(ex4_s.sem, ex4_s.at(b - 1))
                    dve.tensor_reduce(negtop[:, :], p_r[:, 0:TT * E].rearrange("p (i e) -> p i e", i=TT), AX.X, ALU.max, negate=True)\
                        .then_inc(lg_s.sem, 1)
                root_step(n, r, 7)
                if active(n, 2):
                    b = n - 2
                    dve.wait_ge(kv_p.sem, kv_p.at(b))
                    if o_p.due(b - 1):
                        dve.wait_ge(o_p.sem, o_p.at(b - 1))
                    dve.tensor_tensor(KVm[:, :], p_kvo[:, 0:D + H], w["kv_mask"][:, :], ALU.mult).then_inc(kv_s.sem, 1)
                root_step(n, r, 8)
                if active(n, 4):
                    b = n - 4
                    dve.wait_ge(ex4_s.sem, ex4_s.at(b))
                    dve.reciprocal(sums[:, :], sums[:, :]).then_inc(pr_s.sem, 1)
                root_step(n, r, 9)
                if active(n, 4):
                    b = n - 4
                    dve.wait_ge(pr_s.sem, pr_s.at(b, 1))
                    dve.tensor_tensor(probs4[:, :, :], probs4[:, :, :], wide(sums[:, :].rearrange("p (i o) -> p i o", o=1), [P, TT, E]), ALU.mult)\
                        .then_inc(pr_s.sem, 1)
                root_step(n, r, 10)
                if active(n, 4):
                    b = n - 4
                    dve.wait_ge(pr_s.sem, pr_s.at(b))
                    steady(dve, t)
                    for i in range(TT):
                        dve.max(best[:, i, :], probs4[:, i, :]).then_inc(top_s.sem, 1)
                root_step(n, r, 11)
                if active(n, 4):
                    b = n - 4
                    for i in range(TT):
                        dve.wait_ge(top_s.sem, top_s.at(b, 1 + i))
                        steady(dve, t)
                        dve.max_index(where[:, i, :], best[:, i, :], probs4[:, i, :]).then_inc(top_s.sem, 1)
                root_step(n, r, 12)
                if active(n, 4):
                    b = n - 4
                    if sent.due(b - PAIR):
                        dve.wait_ge(sent.sem, sent.at(b - PAIR))
                    dve.tensor_tensor(z[:, :], best[:, :, 0], best[:, :, 1], ALU.add).then_inc(pay_s.sem, 1)
                if active(n, 2):
                    b = n - 2
                    dve.wait_ge(o_p.sem, o_p.at(b))
                    if onT3_p.due(b - 1):
                        dve.wait_ge(onT3_p.sem, onT3_p.at(b - 1))
                    dve.tensor_scalar(den[:, :, :], outs[:, :, D:D + H], 1e-6, None, ALU.max).then_inc(o_s.sem, 1)
                if active(n, 4):
                    b = n - 4
                    dve.wait_ge(top_s.sem, top_s.at(b))
                    dve.tensor_copy(wheref[:, :, :], where[:, :, 0:TOP]).then_inc(hot_s.sem, 1)
                if active(n, 2):
                    b = n - 2
                    dve.wait_ge(o_s.sem, o_s.at(b, 1))
                    dve.reciprocal(den[:, :, :], den[:, :, :]).then_inc(o_s.sem, 1)
                if active(n, 4):
                    b = n - 4
                    dve.wait_ge(pay_s.sem, pay_s.at(b, 1))
                    dve.tensor_scalar(z[:, :], z[:, :], 1e-9, None, ALU.max).then_inc(pay_s.sem, 1)
                if active(n, 4):
                    b = n - 4
                    dve.wait_ge(hot_s.sem, hot_s.at(b, 1))
                    dve.tensor_tensor(hot[r][:, :, :, :], wide(w["iota_e"][:, :].rearrange("p (a o e) -> p a o e", a=1, o=1), [P, TT, TOP, E]),
                                      wide(wheref[:, :, :].rearrange("p i (k o) -> p i k o", o=1), [P, TT, TOP, E]), ALU.is_equal)\
                        .then_inc(hot_s.sem, 1)
                if active(n, 2):
                    b = n - 2
                    dve.wait_ge(o_s.sem, o_s.at(b, 2))
                    dve.tensor_tensor(on3[:, :, :].rearrange("p i (h d) -> p i h d", d=HD), outs[:, :, 0:D].rearrange("p i (h d) -> p i h d", d=HD),
                                      wide(den[:, :, :].rearrange("p i (h o) -> p i h o", o=1), [P, TT, H, HD]), ALU.mult).then_inc(o_s.sem, 1)
                if active(n, 4):
                    b = n - 4
                    dve.wait_ge(pay_s.sem, pay_s.at(b, 2))
                    dve.reciprocal(z[:, :], z[:, :]).then_inc(pay_s.sem, 1)
                if active(n, 4):
                    b = n - 4
                    dve.wait_ge(hot_s.sem, hot_s.at(b))
                    if rank_p.due(b - PAIR):
                        dve.wait_ge(rank_p.sem, rank_p.at(b - PAIR))
                    dve.tensor_tensor(sel[r][:, :, :], hot[r][:, :, 0, :], hot[r][:, :, 1, :], ALU.add).then_inc(sel_s.sem, 1)
                if active(n, 4):
                    b = n - 4
                    dve.wait_ge(pay_s.sem, pay_s.at(b, 3))
                    dve.tensor_tensor(pay[r][:, :, :, D], best[:, :, 0:TOP].rearrange("p i k -> p k i"),
                                      wide(z[:, :].rearrange("p (o i) -> p o i", o=1), [P, TOP, TT]), ALU.mult).then_inc(gate_in.sem, 1)

            pipeline(dve, iteration)

        @block.scalar
        def _(act):
            act.wait_ge(uc_ready.sem, 1)
            act.activation(UC[:, :], p_u[:, 0:S], ACT.Identity, bias=w["bo"][:, 0:1]).then_inc(uc_ready.sem, 1)

            def iteration(n, r):
                o = 1 - r
                if active(n, 1):
                    b = n - 1
                    act.wait_ge(nw.sem, nw.at(b))
                    act.wait_ge(x2_s.sem, x2_s.at(b))
                    if x3T_p.due(b - PAIR):
                        act.wait_ge(x3T_p.sem, x3T_p.at(b - PAIR))
                    for i in range(TT):
                        act.activation(xn3[o][:, i, :], X[:, 2 * b + i, :], ACT.Identity, bias=root[o][:, 2, i:i + 1],
                                       scale=root[o][:, 0, i:i + 1]).then_inc(nm3.sem, 1)
                if active(n, 0):
                    act.wait_ge(z_s.sem, z_s.at(n))
                    if hT_p.due(n - PAIR):
                        act.wait_ge(hT_p.sem, hT_p.at(n - PAIR))
                    act.activation(hT[r][:, :], zs[r][:, :], ACT.Tanh).then_inc(h_s.sem, 1)
                if active(n, 3):
                    b = n - 3
                    act.wait_ge(onT3_p.sem, onT3_p.at(b))
                    if u_p.due(b - 1):
                        act.wait_ge(u_p.sem, u_p.at(b - 1))
                    act.activation(on3T[:, :], p_tb[:, 0:S], ACT.Copy).then_inc(onT3_s.sem, 1)
                if active(n, 1):
                    b = n - 1
                    act.wait_ge(x3T_p.sem, x3T_p.at(b))
                    if qkv_p.due(b - PAIR):
                        act.wait_ge(qkv_p.sem, qkv_p.at(b - PAIR))
                    act.activation(xn3T[o][:, :], p_ta[:, 0:S], ACT.Copy).then_inc(x3T_s.sem, 1)
                if active(n, 2):
                    b = n - 2
                    act.wait_ge(rot_s.sem, rot_s.at(b))
                    if feat_s.due(b - 1):
                        act.wait_ge(feat_s.sem, feat_s.at(b - 1))
                    act.activation(ex[:, :, :], rot[r][:, :, :], ACT.Exp).then_inc(el_s.sem, 1)
                    act.activation(rl[:, :, :], rot[r][:, :, :], ACT.Relu).then_inc(el_s.sem, 1)
                if active(n, 4):
                    b = n - 4
                    act.wait_ge(nw.sem, nw.at(n - 1))
                    if sent.due(b - PAIR):
                        act.wait_ge(sent.sem, sent.at(b - PAIR))
                    if res.due(b - PAIR):
                        act.wait_ge(res.sem, res.at(b - PAIR))
                    for i in range(TT):
                        act.activation(pay[r][:, :, i, 0:D], X[:, bass.ds(2 * b + i, 1), :].broadcast_to([P, TOP, D]), ACT.Identity,
                                       bias=root[o][:, 2, TT + i:TT + i + 1], scale=root[o][:, 0, TT + i:TT + i + 1]).then_inc(nm4.sem, 1)
                if active(n, 4):
                    b = n - 4
                    act.wait_ge(x4T_p.sem, x4T_p.at(b))
                    if lg_p.due(b - 1):
                        act.wait_ge(lg_p.sem, lg_p.at(b - 1))
                    act.activation(xn4T[:, :], p_tb[:, 0:S], ACT.Copy).then_inc(x4T_s.sem, 1)
                if active(n, 4):
                    b = n - 4
                    act.wait_ge(lg_s.sem, lg_s.at(b))
                    if top_s.due(b - 1):
                        act.wait_ge(top_s.sem, top_s.at(b - 1))
                    for i in range(TT):
                        act.activation(probs4[:, i, :], p_r[:, i * E:(i + 1) * E], ACT.Exp, bias=negtop[:, i:i + 1], accum_out=sums[:, i:i + 1])\
                            .then_inc(ex4_s.sem, 1)
                if active(n, 1):
                    b = n - 1
                    act.wait_ge(qkv_p.sem, qkv_p.at(b))
                    act.wait_ge(t_s.sem, t_s.at(b))
                    if kv_p.due(b - PAIR):
                        act.wait_ge(kv_p.sem, kv_p.at(b - PAIR))
                    if at(n, 1):
                        act.wait_ge(s2.sem, 5)
                    act.activation(KVones[o][:, :, 0:D], p_qkv[:, :].rearrange("p (i c) -> p i c", i=TT)[:, :, 2 * D:3 * D], ACT.Copy)\
                        .then_inc(v3_s.sem, 1)
                if active(n, 2):
                    act.wait_ge(qfT_p.sem, qfT_p.at(n - 2))
                    if o_p.due(n - 3):
                        act.wait_ge(o_p.sem, o_p.at(n - 3))
                    act.activation(qfT[:, :], p_ta[:, 0:S], ACT.Copy).then_inc(qfT_s.sem, 1)

            pipeline(act, iteration)

        @block.tensor
        def _(pe):
            if t["cell"].due(B - 1):
                pe.wait_ge(t["cell"].sem, t["cell"].at(B - 1))
            pe.wait_ge(s2.sem, 5)
            pe.wait_ge(w["loaded"].sem, w["loaded"].at(0))
            pe.matmul(p_u[:, 0:S], uoh[:, :], state[:, :], start=True, stop=True).then_inc(uc_ready.sem, 1)
            pe.wait_ge(uc_ready.sem, 2)
            pe.matmul(p_h[:, 0:S], w["wo"][:, :], XN2T[:, 0, :], start=True, stop=True).then_inc(z_p.sem, 1)

            def turn(dst, src):
                for i in range(TT):
                    mm = pe.transpose(dst[:, i * P:(i + 1) * P], src[:, i, 0:P], ident[:, :])
                return mm

            def iteration(n, r):
                o = 1 - r
                if active(n, 3):
                    b = n - 3
                    pe.wait_ge(o_s.sem, o_s.at(b))
                    if active(n, 5):
                        pe.wait_ge(x4T_s.sem, x4T_s.at(n - 5))
                    turn(p_tb, on3).then_inc(onT3_p.sem, 1)
                if active(n, 1):
                    b = n - 1
                    pe.wait_ge(nm3.sem, nm3.at(b))
                    if active(n, 3):
                        pe.wait_ge(qfT_s.sem, qfT_s.at(n - 3))
                    turn(p_ta, xn3[o]).then_inc(x3T_p.sem, 1)
                if active(n, 0):
                    pe.wait_ge(h_s.sem, h_s.at(n))
                    pe.wait_ge(z_s.sem, z_s.at(n))
                    turn(p_h, hT[r][:, :].rearrange("p (i d) -> p i d", i=TT)).then_inc(hT_p.sem, 1)
                if active(n, 3):
                    b = n - 3
                    pe.wait_ge(onT3_s.sem, onT3_s.at(b))
                    if x3_s.due(b - 1):
                        pe.wait_ge(x3_s.sem, x3_s.at(b - 1))
                    for i in range(TT):
                        mm = pe.matmul(p_u[:, i * P:(i + 1) * P], on3T[:, i * P:(i + 1) * P], w["Wout2"][:, :], start=True, stop=True)
                    mm.then_inc(u_p.sem, 1)
                if active(n, 1):
                    b = n - 1
                    pe.wait_ge(x3T_s.sem, x3T_s.at(b))
                    if t_s.due(b - 1):
                        pe.wait_ge(t_s.sem, t_s.at(b - 1))
                    if v3_s.due(b - 1):
                        pe.wait_ge(v3_s.sem, v3_s.at(b - 1))
                    pe.matmul(p_qkv[:, 0:Z2], xn3T[o][:, 0:P], w["Wqkv2"][:, :], start=True, stop=True)
                if active(n, 1):
                    pe.matmul(p_qkv[:, 512:512 + Z2], xn3T[o][:, P:2 * P], w["Wqkv2"][:, :], start=True, stop=True).then_inc(qkv_p.sem, 1)
                if active(n, 4):
                    b = n - 4
                    pe.wait_ge(nm4.sem, nm4.at(b))
                    if active(n, 3):
                        pe.wait_ge(onT3_s.sem, onT3_s.at(n - 3))
                    elif x4T_s.due(b - 1):
                        pe.wait_ge(x4T_s.sem, x4T_s.at(b - 1))
                    turn(p_tb, pay[r][:, 0, :, :]).then_inc(x4T_p.sem, 1)
                if active(n, 4):
                    b = n - 4
                    pe.wait_ge(x4T_s.sem, x4T_s.at(b))
                    if pos_s.due(b - 1):
                        pe.wait_ge(pos_s.sem, pos_s.at(b - 1, 2))
                    for i in range(TT):
                        pe.matmul(p_r[:, i * E:(i + 1) * E], xn4T[:, i * P:(i + 1) * P], w["Wr"][:, :], start=True, stop=False)
                        mm = pe.matmul(p_r[:, i * E:(i + 1) * E], w["one_row"][:, :], w["br"][:, :], start=False, stop=True)
                    mm.then_inc(lg_p.sem, 1)
                if active(n, 2):
                    b = n - 2
                    pe.wait_ge(feat_s.sem, feat_s.at(b))
                    pe.wait_ge(v3_s.sem, v3_s.at(b))
                    if o_s.due(b - 1):
                        pe.wait_ge(o_s.sem, o_s.at(b - 1))
                    for i in range(TT):
                        mm = pe.matmul(p_kvo[:, 0:D + H], feat[r][:, i, D:2 * D], KVones[r][:, i, :], start=(i == 0), stop=(i == 1))
                    mm.then_inc(kv_p.sem, 1)
                    if active(n, 1):
                        pe.wait_ge(x3T_s.sem, x3T_s.at(n - 1))
                    turn(p_ta, feat[r]).then_inc(qfT_p.sem, 1)
                if not isinstance(n, int) or n + 1 < B:
                    pe.wait_ge(x2_s.sem, x2_s.at(n))
                    pe.matmul(p_h[:, 0:S], w["wo"][:, :], XN2T[:, n + 1, :], start=True, stop=True).then_inc(z_p.sem, 1)
                if active(n, 2):
                    b = n - 2
                    pe.wait_ge(qfT_s.sem, qfT_s.at(b))
                    pe.wait_ge(kv_s.sem, kv_s.at(b))
                    for i in range(TT):
                        mm = pe.matmul(p_kvo[:, i * S:i * S + D + H], qfT[:, i * P:(i + 1) * P], KVm[:, :], start=True, stop=True)
                    mm.then_inc(o_p.sem, 1)
                if active(n, 4):
                    b = n - 4
                    pe.wait_ge(sel_s.sem, sel_s.at(b))
                    pe.wait_ge(ex4_s.sem, ex4_s.at(b))
                    tri, ones = w["before"], w["ones16"]
                    k0, k1 = sel[r][:, 0, :], sel[r][:, 1, :]
                    c = 64
                    pe.matmul(p_r[:, c:c + E], tri[:, :], k0, start=True, stop=True)
                    pe.matmul(p_r[:, c + E:c + 2 * E], tri[:, :], k1, start=True, stop=False)
                    pe.matmul(p_r[:, c + E:c + 2 * E], ones[:, :], k0, start=False, stop=True)
                    pe.matmul(p_r[:, c + 2 * E:c + 3 * E], ones[:, :], k0, start=True, stop=False)
                    pe.matmul(p_r[:, c + 2 * E:c + 3 * E], ones[:, :], k1, start=False, stop=True).then_inc(rank_p.sem, 1)

            pipeline(pe, iteration)


def experts(nc, ctx, t):

    def sig(name, per=1):
        return Signal(nc, ctx, name, per)

    with ExitStack() as scope:
        def psum(name, cols=512):
            return scope.enter_context(nc.psum_tensor(name, [P, cols], F32))

        def tmp(name, shape, dt=F32):
            return scope.enter_context(nc.sbuf_tensor(name, shape, dt))

        w, X, ident, disp, back = t["w2"], t["X"], t["ident"], t["disp"], t["back"]
        count = t["count"]
        PACK = 4
        R3 = 8

        fill = tmp("fill", [P, ROW])
        counti, endi = tmp("counti", [P, E], I32), tmp("endi", [P, E], I32)
        full, tiles = tmp("full", [P, E]), [tmp(f"tiles{i}", [P, E // 2 + E]) for i in range(2)]
        passed, prev, prevt, here = tmp("passed", [P, E]), tmp("prev", [P, E]), tmp("prevt", [P, 1]), tmp("here", [P, 2])
        tablef, tablei = tmp("tablef", [1, 2, TILES + PACK]), tmp("tablei", [1, 2, TILES], I32)
        rows = [tmp(f"rows{r}", [P, ROW]) for r in range(R3)]
        xT = [tmp(f"xT{r}", [P, P]) for r in range(R3)]
        w1 = [tmp(f"w1_{r}", [P, HID + 2]) for r in range(R3)]
        hid = [tmp(f"hid{r}", [P, 2, P]) for r in range(R3)]
        y = [tmp(f"y{r}", [P, D]) for r in range(R3)]
        to = [tmp(f"to{r}", [P, 1], U32) for r in range(R3)]
        NB = 4
        yb = [tmp(f"yb{i}", [P, NB, TOP * D]) for i in range(2 * B // NB)]

        p_x = [psum(f"p_x{i}") for i in range(2)]
        p_hid = [psum(f"p_hid{i}") for i in range(2)]
        p_y = [psum(f"p_y{i}") for i in range(2)]

        fill_s, plan, table_p, table, pad = sig("fill_s"), sig("plan"), sig("table_p"), sig("table"), [sig(f"pad{q}") for q in range(3)]
        row_s = sig("row_s")
        PLAN_STEPS = 18
        rows_in = [sig(f"rows_in{i}", 16) for i in range(R3)]
        x_p, x_s, w_s, hid_p, hid_s, y_p, y_s, to_s = sig("x_p"), sig("x_s"), sig("w_s"), sig("hid_p"), sig("hid_s", 2), sig("y_p"), sig("y_s"), sig("to_s")
        yout = [sig(f"yout{i}", 16) for i in range(R3)]
        yb_in = [sig(f"yb_in{i}", 16) for i in range(2 * B // NB)]
        sum_s, out_done = [sig(f"sum_s{i}", 2) for i in range(2 * B // NB)], sig("out_done")

        def pipeline(eng, step):
            for k in range(2):
                for r in range(R3):
                    step(k * R3 + r, k, r)
            with eng.Fori(2, TILES // R3, 1) as k:
                for r in range(R3):
                    step(k * R3 + r, k, r)
            for r in range(2):
                step(None, TILES // R3, r)

        def behind(i, k, r, lag):
            last = i is None
            i = TILES + r if last else i
            if isinstance(i, int) and (i < lag or i - lag >= TILES):
                return []
            return [(i - lag, (r - lag) % R3, k if r >= lag else k - 1)]

        def expert(eng, held, i, r):
            if r % PACK == 0 or (isinstance(i, int) and i == 0):
                held["step"], held["word"] = r, eng.value_load(tablei[0:1, 0, bass.ds(i, 1)], min_val=0, max_val=E ** PACK - 1)
            return (held["word"] >> 4 * (r - held["step"])) & (E - 1)

        block = scope.enter_context(nc.Block())

        POOL_SUMS = (2, 6)

        def last_sum(eng, chunks):
            for c in chunks:
                sl = X[:, c * NB:(c + 1) * NB, :]
                eng.wait_ge(yb_in[c].sem, yb_in[c].at(0))
                eng.tensor_tensor(sl, sl, yb[c][:, :, 0:D], ALU.add).then_inc(sum_s[c].sem, 1)
                eng.wait_ge(sum_s[c].sem, sum_s[c].at(0, 1))
                eng.tensor_tensor(sl, sl, yb[c][:, :, D:2 * D], ALU.add).then_inc(sum_s[c].sem, 1)

        PADS = (6, 11, E)

        def fill_tiles(eng, q, low, high):
            eng.wait_ge(fill_s.sem, 4)
            if t["sent"].due(B - 1):
                eng.wait_ge(t["sent"].sem, t["sent"].at(B - 1))
            eng.wait_ge(plan.sem, plan.at(0, 1))
            for e in range(low, high):
                end = eng.value_load(endi[0:1, e:e + 1], min_val=e * REGION, max_val=e * REGION + TOKENS)
                eng.dma_start(disp[bass.ds(end, P), :], fill[:, :]).then_inc(pad[q].sem, 16)

        @block.gpsimd
        def _(pool):
            pool.memset(fill[:, 0:D + 1], 0.0).then_inc(fill_s.sem, 1)
            pool.memset(fill[:, D + 1:ROW], NOWHERE).then_inc(fill_s.sem, 1)
            for i in range(2):
                pool.memset(tiles[i][:, 0:E // 2], 0.0).then_inc(fill_s.sem, 1)
            fill_tiles(pool, 2, PADS[1], PADS[2])

            def step(i, k, r):
                if i is None:
                    return
                pool.wait_ge(y_s.sem, y_s.at(i))
                pool.wait_ge(to_s.sem, to_s.at(i))
                steady(pool, t)
                pool.indirect_dma_start(out=back, out_offset=bass.IndirectOffsetOnAxis(ap=to[r][:, 0:1], axis=0), in_=y[r][:, :],
                                        in_offset=None, bounds_check=TOP * TOKENS - 1, oob_is_err=False).then_inc(yout[r].sem, 16)

            pipeline(pool, step)
            last_sum(pool, POOL_SUMS)

        @block.sync
        def _(sp):
            fill_tiles(sp, 0, 0, PADS[0])
            sp.dma_start(disp[E * REGION:E * REGION + P, :], fill[:, :]).then_inc(pad[0].sem, 16)
            sp.wait_ge(pad[0].sem, 16 * (PADS[0] + 1))
            sp.wait_ge(pad[1].sem, 16 * (PADS[1] - PADS[0]))
            sp.wait_ge(pad[2].sem, 16 * (PADS[2] - PADS[1]))
            sp.wait_ge(table.sem, 1)

            def step(i, k, r):
                if i is None:
                    return
                at = sp.value_load(tablei[0:1, 1, bass.ds(i, 1)], min_val=0, max_val=E * REGION)
                if x_p.due(i - R3):
                    sp.wait_ge(x_p.sem, x_p.at(i - R3))
                if to_s.due(i - R3):
                    sp.wait_ge(to_s.sem, to_s.at(i - R3))
                if y_s.due(i - R3):
                    sp.wait_ge(y_s.sem, y_s.at(i - R3))
                steady(sp, t)
                sp.dma_start(rows[r][:, :], disp[bass.ds(at, P), :]).then_inc(rows_in[r].sem, 16)

            pipeline(sp, step)
            for r in range(R3):
                if yout[r].due(TILES // R3 - 1):
                    sp.wait_ge(yout[r].sem, yout[r].at(TILES // R3 - 1))
            bv = back.rearrange("(n p k) d -> p n (k d)", p=P, k=TOP)
            ov = t["out"].rearrange("(n p) d -> p n d", p=P)
            for c in range(2 * B // NB):
                sp.dma_start(yb[c][:, :, :], bv[:, c * NB:(c + 1) * NB, :]).then_inc(yb_in[c].sem, 16)
            for c in range(2 * B // NB):
                sp.wait_ge(sum_s[c].sem, sum_s[c].at(0))
                sp.dma_start(ov[:, c * NB:(c + 1) * NB, :], X[:, c * NB:(c + 1) * NB, :]).then_inc(out_done.sem, 16)
            sp.wait_ge(out_done.sem, 16 * (2 * B // NB))

        @block.vector
        def _(dve):
            n = [0]

            def then(ins, mark=plan):
                n[0] += 1
                ins.then_inc(mark.sem, 1)
                dve.wait_ge(mark.sem, n[0])

            dve.wait_ge(w["loaded3"].sem, w["loaded3"].at(0))
            if t["pos_s"].due(B - 1):
                dve.wait_ge(t["pos_s"].sem, t["pos_s"].at(B - 1))
            then(dve.tensor_copy(endi[:, :], count[:, :]))
            dve.wait_ge(fill_s.sem, 4)
            dve.memset(tablef[:, 0, TILES:TILES + PACK], 0.0).then_inc(row_s.sem, 1)
            z = E // 2
            then(dve.tensor_tensor(full[:, :], count[:, :], w["region"][:, :], ALU.subtract))
            then(dve.tensor_scalar(counti[:, :], full[:, :], float(P - 1), None, ALU.add))
            then(dve.tensor_scalar(counti[:, :], counti[:, :], 7, None, ALU.logical_shift_right))
            then(dve.tensor_copy(tiles[0][:, z:], counti[:, :]))
            for j, s in enumerate((1, 2, 4, 8)):
                a, b = tiles[j % 2], tiles[(j + 1) % 2]
                then(dve.tensor_tensor(b[:, z:], a[:, z:], a[:, z - s:z - s + E], ALU.add))
            cum = tiles[0][:, z:]
            then(dve.tensor_scalar(passed[:, :], cum, w["iota_t"][:, 0:1], None, ALU.is_le))
            then(dve.tensor_tensor(prev[:, :], passed[:, :], cum, ALU.mult))
            then(dve.tensor_reduce(here[:, 0:1], passed[:, :], AX.X, ALU.add))
            then(dve.tensor_reduce(prevt[:, :], prev[:, :], AX.X, ALU.max))
            then(dve.tensor_tensor(prevt[:, :], w["iota_t"][:, 0:1], prevt[:, :], ALU.subtract))
            then(dve.tensor_scalar(prevt[:, :], prevt[:, :], float(P), None, ALU.mult))
            then(dve.scalar_tensor_tensor(out=here[:, 1:2], in0=here[:, 0:1], scalar=float(REGION), in1=prevt[:, :], op0=ALU.mult, op1=ALU.add))
            then(dve.tensor_scalar(here[:, 1:2], here[:, 1:2], float(E * REGION), None, ALU.min))
            then(dve.tensor_scalar(here[:, 0:1], here[:, 0:1], float(E - 1), None, ALU.min))
            assert n[0] == PLAN_STEPS
            dve.wait_ge(table_p.sem, 2)
            dve.tensor_copy(tablef[:, 0:2, 0:TILES], p_x[0][0:1, 0:2 * TILES].rearrange("p (a t) -> p a t", a=2)).then_inc(row_s.sem, 1)
            for j, (ahead, n_tiles) in enumerate(((1, TILES + 2), (2, TILES))):
                dve.wait_ge(row_s.sem, 2 + j)
                dve.scalar_tensor_tensor(out=tablef[:, 0, 0:n_tiles], in0=tablef[:, 0, ahead:n_tiles + ahead], scalar=float(E ** ahead),
                                         in1=tablef[:, 0, 0:n_tiles], op0=ALU.mult, op1=ALU.add).then_inc(row_s.sem, 1)
            dve.wait_ge(row_s.sem, 4)
            dve.tensor_copy(tablei[:, :, :], tablef[:, :, 0:TILES]).then_inc(table.sem, 1)
            dve.wait_ge(table.sem, 1)
            held = {}

            def step(i, k, r):
                if i is not None:
                    e = expert(dve, held, i, r)
                    if hid_p.due(i - R3):
                        dve.wait_ge(hid_p.sem, hid_p.at(i - R3))
                    if hid_s.due(i - R3):
                        dve.wait_ge(hid_s.sem, hid_s.at(i - R3))
                    dve.tensor_copy(w1[r][:, :], w["W1"][:, bass.ds(e, 1), :].rearrange("p o c -> p (o c)")).then_inc(w_s.sem, 1)
                    dve.wait_ge(rows_in[r].sem, rows_in[r].at(k))
                    if yout[r].due(k - 1):
                        dve.wait_ge(yout[r].sem, yout[r].at(k - 1))
                    dve.tensor_copy(to[r][:, :], rows[r][:, D + 1:ROW]).then_inc(to_s.sem, 1)
                for j, q, kq in behind(i, k, r, 2):
                    dve.wait_ge(y_p.sem, y_p.at(j))
                    if yout[q].due(kq - 1):
                        dve.wait_ge(yout[q].sem, yout[q].at(kq - 1))
                    dve.tensor_scalar(y[q][:, :], p_y[q % 2][:, 0:D], rows[q][:, D:D + 1], None, ALU.mult).then_inc(y_s.sem, 1)

            pipeline(dve, step)
            last_sum(dve, [c for c in range(2 * B // NB) if c not in POOL_SUMS])

        @block.scalar
        def _(act):
            fill_tiles(act, 1, PADS[0], PADS[1])

            def step(i, k, r):
                if i is not None:
                    act.wait_ge(x_p.sem, x_p.at(i))
                    if hid_p.due(i - R3):
                        act.wait_ge(hid_p.sem, hid_p.at(i - R3))
                    act.activation(xT[r][:, :], p_x[r % 2][:, 0:P], ACT.Copy).then_inc(x_s.sem, 1)
                for j, q, _ in behind(i, k, r, 1):
                    act.wait_ge(hid_p.sem, hid_p.at(j))
                    act.wait_ge(w_s.sem, w_s.at(j))
                    if y_p.due(j - R3):
                        act.wait_ge(y_p.sem, y_p.at(j - R3))
                    for c in range(2):
                        act.activation(hid[q][:, c, :], p_hid[q % 2][:, c * P:(c + 1) * P], ACT.Gelu, bias=w1[q][:, HID + c:HID + c + 1])\
                            .then_inc(hid_s.sem, 1)

            pipeline(act, step)

        @block.tensor
        def _(pe):
            pe.wait_ge(w["loaded3"].sem, w["loaded3"].at(0))
            pe.wait_ge(plan.sem, plan.at(0, PLAN_STEPS))
            for i in range(2):
                pe.transpose(p_x[0][0:1, i * TILES:(i + 1) * TILES], here[0:TILES, i:i + 1], ident[0:TILES, 0:TILES]).then_inc(table_p.sem, 1)
            pe.wait_ge(table.sem, 1)

            held = {}

            def step(i, k, r):
                for j, q, _ in behind(i, k, r, 2):
                    e = expert(pe, held, j, r)
                if i is not None:
                    pe.wait_ge(rows_in[r].sem, rows_in[r].at(k))
                    if x_s.due(i - 2):
                        pe.wait_ge(x_s.sem, x_s.at(i - 2))
                    pe.transpose(p_x[r % 2][:, 0:P], rows[r][:, 0:D], ident[:, :]).then_inc(x_p.sem, 1)
                for j, q, _ in behind(i, k, r, 1):
                    pe.wait_ge(x_s.sem, x_s.at(j))
                    pe.wait_ge(w_s.sem, w_s.at(j))
                    if hid_s.due(j - 2):
                        pe.wait_ge(hid_s.sem, hid_s.at(j - 2))
                    for c in range(2):
                        mm = pe.matmul(p_hid[q % 2][:, c * P:(c + 1) * P], w1[q][:, c * P:(c + 1) * P], xT[q][:, :], start=True, stop=True)
                    mm.then_inc(hid_p.sem, 1)
                for j, q, _ in behind(i, k, r, 2):
                    if y_s.due(j - 2):
                        pe.wait_ge(y_s.sem, y_s.at(j - 2))
                    pe.matmul(p_y[q % 2][:, 0:D], w["one_row"][:, :], w["b2"][0:1, bass.ds(e, 1), :].rearrange("p o c -> p (o c)"),
                              start=True, stop=False)
                    pe.wait_ge(hid_s.sem, hid_s.at(j))
                    for c in range(2):
                        mm = pe.matmul(p_y[q % 2][:, 0:D], hid[q][:, c, :], w["W2"][:, bass.ds(e, 1), c, :].rearrange("p o c -> p (o c)"),
                                       start=False, stop=(c == 1))
                    mm.then_inc(y_p.sem, 1)

            pipeline(pe, step)


def program(nc, x, Wqkv, bqk, bv, Wout, bout, gates_w, gates_u, gates_b, in_c, wo, uo, bo, Wqkv2, Wout2, Wr, br, W1, W2, b2, cosf, sinf, out):
    with ExitStack() as ctx:
        def sb(name, shape, dt=F32):
            return ctx.enter_context(nc.sbuf_tensor(name, shape, dt))

        t = dict(x_dram=x, Wqkv=Wqkv, bqk=bqk, bv=bv, Wout=Wout, bout=bout, gates_w=gates_w, gates_u=gates_u, gates_b=gates_b,
                 in_c=in_c, out=out)
        t["X"], t["XN2T"], t["state"] = sb("X", [P, 2 * B, D]), sb("XN2T", [P, B, S]), sb("state", [P, S])
        t["ident"], t["ident16"] = sb("ident", [P, P]), sb("ident16", [P, P], BF16)
        t["disp"] = nc.dram_tensor("disp", [E * REGION + P, ROW], F32).ap()
        t["back"] = nc.dram_tensor("back", [TOP * TOKENS, D], F32).ap()
        t["count"] = sb("count", [P, E])
        w = t["w2"] = dict(wo=sb("wo", [P, D]), uo=sb("uo", [P, D]), bo=sb("bo2", [P, 1]), Wqkv2=sb("Wqkv2", [P, 3 * D]),
                           Wout2=sb("Wout2", [P, D]), Wr=sb("Wr", [P, E]), br=sb("br", [1, E]), cosf=sb("cosf", [P, TT, 2 * D]),
                           sinf=sb("sinf", [P, TT, 2 * D]), W1=sb("W1", [P, E, HID + 2]), W2=sb("W2", [P, E, 2, D]),
                           b2=sb("b2", [1, E, D]), kv_mask=sb("kv_mask", [P, D + H]),
                           before=sb("before", [P, P], BF16), ones16=sb("ones16", [P, P], BF16), iota_e=sb("iota_e", [P, E]),
                           iota_t=sb("iota_t", [P, 1]), region=sb("region", [P, E]), one_row=sb("one_row", [1, P]),
                           loaded=Signal(nc, ctx, "loaded", 16 * 9), loaded3=Signal(nc, ctx, "loaded3", 16 * 3))
        for name in ("consts", "v_set", "count_set", "const_steps"):
            t[name] = Signal(nc, ctx, name)

        t["n_consts"] = 7
        t["w2_loads"] = [(w["wo"], wo), (w["uo"], uo), (w["bo"], bo), (w["Wqkv2"], Wqkv2), (w["Wout2"], Wout2), (w["Wr"], Wr),
                         (w["br"], br), (w["cosf"], cosf), (w["sinf"], sinf)]
        t["w3_loads"] = [(w["W1"], W1), (w["W2"], W2), (w["b2"], b2)]
        attention_and_recurrence(nc, ctx, t)
        linear_attention_and_routing(nc, ctx, t)
        experts(nc, ctx, t)


def kernel(**inputs):
    import numpy as np
    import concourse.bacc as bacc
    from concourse.bass_utils import run_bass_kernel_spmd

    g = {k: np.asarray(v) for k, v in inputs.items()}
    ffn = lambda name: g["L0_ffn_" + name]
    bqkv = g["L0_attn_bqkv"]
    angle = np.arange(S, dtype=np.float32)[:, None] * (1.0 / 10000.0 ** (np.arange(0, HD, 2, dtype=np.float32) / HD))[None, :]
    cos, sin = np.cos(angle), np.sin(angle)
    factors = np.array([SCALE, 1.0], np.float32)[None, :, None, None, None]
    full = lambda lo, hi: np.broadcast_to(factors * np.stack([lo, hi], 1)[:, None, None], (S, 2, H, 2, HD // 2))
    table = lambda a: np.ascontiguousarray(a.reshape(TT, P, 2 * D).transpose(1, 0, 2)).astype(np.float32)
    b1 = g["L1_ffn_b1"].reshape(E, 2, P).transpose(2, 0, 1)
    laid = {
        "x": g["L0_attn_x"].reshape(TOKENS, D),
        "Wqkv": g["L0_attn_Wqkv"], "bqk": bqkv[:2 * D].reshape(2, P).T, "bv": bqkv[2 * D:],
        "Wout": g["L0_attn_Wout"], "bout": g["L0_attn_bout"],
        "gates_w": np.stack([ffn("wf").T, ffn("wi").T, ffn("wc").T], 1),
        "gates_u": np.stack([ffn("uf").T, ffn("ui").T, ffn("uc").T], 1),
        "gates_b": np.stack([ffn("bf"), ffn("bi"), ffn("bc")], 1),
        "in_c": ffn("in_c").reshape(P, 1),
        "wo": ffn("wo").T, "uo": ffn("uo").T, "bo": ffn("bo").reshape(P, 1),
        "Wqkv2": g["L1_attn_w_qkv"].T, "Wout2": g["L1_attn_w_out"].T,
        "Wr": g["L1_ffn_Wr"], "br": g["L1_ffn_br"].reshape(1, E),
        "W1": np.concatenate([g["L1_ffn_W1"].transpose(1, 0, 2), b1], 2),
        "W2": g["L1_ffn_W2"].reshape(E, 2, P, D).transpose(2, 0, 1, 3),
        "b2": g["L1_ffn_b2"].reshape(1, E, D),
        "cosf": table(full(cos, cos)), "sinf": table(full(-sin, sin)),
    }
    nc = bacc.Bacc("TRN2", target_bir_lowering=False, num_devices=1)
    arrays, args = {}, []
    for name, a in laid.items():
        a = np.ascontiguousarray(a)
        arrays[f"in_{name}_dram"] = a
        args.append(nc.dram_tensor(f"in_{name}_dram", a.shape, mybir.dt.from_np(a.dtype), kind="ExternalInput").ap())
    args.append(nc.dram_tensor("out_dram", (TOKENS, D), F32, kind="ExternalOutput").ap())
    program(nc, *args)
    result = run_bass_kernel_spmd(nc, [arrays], core_ids=[0])
    return result.results[0]["out_dram"].reshape(B, S, D)
```
